# Optimizing a Trainium2 kernel written in Bass

```python
import numpy as np
import jax
import jax.numpy as jnp

def _softmax(x, axis=-1):
    return jax.nn.softmax(x, axis=axis)

def _gelu(x):
    return jax.nn.gelu(x, approximate=True)

def _silu(x):
    return jax.nn.silu(x)

def _sigmoid(x):
    return jax.nn.sigmoid(x)

def _layernorm(x, axis=-1, eps=1e-05):
    m = jnp.mean(x, axis=axis, keepdims=True)
    v = jnp.var(x, axis=axis, keepdims=True)
    return (x - m) / jnp.sqrt(v + eps)

def _scatter_add(tgt, idx, src, axis=0):
    return tgt.at[idx].add(src)

def _segment_sum(src, seg, n):
    return jax.ops.segment_sum(src, seg, n)
kernel_name = 'mk_decoder_preln_d1_seqx_r8_5a6cbc'

def setup_inputs(seed: int=0):
    np.random.seed(seed)
    _w = jnp.asarray

    def _rec_inputs():
        import jax
        import jax.numpy as jnp
        _rk = jax.random.key(seed)
        x = 7.22e-05 + 1 * jax.random.normal(jax.random.fold_in(_rk, 1), (64, 128, 128), jnp.float32)
        _lenS = 128 - jax.random.randint(jax.random.fold_in(_rk, 7), (64,), 0, max(1, 128 // 4) + 1, jnp.int32)
        _lenS2 = 77 - jax.random.randint(jax.random.fold_in(_rk, 8), (64,), 0, max(1, 77 // 4) + 1, jnp.int32)
        _ctx_1024P = jax.random.normal(jax.random.fold_in(_rk, 11), (64, 16, 128), jnp.float32)
        _ctx_1024c = jax.random.dirichlet(jax.random.fold_in(_rk, 511), 0.3 * jnp.ones((16,), jnp.float32), (64, 77))
        _ctx_1024t = jnp.einsum('bsk,bkd->bsd', _ctx_1024c, _ctx_1024P)
        _ctx_1024t = _ctx_1024t * jax.lax.rsqrt(jnp.mean(jnp.square(_ctx_1024t)) + 1e-12) * 0.953939
        ctx_1024 = -7.36909e-05 + 0.999899 * (_ctx_1024t + 0.3 * jax.random.normal(jax.random.fold_in(_rk, 611), (64, 77, 128), jnp.float32))
        _validS = jnp.arange(128)[None, :] < _lenS[:, None]
        _validS2 = jnp.arange(77)[None, :] < _lenS2[:, None]
        _causal = jnp.tril(jnp.ones((128, 128), dtype=bool))
        mask_BxS2_bf0 = jnp.logical_not(jnp.ones((64, 77), dtype=bool))
        return (x, ctx_1024, mask_BxS2_bf0)
    x, ctx_1024, mask_BxS2_bf0 = _rec_inputs()

    def _L0_attn_setup():
        import jax, jax.numpy as jnp
        import numpy as np
        D_MODEL = 128
        N_HEAD = 16
        HEAD_D = D_MODEL // N_HEAD
        D_FF = 512
        LN_EPS = 1e-05
        ATTN_EPS = 1e-06

        def _layer_norm(x, g, b, eps=LN_EPS):
            mu = jnp.mean(x, axis=-1, keepdims=True)
            var = jnp.var(x, axis=-1, keepdims=True)
            return (x - mu) * jax.lax.rsqrt(var + eps) * g + b

        def _linear_attention(x, qkv_w, qkv_b, out_w, out_b):
            B, N, C = x.shape
            qkv = (x @ qkv_w + qkv_b).reshape(B, N, 3, N_HEAD, HEAD_D)
            qkv = jnp.transpose(qkv, (2, 0, 3, 1, 4))
            q, k, v = (qkv[0], qkv[1], qkv[2])
            qf = jax.nn.elu(q) + 1.0
            kf = jax.nn.elu(k) + 1.0
            kv = jnp.einsum('bhnd,bhne->bhde', kf.astype(jnp.float32), v.astype(jnp.float32)).astype(v.dtype)
            y_num = jnp.einsum('bhnd,bhde->bhne', qf, kv)
            z = jnp.sum(kf.astype(jnp.float32), axis=2)
            y_den = jnp.einsum('bhnd,bhd->bhn', qf, z.astype(qf.dtype))
            y_den = jnp.maximum(y_den, ATTN_EPS)[..., None]
            y = (y_num / y_den).transpose(0, 2, 1, 3).reshape(B, N, C)
            return y @ out_w + out_b
        key = jax.random.key(seed)
        ks = jax.random.split(key, 16)
        s = 0.02
        return {'src': jax.random.normal(ks[0], (4, 512, D_MODEL), dtype=jnp.float32), 'qkv_w': jax.random.normal(ks[1], (D_MODEL, 3 * D_MODEL), dtype=jnp.float32) * s, 'qkv_b': jax.random.normal(ks[2], (3 * D_MODEL,), dtype=jnp.float32) * s, 'out_w': jax.random.normal(ks[3], (D_MODEL, D_MODEL), dtype=jnp.float32) * s, 'out_b': jax.random.normal(ks[4], (D_MODEL,), dtype=jnp.float32) * s, 'w1': jax.random.normal(ks[5], (D_MODEL, D_FF), dtype=jnp.float32) * s, 'b1': jax.random.normal(ks[6], (D_FF,), dtype=jnp.float32) * s, 'w2': jax.random.normal(ks[7], (D_FF, D_MODEL), dtype=jnp.float32) * s, 'b2': jax.random.normal(ks[8], (D_MODEL,), dtype=jnp.float32) * s, 'g1': jnp.ones((D_MODEL,), dtype=jnp.float32), 'be1': jnp.zeros((D_MODEL,), dtype=jnp.float32), 'g2': jnp.ones((D_MODEL,), dtype=jnp.float32), 'be2': jnp.zeros((D_MODEL,), dtype=jnp.float32)}
    _L0_attn_all = _L0_attn_setup()
    _L0_attn_in = {k: v for k, v in _L0_attn_all.items() if k in ('qkv_w', 'qkv_b', 'out_w', 'out_b', 'w1', 'b1', 'w2', 'b2', 'g1', 'be1', 'g2', 'be2')}
    del _L0_attn_all

    def _L0_xattn_setup():
        import jax, jax.numpy as jnp
        import numpy as np
        D = 128
        H = 16
        HD = D // H
        key = jax.random.key(seed)
        ks = jax.random.split(key, 11)
        B, T, N = (8, 128, 192)
        s = 1.0 / np.sqrt(D)
        return {'query': jax.random.normal(ks[0], (B, T, D), dtype=jnp.float32), 'key_value': jax.random.normal(ks[1], (B, N, D), dtype=jnp.float32), 'key_padding_mask': jnp.zeros((B, N), dtype=bool), 'Wq': jax.random.normal(ks[2], (D, D), dtype=jnp.float32) * s, 'bq': jax.random.normal(ks[3], (D,), dtype=jnp.float32) * s, 'Wk': jax.random.normal(ks[4], (D, D), dtype=jnp.float32) * s, 'bk': jax.random.normal(ks[5], (D,), dtype=jnp.float32) * s, 'Wv': jax.random.normal(ks[6], (D, D), dtype=jnp.float32) * s, 'bv': jax.random.normal(ks[7], (D,), dtype=jnp.float32) * s, 'Wo': jax.random.normal(ks[8], (D, D), dtype=jnp.float32) * s, 'bo': jax.random.normal(ks[9], (D,), dtype=jnp.float32) * s}
    _L0_xattn_all = _L0_xattn_setup()
    _L0_xattn_in = {k: v for k, v in _L0_xattn_all.items() if k in ('Wq', 'bq', 'Wk', 'bk', 'Wv', 'bv', 'Wo', 'bo')}
    del _L0_xattn_all

    def _L0_ffn_setup():
        import jax, jax.numpy as jnp
        import numpy as np
        NUM_EXPERTS = 8
        TOP_K = 2
        CAPACITY_FACTOR = 1.25
        key = jax.random.key(seed)
        ks = jax.random.split(key, 5)
        B, S, D, H, E = (4, 256, 128, 256, NUM_EXPERTS)
        scale = 0.02
        return {'x': jax.random.normal(ks[0], (B, S, D), dtype=jnp.float32), 'gate_w': jax.random.normal(ks[1], (E, D), dtype=jnp.float32) * scale, 'gate_proj_w': jax.random.normal(ks[2], (E, H, D), dtype=jnp.float32) * scale, 'up_proj_w': jax.random.normal(ks[3], (E, H, D), dtype=jnp.float32) * scale, 'down_proj_w': jax.random.normal(ks[4], (E, D, H), dtype=jnp.float32) * scale}
    _L0_ffn_all = _L0_ffn_setup()
    _L0_ffn_in = {k: v for k, v in _L0_ffn_all.items() if k in ('gate_w', 'gate_proj_w', 'up_proj_w', 'down_proj_w')}
    del _L0_ffn_all
    return {'x': x, 'ctx_1024': ctx_1024, 'mask_BxS2_bf0': mask_BxS2_bf0, 'L0_attn_qkv_w': _L0_attn_in['qkv_w'], 'L0_attn_qkv_b': _L0_attn_in['qkv_b'], 'L0_attn_out_w': _L0_attn_in['out_w'], 'L0_attn_out_b': _L0_attn_in['out_b'], 'L0_attn_w1': _L0_attn_in['w1'], 'L0_attn_b1': _L0_attn_in['b1'], 'L0_attn_w2': _L0_attn_in['w2'], 'L0_attn_b2': _L0_attn_in['b2'], 'L0_attn_g1': _L0_attn_in['g1'], 'L0_attn_be1': _L0_attn_in['be1'], 'L0_attn_g2': _L0_attn_in['g2'], 'L0_attn_be2': _L0_attn_in['be2'], 'L0_xattn_Wq': _L0_xattn_in['Wq'], 'L0_xattn_bq': _L0_xattn_in['bq'], 'L0_xattn_Wk': _L0_xattn_in['Wk'], 'L0_xattn_bk': _L0_xattn_in['bk'], 'L0_xattn_Wv': _L0_xattn_in['Wv'], 'L0_xattn_bv': _L0_xattn_in['bv'], 'L0_xattn_Wo': _L0_xattn_in['Wo'], 'L0_xattn_bo': _L0_xattn_in['bo'], 'L0_ffn_gate_w': _L0_ffn_in['gate_w'], 'L0_ffn_gate_proj_w': _L0_ffn_in['gate_proj_w'], 'L0_ffn_up_proj_w': _L0_ffn_in['up_proj_w'], 'L0_ffn_down_proj_w': _L0_ffn_in['down_proj_w']}

def reference(x, ctx_1024, mask_BxS2_bf0, L0_attn_qkv_w, L0_attn_qkv_b, L0_attn_out_w, L0_attn_out_b, L0_attn_w1, L0_attn_b1, L0_attn_w2, L0_attn_b2, L0_attn_g1, L0_attn_be1, L0_attn_g2, L0_attn_be2, L0_xattn_Wq, L0_xattn_bq, L0_xattn_Wk, L0_xattn_bk, L0_xattn_Wv, L0_xattn_bv, L0_xattn_Wo, L0_xattn_bo, L0_ffn_gate_w, L0_ffn_gate_proj_w, L0_ffn_up_proj_w, L0_ffn_down_proj_w):
    import jax
    import jax.numpy as jnp

    def _L0_attn_ref(src, qkv_w, qkv_b, out_w, out_b, w1, b1, w2, b2, g1, be1, g2, be2):
        import jax, jax.numpy as jnp
        import numpy as np
        D_MODEL = 128
        N_HEAD = 16
        HEAD_D = D_MODEL // N_HEAD
        D_FF = 512
        LN_EPS = 1e-05
        ATTN_EPS = 1e-06

        def _layer_norm(x, g, b, eps=LN_EPS):
            mu = jnp.mean(x, axis=-1, keepdims=True)
            var = jnp.var(x, axis=-1, keepdims=True)
            return (x - mu) * jax.lax.rsqrt(var + eps) * g + b

        def _linear_attention(x, qkv_w, qkv_b, out_w, out_b):
            B, N, C = x.shape
            qkv = (x @ qkv_w + qkv_b).reshape(B, N, 3, N_HEAD, HEAD_D)
            qkv = jnp.transpose(qkv, (2, 0, 3, 1, 4))
            q, k, v = (qkv[0], qkv[1], qkv[2])
            qf = jax.nn.elu(q) + 1.0
            kf = jax.nn.elu(k) + 1.0
            kv = jnp.einsum('bhnd,bhne->bhde', kf.astype(jnp.float32), v.astype(jnp.float32)).astype(v.dtype)
            y_num = jnp.einsum('bhnd,bhde->bhne', qf, kv)
            z = jnp.sum(kf.astype(jnp.float32), axis=2)
            y_den = jnp.einsum('bhnd,bhd->bhn', qf, z.astype(qf.dtype))
            y_den = jnp.maximum(y_den, ATTN_EPS)[..., None]
            y = (y_num / y_den).transpose(0, 2, 1, 3).reshape(B, N, C)
            return y @ out_w + out_b
        attn_out = _linear_attention(_layer_norm(src, g1, be1), qkv_w, qkv_b, out_w, out_b)
        x = src + attn_out
        h = jax.nn.gelu(_layer_norm(x, g2, be2) @ w1 + b1, approximate=False)
        return x + h @ w2 + b2

    def _L0_xattn_ref(query, key_value, key_padding_mask, Wq, bq, Wk, bk, Wv, bv, Wo, bo):
        import jax, jax.numpy as jnp
        import numpy as np
        D = 128
        H = 16
        HD = D // H
        B, T, _ = query.shape
        N = key_value.shape[1]
        scale = HD ** (-0.5)
        q = (query @ Wq.T + bq).reshape(B, T, H, HD).transpose(0, 2, 1, 3)
        k = (key_value @ Wk.T + bk).reshape(B, N, H, HD).transpose(0, 2, 1, 3)
        v = (key_value @ Wv.T + bv).reshape(B, N, H, HD).transpose(0, 2, 1, 3)
        attn = jnp.einsum('bhtd,bhnd->bhtn', q, k) * scale
        attn = jnp.where(key_padding_mask[:, None, None, :], -jnp.inf, attn)
        attn = jax.nn.softmax(attn, axis=-1)
        out = jnp.einsum('bhtn,bhnd->bhtd', attn, v)
        out = out.transpose(0, 2, 1, 3).reshape(B, T, D)
        return out @ Wo.T + bo

    def _L0_ffn_ref(x, gate_w, gate_proj_w, up_proj_w, down_proj_w):
        import jax, jax.numpy as jnp
        import numpy as np
        NUM_EXPERTS = 8
        TOP_K = 2
        CAPACITY_FACTOR = 1.25
        B, S, D = x.shape
        E, K = (NUM_EXPERTS, TOP_K)
        T = B * S
        xf = x.reshape(T, D)
        logits = xf @ gate_w.T
        probs = jax.nn.softmax(logits, axis=-1)
        top_p, top_i = jax.lax.top_k(probs, K)
        w = top_p / (jnp.sum(top_p, axis=-1, keepdims=True) + 1e-09)
        capacity = int(CAPACITY_FACTOR * T / E)
        oh = jax.nn.one_hot(top_i, E, dtype=jnp.int32)
        rank = jnp.cumsum(oh, axis=0) - 1
        my_rank = jnp.sum(rank * oh, axis=-1)
        keep = (my_rank < capacity).astype(w.dtype)
        comb = jnp.einsum('tk,tke->te', w * keep, oh.astype(w.dtype))
        out = jnp.zeros_like(xf)
        for e in range(E):
            g = jax.nn.silu(xf @ gate_proj_w[e].T)
            u = xf @ up_proj_w[e].T
            y = g * u @ down_proj_w[e].T
            out = out + comb[:, e:e + 1] * y
        return out.reshape(B, S, D)
    x = x + _L0_attn_ref(_layernorm(x, axis=-1), L0_attn_qkv_w, L0_attn_qkv_b, L0_attn_out_w, L0_attn_out_b, L0_attn_w1, L0_attn_b1, L0_attn_w2, L0_attn_b2, L0_attn_g1, L0_attn_be1, L0_attn_g2, L0_attn_be2)
    x = x + _L0_xattn_ref(_layernorm(x, axis=-1), ctx_1024, mask_BxS2_bf0, L0_xattn_Wq, L0_xattn_bq, L0_xattn_Wk, L0_xattn_bk, L0_xattn_Wv, L0_xattn_bv, L0_xattn_Wo, L0_xattn_bo)
    x = x + _L0_ffn_ref(_layernorm(x, axis=-1), L0_ffn_gate_w, L0_ffn_gate_proj_w, L0_ffn_up_proj_w, L0_ffn_down_proj_w)
    return x

_drawn_inputs = setup_inputs


def setup_inputs(seed=0):
    import zlib

    import numpy as np

    out = dict(_drawn_inputs(seed))
    spreads = {'L0_attn_g1': (1.0, 0.6),
     'L0_attn_be1': (0.0, 0.8),
     'L0_attn_g2': (1.0, 0.6),
     'L0_attn_be2': (0.0, 0.8)}
    factors = {'L0_attn_qkv_w': 8.0,
     'L0_attn_qkv_b': 8.0,
     'L0_attn_out_w': 8.0,
     'L0_attn_out_b': 5.761,
     'L0_attn_b1': 8.0,
     'L0_attn_b2': 5.552,
     'L0_xattn_bq': 5.105,
     'L0_xattn_bk': 8.0,
     'L0_ffn_gate_w': 8.0,
     'L0_ffn_gate_proj_w': 8.0,
     'L0_ffn_up_proj_w': 8.0,
     'L0_ffn_down_proj_w': 8.0}
    for name, (base, spread) in spreads.items():
        noise = np.random.default_rng([zlib.crc32(name.encode()), seed]).standard_normal(out[name].shape)
        drawn = base * np.exp(spread * noise) if base else spread * noise
        out[name] = jnp.asarray(drawn.astype(out[name].dtype))
    for name, factor in factors.items():
        out[name] = (out[name] * factor).astype(out[name].dtype)
    return out
```

```python
from contextlib import ExitStack

import numpy as np

import concourse.bass as bass
from concourse import mybir

F32 = mybir.dt.float32
BF16 = mybir.dt.bfloat16
F16 = mybir.dt.float16
I32 = mybir.dt.int32
U8 = mybir.dt.uint8
ALU = mybir.AluOpType
ACT = mybir.ActivationFunctionType
AX = mybir.AxisListType

P = 128
B = 64
G4 = 4
NG = B // G4
H = 16
HD = P // H
S2 = 77
HB = 4
NQ = H // HB
FF = 512
FC = FF // P
E = 8
HID = 256
K2 = 2
CAP = int(1.25 * B * P / E)
ROWS = E * K2 * CAP
GROUP_ROWS = G4 * P
EG = K2 * CAP // GROUP_ROWS
VC = 3 * HD + 1
EPS = 1e-5
ATTN_EPS = 1e-6
OUT_OF_RANGE = 1.0e6




def some(count):
    return not isinstance(count, int) or count > 0


def over(ap, axis, n):
    a = ap.unsqueeze(axis)
    shape = list(a.shape)
    shape[axis] = n
    return a.broadcast_to(shape)


def build(nc, d, out):
    ctx = ExitStack()
    with ctx:
        def sb(name, shape, dt=F32):
            return ctx.enter_context(nc.sbuf_tensor(name, shape, dt))

        def sem(name):
            return ctx.enter_context(nc.semaphore(name))

        X = sb("X", [P, B, P])
        ident = sb("ident", [P, P])
        block_mask = sb("block_mask", [P, P])
        head_mask = sb("head_mask", [P, H])
        neghalf = sb("neghalf", [P, 8])
        psum = ctx.enter_context(nc.psum_tensor("psum", [P, 8, 512], F32))
        banks = [psum[:, i, :] for i in range(8)]

        xg = nc.dram_tensor("dispatched", [ROWS + GROUP_ROWS, P], F32, kind="Internal").ap()
        yg = nc.dram_tensor("expert_out", [ROWS, P], F32, kind="Internal").ap()

        W = sb("W", [P, B, K2])
        IDX = sb("IDX", [P, B, K2], I32)

        linear_attention_and_ffn(nc, d, X, ident, block_mask, head_mask, neghalf, psum, banks, xg)
        cross_attention(nc, d, X, ident, head_mask, neghalf, psum, banks)
        route(nc, d, X, ident, neghalf, psum, banks, xg, W, IDX)
        experts(nc, d, ident, psum, banks, xg, yg)
        combine(nc, X, W, IDX, yg, out)


def linear_attention_and_ffn(nc, d, X, ident, block_mask, head_mask, neghalf, psum, banks, xg):
    with ExitStack() as ctx:
        def sb(name, shape, dt=F32):
            return ctx.enter_context(nc.sbuf_tensor(name, shape, dt))

        def sem(name):
            return ctx.enter_context(nc.semaphore(name))

        qkv_w = sb("qkv_w", [P, 3 * P])
        out_w = sb("out_w", [P, P])
        w1 = sb("w1", [P, FF])
        w2 = sb("w2", [P, FC, P])
        kb_row, vb_row, ob_row, b2_row = (sb(n, [P, P]) for n in ("kb_row", "vb_row", "ob_row", "b2_row"))
        cols = sb("cols", [P, 6 + FC])
        q_bias, q_bias1, g1, be1, g2, be2 = (cols[:, i:i + 1] for i in range(6))
        zeros = sb("zeros", [P, 4, P])

        mom0, stat0 = sb("mom0", [P, G4, 2]), sb("stat0", [P, G4, 6])
        mom2, stat2 = sb("mom2", [P, G4, 2]), sb("stat2", [P, G4, 6])
        var0, rs0 = sb("var0", [P, 2, G4]), sb("rs0", [P, 2, G4])
        var2, rs2 = sb("var2", [P, G4]), sb("rs2", [P, G4])
        n0, n0b, z1, z2 = (sb(n, [P, G4, P]) for n in ("n0", "n0b", "z1", "z2"))
        ln1T, ln2T, yT = (sb(n, [P, G4 * P]) for n in ("ln1T", "ln2T", "yT"))
        kb, ek, ekm, kf = (sb(n, [P, G4, P]) for n in ("kb", "ek", "ekm", "kf"))
        eq, eqm, qf = (sb(n, [P, G4 * P]) for n in ("eq", "eqm", "qf"))
        v1 = sb("v1", [P, G4, P + 1])
        KV = sb("KV", [P, G4, P + H])
        den, rden = sb("den", [P, G4, H]), sb("rden", [P, G4, H])
        y, x1, x1b, xs = (sb(n, [P, G4, P]) for n in ("y", "x1", "x1b", "xs"))
        hT = sb("hT", [P, FC, G4 * P])

        names = ("passed const_loaded x_loaded zeros_ready zeros_stored neghalf_ready ones_ready "
                 "ln0_stats ln0_moments ln0_var ln0_rstd z1_ready n0_ready n0b_ready z1T_ps ln1T_ready "
                 "kv_ps q_ps kb_ready v_ready ek_ready eq_ready ekm_ready eqm_ready kf_ready qf_ready "
                 "KV_ps KV_ready y_ps den_ready rden_ready y_ready yT_ps yT_ready attn_ps x1_ready x1b_ready xs_ready "
                 "ln2_stats ln2_moments ln2_var ln2_rstd z2_ready z2T_ps ln2T_ready h_ps h_ready w2_ps x_out").split()
        s = {n: sem("a_" + n) for n in names}

        kvp = psum[:, 0:2, :].rearrange("p a (b c) -> p (a b) c", b=2)
        kvs = psum[:, 2:4, :].rearrange("p a (b c) -> p (a b) c", b=2)
        q_ps = banks[2]
        attn_ps = banks[3].rearrange("p (t c) -> p t c", t=G4)
        tp = banks[4]
        w2_ps = banks[5].rearrange("p (t c) -> p t c", t=G4)
        h_ps = [banks[6], banks[7]]

        block = ctx.enter_context(nc.Block())

        consts = [(qkv_w, "qkv_w"), (out_w, "out_w"), (w1, "w1"), (w2, "w2"), (kb_row, "kb_row"),
                  (vb_row, "vb_row"), (ob_row, "ob_row"), (b2_row, "b2_row"), (ident, "ident"),
                  (block_mask, "block_mask"), (head_mask, "head_mask")]
        COLS = ["q_bias", "g1", "be1", "g2", "be2"]
        n_const = 16 * (len(consts) + len(COLS) + 1)

        @block.sync
        def _(sp):
            sp.dma_start(X[:, 0:G4, :], d["x"][:, 0:G4, :]).then_inc(s["x_loaded"], 16)
            for t, n in consts:
                sp.dma_start(t[:], d[n]).then_inc(s["const_loaded"], 16)
            for i, n in zip((0, 2, 3, 4, 5), COLS):
                sp.dma_start(cols[:, i:i + 1], d[n]).then_inc(s["const_loaded"], 16)
            sp.dma_start(cols[:, 6:6 + FC], d["b1"]).then_inc(s["const_loaded"], 16)
            with sp.Fori(1, NG) as g:
                sp.wait_ge(s["x_loaded"], 16 * g)
                sp.dma_start(X[:, bass.ts(g, G4), :], d["x"][:, bass.ts(g, G4), :]).then_inc(s["x_loaded"], 16)
            sp.wait_ge(s["zeros_ready"], 1)
            with sp.Fori(0, (ROWS + GROUP_ROWS) // GROUP_ROWS) as i:
                sp.dma_start(xg[bass.ts(i, GROUP_ROWS), :].rearrange("(p a) c -> p a c", p=P),
                             zeros[:]).then_inc(s["zeros_stored"], 16)
            sp.wait_ge(s["zeros_stored"], 16 * (ROWS + GROUP_ROWS) // GROUP_ROWS)

        @block.gpsimd
        def _(pool):
            pool.memset(neghalf[:], -0.5).then_inc(s["neghalf_ready"], 1)
            pool.memset(zeros[:], 0.0).then_inc(s["zeros_ready"], 1)
            pool.wait_ge(s["const_loaded"], n_const)
            pool.wait_ge(s["neghalf_ready"], 1)
            pool.wait_ge(s["zeros_ready"], 1)

            def ln0_scale(g):
                pool.wait_ge(s["ln0_moments"], g + 1)
                pool.sem_inc(s["passed"], 1)
                pool.tensor_scalar(var0[:, 0, :], mom0[:, :, 1], EPS, None, ALU.add)
                pool.tensor_scalar(var0[:, 1, :], mom0[:, :, 1], 1.0 + EPS, EPS * EPS, ALU.mult, ALU.add).then_inc(s["ln0_var"], 1)
                pool.wait_ge(s["ln0_var"], g + 1)
                pool.tensor_tensor(rs0[:].rearrange("p a b -> p (a b)"), var0[:].rearrange("p a b -> p (a b)"),
                                   neghalf[:, 0:2 * G4], ALU.pow).then_inc(s["ln0_rstd"], 1)

            def add_out_bias(g):
                pool.wait_ge(s["n0_ready"], g + 1)
                if some(g):
                    pool.wait_ge(s["x1_ready"], g)
                pool.tensor_tensor(n0b[:], n0[:], over(ob_row[:], 1, G4), ALU.add).then_inc(s["n0b_ready"], 1)

            def clamp_exps(g):
                pool.wait_ge(s["ek_ready"], g + 1)
                if some(g):
                    pool.wait_ge(s["kf_ready"], g)
                pool.sem_inc(s["passed"], 1)
                pool.tensor_scalar(ekm[:], ek[:], 1.0, None, ALU.min).then_inc(s["ekm_ready"], 1)
                pool.wait_ge(s["eq_ready"], g + 1)
                if some(g):
                    pool.wait_ge(s["qf_ready"], g)
                pool.sem_inc(s["passed"], 1)
                pool.tensor_scalar(eqm[:], eq[:], 1.0, None, ALU.min).then_inc(s["eqm_ready"], 1)

            def ln2_scale(f):
                pool.wait_ge(s["ln2_moments"], f + 1)
                pool.sem_inc(s["passed"], 1)
                pool.tensor_scalar(var2[:], mom2[:, :, 1], EPS, None, ALU.add).then_inc(s["ln2_var"], 1)
                pool.wait_ge(s["ln2_var"], f + 1)
                pool.tensor_tensor(rs2[:], var2[:], neghalf[:, 0:G4], ALU.pow).then_inc(s["ln2_rstd"], 1)

            def residual(f):
                pool.wait_ge(s["x1_ready"], f + 1)
                pool.tensor_tensor(x1b[:], x1[:], over(b2_row[:], 1, G4), ALU.add).then_inc(s["x1b_ready"], 1)
                pool.wait_ge(s["x1b_ready"], f + 1)
                if some(f):
                    pool.wait_ge(s["x_out"], f)
                pool.tensor_tensor(xs[:], x1b[:], X[:, bass.ts(f, G4), :], ALU.add).then_inc(s["xs_ready"], 1)

            ln0_scale(0)
            add_out_bias(0)
            clamp_exps(0)
            ln0_scale(1)

            def both(g):
                ln2_scale(g - 1)
                add_out_bias(g)
                clamp_exps(g)
                residual(g - 1)
                ln0_scale(g + 1)

            both(1)
            with pool.Fori(2, NG - 1) as g:
                both(g)
            ln2_scale(NG - 2)
            add_out_bias(NG - 1)
            clamp_exps(NG - 1)
            residual(NG - 2)
            ln2_scale(NG - 1)
            residual(NG - 1)

        @block.vector
        def _(dve):
            nc.vector.memset(v1[:, :, P:P + 1], 1.0).then_inc(s["ones_ready"], 1)

            def ln0(g):
                dve.wait_ge(s["x_loaded"], 16 * g + 16)
                for t in range(G4):
                    last = nc.vector.bn_stats(stat0[:, t, :], X[:, bass.ds(G4 * g + t, 1), :].rearrange("p a c -> p (a c)"))
                last.then_inc(s["ln0_stats"], 1)
                dve.wait_ge(s["ln0_stats"], g + 1)
                dve.sem_inc(s["passed"], 1)
                for t in range(G4):
                    last = nc.vector.bn_aggr(mom0[:, t, :], stat0[:, t, :])
                last.then_inc(s["ln0_moments"], 1)
                dve.wait_ge(s["ln0_rstd"], g + 1)
                if some(g):
                    dve.wait_ge(s["z1T_ps"], g)
                dve.wait_ge(s["ln0_moments"], g + 1)
                for t in range(G4):
                    xt = X[:, bass.ds(G4 * g + t, 1), :].rearrange("p a c -> p (a c)")
                    last = nc.vector.tensor_scalar(z1[:, t, :], xt, mom0[:, t, 0:1], rs0[:, 1, t:t + 1], ALU.subtract, ALU.mult)
                last.then_inc(s["z1_ready"], 1)
                if some(g):
                    dve.wait_ge(s["n0b_ready"], g)
                for t in range(G4):
                    xt = X[:, bass.ds(G4 * g + t, 1), :].rearrange("p a c -> p (a c)")
                    last = nc.vector.tensor_scalar(n0[:, t, :], xt, mom0[:, t, 0:1], rs0[:, 0, t:t + 1], ALU.subtract, ALU.mult)
                last.then_inc(s["n0_ready"], 1)

            def features(g):
                dve.wait_ge(s["kv_ps"], g + 1)
                if some(g):
                    dve.wait_ge(s["ek_ready"], g)
                nc.vector.tensor_tensor(kb[:], kvp[:, :, 0:P], over(kb_row[:], 1, G4), ALU.add).then_inc(s["kb_ready"], 1)
                if some(g):
                    dve.wait_ge(s["KV_ps"], g)
                nc.vector.tensor_tensor(v1[:, :, 0:P], kvp[:, :, P:2 * P], over(vb_row[:], 1, G4), ALU.add).then_inc(s["v_ready"], 1)
                dve.wait_ge(s["ekm_ready"], g + 1)
                nc.vector.scalar_tensor_tensor(kf[:], kb[:], 1.0, ekm[:], ALU.add, ALU.max).then_inc(s["kf_ready"], 1)
                dve.wait_ge(s["eqm_ready"], g + 1)
                dve.wait_ge(s["q_ps"], g + 1)
                if some(g):
                    dve.wait_ge(s["y_ps"], g)
                nc.vector.scalar_tensor_tensor(qf[:], q_ps, q_bias1, eqm[:], ALU.add, ALU.max).then_inc(s["qf_ready"], 1)

            def mask_kv(g):
                dve.wait_ge(s["KV_ps"], g + 1)
                if some(g):
                    dve.wait_ge(s["y_ps"], g)
                nc.vector.tensor_tensor(KV[:, :, 0:P], kvs[:, :, 0:P], over(block_mask[:], 1, G4), ALU.mult)
                nc.vector.tensor_tensor(KV[:, :, P:P + H], kvs[:, :, P:P + 1].broadcast_to([P, G4, H]),
                                        over(head_mask[:], 1, G4), ALU.mult).then_inc(s["KV_ready"], 1)

            def normalise(g):
                dve.wait_ge(s["y_ps"], g + 1)
                nc.vector.tensor_scalar(den[:], kvp[:, :, P:P + H], ATTN_EPS, None, ALU.max).then_inc(s["den_ready"], 1)
                dve.wait_ge(s["den_ready"], g + 1)
                nc.vector.reciprocal(rden[:], den[:]).then_inc(s["rden_ready"], 1)
                dve.wait_ge(s["rden_ready"], g + 1)
                if some(g):
                    dve.wait_ge(s["yT_ps"], g)
                nc.vector.tensor_tensor(y[:].rearrange("p t (h c) -> p t h c", h=H),
                                        kvp[:, :, 0:P].rearrange("p t (h c) -> p t h c", h=H),
                                        over(rden[:], 3, HD), ALU.mult).then_inc(s["y_ready"], 1)

            def add_attention(g):
                dve.wait_ge(s["attn_ps"], g + 1)
                dve.wait_ge(s["n0b_ready"], g + 1)
                if some(g):
                    dve.wait_ge(s["x1b_ready"], g)
                if some(g):
                    dve.wait_ge(s["z2_ready"], g)
                nc.vector.tensor_tensor(x1[:], attn_ps, n0b[:], ALU.add).then_inc(s["x1_ready"], 1)

            def ln2(f):
                dve.wait_ge(s["x1_ready"], f + 1)
                for t in range(G4):
                    last = nc.vector.bn_stats(stat2[:, t, :], x1[:, t, :])
                last.then_inc(s["ln2_stats"], 1)
                dve.wait_ge(s["ln2_stats"], f + 1)
                dve.sem_inc(s["passed"], 1)
                for t in range(G4):
                    last = nc.vector.bn_aggr(mom2[:, t, :], stat2[:, t, :])
                last.then_inc(s["ln2_moments"], 1)
                dve.wait_ge(s["ln2_rstd"], f + 1)
                if some(f):
                    dve.wait_ge(s["z2T_ps"], f)
                dve.wait_ge(s["ln2_moments"], f + 1)
                for t in range(G4):
                    last = nc.vector.tensor_scalar(z2[:, t, :], x1[:, t, :], mom2[:, t, 0:1], rs2[:, t:t + 1], ALU.subtract, ALU.mult)
                last.then_inc(s["z2_ready"], 1)

            def finish(f):
                dve.wait_ge(s["w2_ps"], f + 1)
                dve.wait_ge(s["xs_ready"], f + 1)
                nc.vector.tensor_tensor(X[:, bass.ts(f, G4), :], w2_ps, xs[:], ALU.add).then_inc(s["x_out"], 1)

            dve.wait_ge(s["const_loaded"], n_const)
            nc.vector.tensor_scalar(q_bias1, q_bias, 1.0, None, ALU.add).then_inc(s["ones_ready"], 1)
            dve.wait_ge(s["ones_ready"], 2)
            ln0(0)
            features(0)
            mask_kv(0)
            normalise(0)
            ln0(1)
            add_attention(0)

            def both(g):
                ln2(g - 1)
                features(g)
                mask_kv(g)
                normalise(g)
                ln0(g + 1)
                finish(g - 1)
                add_attention(g)

            both(1)
            with dve.Fori(2, NG - 1) as g:
                both(g)
            ln2(NG - 2)
            features(NG - 1)
            mask_kv(NG - 1)
            normalise(NG - 1)
            finish(NG - 2)
            add_attention(NG - 1)
            ln2(NG - 1)
            finish(NG - 1)
            dve.wait_ge(s["x_out"], NG)

        @block.scalar
        def _(act):
            def attention_side(g):
                act.wait_ge(s["z1T_ps"], g + 1)
                if some(g):
                    act.wait_ge(s["kv_ps"], g)
                if some(g):
                    act.wait_ge(s["q_ps"], g)
                nc.scalar.activation(ln1T[:], tp, ACT.Identity, scale=g1, bias=be1).then_inc(s["ln1T_ready"], 1)
                act.wait_ge(s["kb_ready"], g + 1)
                if some(g):
                    act.wait_ge(s["ekm_ready"], g)
                nc.scalar.activation(ek[:], kb[:], ACT.Exp).then_inc(s["ek_ready"], 1)
                act.wait_ge(s["q_ps"], g + 1)
                if some(g):
                    act.wait_ge(s["eqm_ready"], g)
                nc.scalar.activation(eq[:], q_ps, ACT.Exp, bias=q_bias).then_inc(s["eq_ready"], 1)

            def ffn_side(f):
                act.wait_ge(s["z2T_ps"], f + 1)
                if some(FC * f):
                    act.wait_ge(s["h_ps"], FC * f)
                nc.scalar.activation(ln2T[:], tp, ACT.Identity, scale=g2, bias=be2).then_inc(s["ln2T_ready"], 1)
                if some(f):
                    act.wait_ge(s["w2_ps"], f)
                for c in range(FC):
                    act.wait_ge(s["h_ps"], FC * f + c + 1)
                    nc.scalar.activation(hT[:, c, :], h_ps[c % 2], ACT.Gelu, bias=cols[:, 6 + c:7 + c]).then_inc(s["h_ready"], 1)

            def yT_side(g):
                act.wait_ge(s["yT_ps"], g + 1)
                if some(g):
                    act.wait_ge(s["attn_ps"], g)
                nc.scalar.activation(yT[:], tp, ACT.Copy).then_inc(s["yT_ready"], 1)

            act.wait_ge(s["const_loaded"], n_const)
            attention_side(0)
            yT_side(0)

            def both(g):
                attention_side(g)
                ffn_side(g - 1)
                yT_side(g)

            both(1)
            with act.Fori(2, NG) as g:
                both(g)
            ffn_side(NG - 1)

        @block.tensor
        def _(pe):
            def t1(g):
                pe.wait_ge(s["z1_ready"], g + 1)
                if some(g):
                    pe.wait_ge(s["yT_ready"], g)
                for t in range(G4):
                    last = nc.tensor.transpose(tp[:, t * P:(t + 1) * P], z1[:, t, :], ident[:])
                last.then_inc(s["z1T_ps"], 1)

            def project(g):
                pe.wait_ge(s["ln1T_ready"], g + 1)
                if some(g):
                    pe.wait_ge(s["y_ready"], g)
                for t in range(G4):
                    last = nc.tensor.matmul(kvp[:, t, :], ln1T[:, t * P:(t + 1) * P], qkv_w[:, P:3 * P], start=True, stop=True)
                last.then_inc(s["kv_ps"], 1)
                if some(g):
                    pe.wait_ge(s["KV_ready"], g)
                nc.tensor.matmul(q_ps, qkv_w[:, 0:P], ln1T[:], start=True, stop=True).then_inc(s["q_ps"], 1)

            def t2(f):
                pe.wait_ge(s["z2_ready"], f + 1)
                pe.wait_ge(s["ln1T_ready"], f + 2)
                for t in range(G4):
                    last = nc.tensor.transpose(tp[:, t * P:(t + 1) * P], z2[:, t, :], ident[:])
                last.then_inc(s["z2T_ps"], 1)

            def ffn_up(f):
                pe.wait_ge(s["ln2T_ready"], f + 1)
                for c in range(FC):
                    if c >= 2:
                        pe.wait_ge(s["h_ready"], FC * f + c - 1)
                    else:
                        if some(FC * f):
                            pe.wait_ge(s["h_ready"], FC * f)
                    nc.tensor.matmul(h_ps[c % 2], w1[:, c * P:(c + 1) * P], ln2T[:], start=True, stop=True).then_inc(s["h_ps"], 1)

            def context(g):
                pe.wait_ge(s["kf_ready"], g + 1)
                pe.wait_ge(s["v_ready"], g + 1)
                pe.wait_ge(s["qf_ready"], g + 1)
                if some(g):
                    pe.wait_ge(s["x1_ready"], g)
                for t in range(G4):
                    last = nc.tensor.matmul(kvs[:, t, 0:P + 1], kf[:, t, :], v1[:, t, :], start=True, stop=True)
                last.then_inc(s["KV_ps"], 1)

            def ffn_down(f, tiles):
                pe.wait_ge(s["h_ready"], FC * f + FC)
                if some(f):
                    pe.wait_ge(s["x_out"], f)
                for t in tiles:
                    for c in range(FC):
                        last = nc.tensor.matmul(w2_ps[:, t, :], hT[:, c, t * P:(t + 1) * P], w2[:, c, :],
                                                start=(c == 0), stop=(c == FC - 1))
                if tiles[-1] == G4 - 1:
                    last.then_inc(s["w2_ps"], 1)

            def attend(g):
                pe.wait_ge(s["KV_ready"], g + 1)
                pe.wait_ge(s["kb_ready"], g + 1)
                for t in range(G4):
                    last = nc.tensor.matmul(kvp[:, t, 0:P + H], qf[:, t * P:(t + 1) * P], KV[:, t, :], start=True, stop=True)
                last.then_inc(s["y_ps"], 1)

            def project_out(g, f):
                pe.wait_ge(s["y_ready"], g + 1)
                if some(f + 1):
                    pe.wait_ge(s["ln2T_ready"], f + 1)
                for t in range(G4):
                    last = nc.tensor.transpose(tp[:, t * P:(t + 1) * P], y[:, t, :], ident[:])
                last.then_inc(s["yT_ps"], 1)
                pe.wait_ge(s["yT_ready"], g + 1)
                for t in range(G4):
                    last = nc.tensor.matmul(attn_ps[:, t, :], yT[:, t * P:(t + 1) * P], out_w[:], start=True, stop=True)
                last.then_inc(s["attn_ps"], 1)

            pe.wait_ge(s["const_loaded"], n_const)
            pe.wait_ge(s["ones_ready"], 2)
            t1(0)
            project(0)
            context(0)
            attend(0)
            project_out(0, -1)

            def both(g):
                t1(g)
                project(g)
                t2(g - 1)
                ffn_up(g - 1)
                context(g)
                ffn_down(g - 1, (0, 1))
                attend(g)
                ffn_down(g - 1, (2, 3))
                project_out(g, g - 1)

            both(1)
            with pe.Fori(2, NG) as g:
                both(g)
            pe.wait_ge(s["z2_ready"], NG)
            pe.wait_ge(s["yT_ready"], NG)
            for t in range(G4):
                last = nc.tensor.transpose(tp[:, t * P:(t + 1) * P], z2[:, t, :], ident[:])
            last.then_inc(s["z2T_ps"], 1)
            ffn_up(NG - 1)
            ffn_down(NG - 1, (0, 1, 2, 3))


def cross_attention(nc, d, X, ident, head_mask, neghalf, psum, banks):
    with ExitStack() as ctx:
        def sb(name, shape, dt=F32):
            return ctx.enter_context(nc.sbuf_tensor(name, shape, dt))

        def sem(name):
            return ctx.enter_context(nc.semaphore(name))

        wq, wk, wv, wo = (sb(n, [P, P]) for n in ("wq", "wk", "wv", "wo"))
        bv_row, bo_row = sb("bv_row", [P, P]), sb("bo_row", [P, P])
        bcols = sb("bcols", [P, 3])
        first_row = sb("first_row", [P, P], BF16)
        masked = sb("masked", [P, B * S2], BF16)
        mask_u8 = sb("mask_u8", [1, B * S2], U8)

        mom3, stat3 = sb("mom3", [P, G4, 2]), sb("stat3", [P, G4, 6])
        var3, rs3 = sb("var3", [P, G4]), sb("rs3", [P, G4])
        z3 = sb("z3", [P, G4, P])
        z3T = sb("z3T", [P, G4 * P])
        cT = [sb(f"cT{i}", [P, G4 * S2]) for i in range(2)]
        qT = [sb(f"qT{i}", [P, G4 * P]) for i in range(2)]
        kT = [sb(f"kT{i}", [P, G4, S2]) for i in range(2)]
        Kb = [sb(f"Kb{i}", [P, H, S2]) for i in range(2)]
        vb, vr = sb("vb", [S2, G4, P]), sb("vr", [S2, G4, P])
        V = [sb(f"V{i}", [S2, G4, H, VC], BF16) for i in range(2)]
        M = sb("M", [P, H])
        Sd = sb("Sd", [P, H, S2])
        Pr = [sb(f"Pr{i}", [P, H, S2]) for i in range(2)]
        hi, lo = sb("hi", [S2, H * P], F16), sb("lo", [S2, H * P], F16)
        osum, rsum = sb("osum", [P, H, HD]), sb("rsum", [P, H])
        o = sb("o", [P, G4, P])
        oT = sb("oT", [P, G4 * P])
        xb = sb("xb", [P, G4, P])

        names = ("passed const_loaded ones_ready mask_ready q_bias_ready ctx_loaded "
                 "ln3_stats ln3_moments ln3_var ln3_rstd z3_ready z3T_ps z3T_ready q_ps qT_ready k_ps kT_ready "
                 "v_ps vb_ready v1_ready vr_ready v2_ready v3_ready Kb_ready S_ps M_ready Sd_ready P_ready PT_ps "
                 "hi_ready lo_ready pv_done osum_ready rsum_ready o_ready oT_ps oT_ready out_ps xb_ready x_out").split()
        s = {n: sem("b_" + n) for n in names}

        S = psum[:, 0:4, 0:HB * S2].rearrange("p a (h n) -> p a h n", h=HB)
        PT = [banks[4], banks[5]]
        O = banks[6][:, 0:H * VC].rearrange("p (h c) -> p h c", h=H)
        misc = banks[7]

        consts = [(wq, "wq"), (wk, "wk"), (wv, "wv"), (wo, "wo"), (bv_row, "bv_row"), (bo_row, "bo_row"),
                  (first_row, "first_row"), (mask_u8, "mask")]
        n_const = 16 * (len(consts) + 2)
        block = ctx.enter_context(nc.Block())

        def groups(eng, slot):
            for j in range(G4):
                slot(0, 0, j)
            with eng.Fori(1, NG - 2, 2) as g:
                for par in (0, 1):
                    for j in range(G4):
                        slot(g + par, (1 + par) % 2, j)
            for j in range(G4):
                slot(NG - 1, (NG - 1) % 2, j)

        def last_group(g):
            return isinstance(g, int) and g == NG - 1

        def first_group(g):
            return isinstance(g, int) and g == 0

        def xrow(g, t):
            return X[:, bass.ds(G4 * g + t, 1), :].rearrange("p a c -> p (a c)")

        @block.sync
        def _(sp):
            for t, n in consts:
                sp.dma_start(t[:], d[n]).then_inc(s["const_loaded"], 16)
            sp.dma_start(bcols[:, 0:1], d["bq"]).then_inc(s["const_loaded"], 16)
            sp.dma_start(bcols[:, 1:2], d["bk"]).then_inc(s["const_loaded"], 16)

            def load(g, par):
                if some(g - 1):
                    sp.wait_ge(s["v_ps"], g - 1)
                if some(g - 1):
                    sp.wait_ge(s["k_ps"], g - 1)
                sp.sem_inc(s["passed"], 1)
                if some(16 * g):
                    sp.wait_ge(s["ctx_loaded"], 16 * g)
                sp.dma_start(cT[par][:], d["ctxT"][:, bass.ts(g, G4 * S2)]).then_inc(s["ctx_loaded"], 16)

            load(0, 0)
            load(1, 1)
            with sp.Fori(2, NG - 1, 2) as g:
                load(g, 0)
                load(g + 1, 1)

        @block.gpsimd
        def _(pool):
            pool.memset(masked[:], 0.0).then_inc(s["ones_ready"], 1)
            for i in range(2):
                pool.memset(V[i][:, :, :, VC - 1:VC], 1.0).then_inc(s["ones_ready"], 1)
            pool.wait_ge(s["const_loaded"], n_const)
            pool.wait_ge(s["ones_ready"], 3)
            pool.tensor_scalar(masked[0:1, :], mask_u8[:], -3e38, 1e38, ALU.mult, ALU.mult).then_inc(s["mask_ready"], 1)

            def ln3_scale(g):
                pool.wait_ge(s["ln3_moments"], g + 1)
                pool.sem_inc(s["passed"], 1)
                pool.tensor_scalar(var3[:], mom3[:, :, 1], EPS, None, ALU.add).then_inc(s["ln3_var"], 1)
                pool.wait_ge(s["ln3_var"], g + 1)
                pool.tensor_tensor(rs3[:], var3[:], neghalf[:, 0:G4], ALU.pow).then_inc(s["ln3_rstd"], 1)

            def spread_keys(g, par, j, b):
                pool.wait_ge(s["kT_ready"], g + 1)
                if some(b - 1):
                    pool.wait_ge(s["S_ps"], b - 1)
                pool.tensor_tensor(Kb[j % 2][:], over(kT[par][:, j, :], 1, H), over(head_mask[:], 2, S2),
                                   ALU.mult).then_inc(s["Kb_ready"], 1)

            def split_values(g, par):
                pool.wait_ge(s["vb_ready"], g + 1)
                if some(NQ * (G4 * g - G4)):
                    pool.wait_ge(s["pv_done"], NQ * (G4 * g - G4))
                pool.sem_inc(s["passed"], 1)
                part = [V[par][:, :, :, HD * i:HD * i + HD] for i in range(3)]
                v4 = vb[:].rearrange("p t (h c) -> p t h c", h=H)
                r4 = vr[:].rearrange("p t (h c) -> p t h c", h=H)
                for t in range(G4):
                    last = pool.tensor_scalar(part[0][:, t], v4[:, t], 1.0, None, ALU.mult)
                last.then_inc(s["v1_ready"], 1)
                pool.wait_ge(s["v1_ready"], g + 1)
                if some(g):
                    pool.wait_ge(s["v3_ready"], g)
                for t in range(G4):
                    last = pool.tensor_tensor(r4[:, t], v4[:, t], part[0][:, t], ALU.subtract)
                last.then_inc(s["vr_ready"], 1)
                pool.wait_ge(s["vr_ready"], g + 1)
                pool.sem_inc(s["passed"], 1)
                for t in range(G4):
                    last = pool.tensor_scalar(part[1][:, t], r4[:, t], 1.0, None, ALU.mult)
                last.then_inc(s["v2_ready"], 1)
                pool.wait_ge(s["v2_ready"], g + 1)
                for t in range(G4):
                    last = pool.tensor_tensor(part[2][:, t], r4[:, t], part[1][:, t], ALU.subtract)
                last.then_inc(s["v3_ready"], 1)

            def add_out_bias(g):
                if last_group(g):
                    pool.wait_ge(s["x_out"], g)
                else:
                    pool.wait_ge(s["vb_ready"], g + 2)
                pool.tensor_tensor(xb[:], X[:, bass.ts(g, G4), :], over(bo_row[:], 1, G4), ALU.add).then_inc(s["xb_ready"], 1)

            def slot(g, par, j):
                b = G4 * g + j
                if j == 0 and not last_group(g):
                    ln3_scale(g + 1)
                if j == 1 and not first_group(g):
                    add_out_bias(g - 1)
                if j < 2:
                    spread_keys(g, par, j + 2, b + 2)
                elif not last_group(g):
                    spread_keys(g + 1, 1 - par, j - 2, b + 2)
                if j == 3 and not last_group(g):
                    split_values(g + 1, 1 - par)

            ln3_scale(0)
            spread_keys(0, 0, 0, 0)
            spread_keys(0, 0, 1, 1)
            split_values(0, 0)
            groups(pool, slot)
            add_out_bias(NG - 1)

        @block.vector
        def _(dve):
            def ln3(g):
                for t in range(G4):
                    last = nc.vector.bn_stats(stat3[:, t, :], xrow(g, t))
                last.then_inc(s["ln3_stats"], 1)
                dve.wait_ge(s["ln3_stats"], g + 1)
                dve.sem_inc(s["passed"], 1)
                for t in range(G4):
                    last = nc.vector.bn_aggr(mom3[:, t, :], stat3[:, t, :])
                last.then_inc(s["ln3_moments"], 1)

            def ln3_apply(g):
                dve.wait_ge(s["ln3_rstd"], g + 1)
                dve.wait_ge(s["ln3_moments"], g + 1)
                if some(g):
                    dve.wait_ge(s["z3T_ps"], g)
                for t in range(G4):
                    last = nc.vector.tensor_scalar(z3[:, t, :], xrow(g, t), mom3[:, t, 0:1], rs3[:, t:t + 1], ALU.subtract, ALU.mult)
                last.then_inc(s["z3_ready"], 1)

            def add_value_bias(g):
                dve.wait_ge(s["v_ps"], g + 1)
                if some(g):
                    dve.wait_ge(s["v3_ready"], g)
                nc.vector.tensor_tensor(vb[:], misc[0:S2, :].rearrange("p (t c) -> p t c", t=G4),
                                        over(bv_row[0:S2, :], 1, G4), ALU.add).then_inc(s["vb_ready"], 1)

            def shift(b):
                dve.wait_ge(s["S_ps"], b + 1)
                nc.vector.reduce_max(M[:].rearrange("p (a h) -> p a h", a=NQ), S, AX.X).then_inc(s["M_ready"], 1)
                dve.wait_ge(s["M_ready"], b + 1)
                if some(b):
                    dve.wait_ge(s["P_ready"], b)
                nc.vector.tensor_tensor(Sd[:].rearrange("p (a h) n -> p a h n", a=NQ), S,
                                        over(M[:].rearrange("p (a h) -> p a h", a=NQ), 3, S2), ALU.subtract).then_inc(s["Sd_ready"], 1)

            def low_part(b, q):
                n = NQ * b + q
                dve.wait_ge(s["hi_ready"], n + 1)
                if some(n - NQ + 1):
                    dve.wait_ge(s["pv_done"], n - NQ + 1)
                nc.vector.tensor_tensor(lo[:, bass.ts(q, 512)], PT[q % 2][0:S2, :], hi[:, bass.ts(q, 512)],
                                        ALU.subtract).then_inc(s["lo_ready"], 1)

            def normalise(b, j):
                dve.wait_ge(s["pv_done"], NQ * b + NQ)
                nc.vector.tensor_reduce(osum[:], O[:, :, 0:3 * HD].rearrange("p h (i c) -> p h c i", i=3), AX.X, ALU.add).then_inc(s["osum_ready"], 1)
                nc.vector.reciprocal(rsum[:], O[:, :, 3 * HD:VC].rearrange("p h c -> p (h c)")).then_inc(s["rsum_ready"], 1)
                dve.wait_ge(s["osum_ready"], b + 1)
                dve.wait_ge(s["rsum_ready"], b + 1)
                nc.vector.tensor_tensor(o[:, j, :].rearrange("p (h c) -> p h c", h=H), osum[:], over(rsum[:], 2, HD), ALU.mult).then_inc(s["o_ready"], 1)

            def add_out(g):
                dve.wait_ge(s["out_ps"], g + 1)
                dve.wait_ge(s["xb_ready"], g + 1)
                nc.vector.tensor_tensor(X[:, bass.ts(g, G4), :], misc.rearrange("p (t c) -> p t c", t=G4), xb[:], ALU.add).then_inc(s["x_out"], 1)

            def slot(g, par, j):
                b = G4 * g + j
                last = last_group(g) and j == G4 - 1
                low_part(b, 0)
                low_part(b, 1)
                if not (first_group(g) and j == 0):
                    if j == 1:
                        if some(g):
                            dve.wait_ge(s["oT_ps"], g)
                    normalise(b - 1, (j - 1) % G4)
                if j == 3 and not last_group(g):
                    add_value_bias(g + 1)
                if not last:
                    shift(b + 1)
                low_part(b, 2)
                low_part(b, 3)
                if j == 0 and not last_group(g):
                    ln3(g + 1)
                if j == 1:
                    if not first_group(g):
                        add_out(g - 1)
                    if not last_group(g):
                        ln3_apply(g + 1)

            dve.wait_ge(s["const_loaded"], n_const)
            dve.wait_ge(s["ones_ready"], 3)
            nc.vector.tensor_scalar(bcols[:, 2:3], bcols[:, 0:1], float(HD) ** -0.5, None, ALU.mult).then_inc(s["q_bias_ready"], 1)
            ln3(0)
            ln3_apply(0)
            add_value_bias(0)
            shift(0)
            groups(dve, slot)
            normalise(B - 1, G4 - 1)
            add_out(NG - 1)
            dve.wait_ge(s["x_out"], NG)

        @block.scalar
        def _(act):
            def z3T_side(g):
                act.wait_ge(s["z3T_ps"], g + 1)
                if some(g):
                    act.wait_ge(s["q_ps"], g)
                nc.scalar.activation(z3T[:], misc, ACT.Copy).then_inc(s["z3T_ready"], 1)

            def kT_side(g, par):
                act.wait_ge(s["k_ps"], g + 1)
                if some(G4 * g - G4):
                    act.wait_ge(s["Kb_ready"], G4 * g - G4)
                nc.scalar.activation(kT[par][:].rearrange("p t n -> p (t n)"), misc[:, 0:G4 * S2], ACT.Identity,
                                     bias=bcols[:, 1:2]).then_inc(s["kT_ready"], 1)

            def qT_side(g, par):
                act.wait_ge(s["q_ps"], g + 1)
                if some(G4 * g - G4):
                    act.wait_ge(s["S_ps"], G4 * g - G4)
                nc.scalar.activation(qT[par][:], misc, ACT.Identity, bias=bcols[:, 2:3], scale=float(HD) ** -0.5).then_inc(s["qT_ready"], 1)

            def exps(b, j):
                act.wait_ge(s["Sd_ready"], b + 1)
                if some(NQ * (b - 1)):
                    act.wait_ge(s["PT_ps"], NQ * (b - 1))
                nc.scalar.activation(Pr[j % 2][:], Sd[:], ACT.Exp).then_inc(s["P_ready"], 1)

            def high_part(b, q):
                n = NQ * b + q
                act.wait_ge(s["PT_ps"], n + 1)
                if some(n - NQ + 1):
                    act.wait_ge(s["pv_done"], n - NQ + 1)
                nc.scalar.activation(hi[:, bass.ts(q, 512)], PT[q % 2][0:S2, :], ACT.Copy).then_inc(s["hi_ready"], 1)

            def slot(g, par, j):
                b = G4 * g + j
                last = last_group(g) and j == G4 - 1
                if j == 2 and not last_group(g):
                    kT_side(g + 1, 1 - par)
                if j == 1 and not first_group(g):
                    act.wait_ge(s["oT_ps"], g)
                    nc.scalar.activation(oT[:], misc, ACT.Copy).then_inc(s["oT_ready"], 1)
                high_part(b, 0)
                high_part(b, 1)
                high_part(b, 2)
                if j == 2 and not last_group(g):
                    qT_side(g + 1, 1 - par)
                high_part(b, 3)
                if not last:
                    exps(b + 1, j + 1)
                if j == 1 and not last_group(g):
                    z3T_side(g + 1)

            act.wait_ge(s["q_bias_ready"], 1)
            act.wait_ge(s["const_loaded"], n_const)
            z3T_side(0)
            kT_side(0, 0)
            qT_side(0, 0)
            exps(0, 0)
            groups(act, slot)
            act.wait_ge(s["oT_ps"], NG)
            nc.scalar.activation(oT[:], misc, ACT.Copy).then_inc(s["oT_ready"], 1)

        @block.tensor
        def _(pe):
            def t3(g):
                pe.wait_ge(s["z3_ready"], g + 1)
                if some(g - 1):
                    pe.wait_ge(s["x_out"], g - 1)
                for t in range(G4):
                    last = nc.tensor.transpose(misc[:, t * P:(t + 1) * P], z3[:, t, :], ident[:])
                last.then_inc(s["z3T_ps"], 1)

            def keys(g, par):
                pe.wait_ge(s["z3T_ready"], g + 1)
                pe.wait_ge(s["ctx_loaded"], 16 * g + 16)
                nc.tensor.matmul(misc[:, 0:G4 * S2], wk[:], cT[par][:], start=True, stop=True).then_inc(s["k_ps"], 1)

            def queries(g):
                pe.wait_ge(s["kT_ready"], g + 1)
                nc.tensor.matmul(misc, wq[:], z3T[:], start=True, stop=True).then_inc(s["q_ps"], 1)

            def values(g, par):
                pe.wait_ge(s["qT_ready"], g + 1)
                for t in range(G4):
                    last = nc.tensor.matmul(misc[0:S2, t * P:(t + 1) * P], cT[par][:, t * S2:(t + 1) * S2], wv[:], start=True, stop=True)
                last.then_inc(s["v_ps"], 1)

            def scores(b, j, par):
                pe.wait_ge(s["Kb_ready"], b + 1)
                if some(b):
                    pe.wait_ge(s["Sd_ready"], b)
                neg = over(masked[:, bass.ds(b * S2, S2)], 1, HB)
                for a in range(NQ):
                    nc.tensor.matmul(S[:, a], qT[par][:, j * P:(j + 1) * P], Kb[j % 2][:, HB * a:HB * a + HB, :], start=True, stop=False)
                    last = nc.tensor.matmul(S[:, a], first_row[:], neg, start=False, stop=True)
                last.then_inc(s["S_ps"], 1)

            def turn(b, j, q):
                n = NQ * b + q
                if q == 0:
                    pe.wait_ge(s["P_ready"], b + 1)
                if some(n - 1):
                    pe.wait_ge(s["lo_ready"], n - 1)
                for h in range(HB):
                    last = nc.tensor.transpose(PT[q % 2][0:S2, h * P:(h + 1) * P], Pr[j % 2][:, HB * q + h, :], ident[:])
                last.then_inc(s["PT_ps"], 1)

            def weigh(b, j, par, q):
                n = NQ * b + q
                pe.wait_ge(s["hi_ready"], n + 1)
                pe.wait_ge(s["lo_ready"], n + 1)
                if q == 0:
                    if some(b):
                        pe.wait_ge(s["o_ready"], b)
                for h in range(HB * q, HB * q + HB):
                    nc.tensor.matmul(O[:, h, :], hi[:, h * P:(h + 1) * P], V[par][:, j, h, :], start=True, stop=False)
                    last = nc.tensor.matmul(O[:, h, :], lo[:, h * P:(h + 1) * P], V[par][:, j, h, :], start=False, stop=True)
                last.then_inc(s["pv_done"], 1)

            def turn_out(g):
                pe.wait_ge(s["o_ready"], G4 * g + G4)
                if last_group(g):
                    pe.wait_ge(s["x_out"], g)
                else:
                    pe.wait_ge(s["vb_ready"], g + 2)
                for t in range(G4):
                    last = nc.tensor.transpose(misc[:, t * P:(t + 1) * P], o[:, t, :], ident[:])
                last.then_inc(s["oT_ps"], 1)

            def project_out(g):
                pe.wait_ge(s["oT_ready"], g + 1)
                for t in range(G4):
                    last = nc.tensor.matmul(misc[:, t * P:(t + 1) * P], oT[:, t * P:(t + 1) * P], wo[:], start=True, stop=True)
                last.then_inc(s["out_ps"], 1)

            def slot(g, par, j):
                b = G4 * g + j
                last = last_group(g) and j == G4 - 1
                if j == 1 and not first_group(g):
                    turn_out(g - 1)
                if j == 2 and not last_group(g):
                    keys(g + 1, 1 - par)
                if j == 0:
                    pe.wait_ge(s["v3_ready"], g + 1)
                turn(b, j, 0)
                turn(b, j, 1)
                if j == 1 and not first_group(g):
                    project_out(g - 1)
                if not last:
                    if j == 3:
                        pe.wait_ge(s["qT_ready"], g + 2)
                        scores(b + 1, 0, 1 - par)
                    else:
                        scores(b + 1, j + 1, par)
                weigh(b, j, par, 0)
                turn(b, j, 2)
                weigh(b, j, par, 1)
                if j == 2 and not last_group(g):
                    queries(g + 1)
                turn(b, j, 3)
                weigh(b, j, par, 2)
                weigh(b, j, par, 3)
                if j == 1 and not last_group(g):
                    t3(g + 1)
                if j == 2 and not last_group(g):
                    values(g + 1, 1 - par)

            pe.wait_ge(s["const_loaded"], n_const)
            pe.wait_ge(s["mask_ready"], 1)
            t3(0)
            keys(0, 0)
            queries(0)
            values(0, 0)
            pe.wait_ge(s["vb_ready"], 1)
            pe.wait_ge(s["qT_ready"], 1)
            scores(0, 0, 0)
            groups(pe, slot)
            turn_out(NG - 1)
            project_out(NG - 1)


def route(nc, d, X, ident, neghalf, psum, banks, xg, W, IDX):
    with ExitStack() as ctx:
        def sb(name, shape, dt=F32):
            return ctx.enter_context(nc.sbuf_tensor(name, shape, dt))

        def sem(name):
            return ctx.enter_context(nc.semaphore(name))

        KE = K2 * E
        gate_w = sb("gate_w", [P, E])
        expert_no = sb("expert_no", [P, E])
        slot_base = sb("slot_base", [P, K2])
        earlier = sb("earlier", [P, P], BF16)
        ones = sb("ones", [P, P], BF16)
        mom4, stat4 = sb("mom4", [P, G4, 2]), sb("stat4", [P, G4, 6])
        var4, rs4 = sb("var4", [P, G4]), sb("rs4", [P, G4])
        z4 = [sb(f"z4{i}", [P, G4, P]) for i in range(2)]
        z4T = sb("z4T", [P, G4 * P])
        top, total, rtotal = sb("top", [P, G4]), sb("total", [P, G4]), sb("rtotal", [P, G4])
        dl, ex, pr, pr2 = (sb(n, [P, G4, E]) for n in ("dl", "ex", "pr", "pr2"))
        is_top = sb("is_top", [P, G4, E])
        best, chosen = sb("best", [P, K2, G4]), sb("chosen", [P, K2, G4])
        hot = sb("hot", [P, G4, K2, E])
        hotb, before = sb("hotb", [P, G4, KE], BF16), sb("before", [P, G4, KE], BF16)
        count = sb("count", [P, G4 + 1, KE])
        pair, rpair = sb("pair", [P, G4]), sb("rpair", [P, G4])
        weight = sb("weight", [P, G4, K2])
        ranked = sb("ranked", [P, G4, K2, E])
        rank, row, drop = (sb(n, [P, G4, K2]) for n in ("rank", "row", "drop"))
        idx = [sb(f"idx{i}", [P, G4, K2], I32) for i in range(2)]

        names = ("passed const_loaded count_ready ln4_stats ln4_moments ln4_var ln4_rstd z4_ready z4T_ps z4T_ready gate_ps dl_ready ex_ready "
                 "hot_ready rank_ps idx_ready step scattered0 scattered1").split()
        s = {n: sem("c_" + n) for n in names}
        tp = banks[0]
        gate_ps = banks[1][:, 0:G4 * E].rearrange("p (t e) -> p t e", t=G4)
        rank_ps = banks[2][:, 0:G4 * KE]
        consts = [(gate_w, "gate_w"), (expert_no, "expert_no"), (slot_base, "slot_base"), (earlier, "earlier"), (ones, "ones")]
        n_const = 16 * len(consts)
        STEPS = 25
        block = ctx.enter_context(nc.Block())

        def xrow(g, t):
            return X[:, bass.ds(G4 * g + t, 1), :].rearrange("p a c -> p (a c)")

        @block.sync
        def _(sp):
            for t, n in consts:
                sp.dma_start(t[:], d[n]).then_inc(s["const_loaded"], 16)

        @block.gpsimd
        def _(pool):
            def ln4_scale(g):
                pool.wait_ge(s["ln4_moments"], g + 1)
                pool.sem_inc(s["passed"], 1)
                pool.tensor_scalar(var4[:], mom4[:, :, 1], EPS, None, ALU.add).then_inc(s["ln4_var"], 1)
                pool.wait_ge(s["ln4_var"], g + 1)
                pool.tensor_tensor(rs4[:], var4[:], neghalf[:, 0:G4], ALU.pow).then_inc(s["ln4_rstd"], 1)

            def scatter(g, par):
                pool.wait_ge(s["idx_ready"], g + 1)
                pool.sem_inc(s["passed"], 1)
                for t in range(G4):
                    for k in range(K2):
                        pool.indirect_dma_start(xg, bass.IndirectOffsetOnAxis(ap=idx[par][:, t, k:k + 1], axis=0), z4[par][:, t, :], None,
                                                bounds_check=ROWS - 1, oob_is_err=False).then_inc(s[f"scattered{par}"], 16)

            ln4_scale(0)
            with pool.Fori(0, NG - 2, 2) as g:
                ln4_scale(g + 1)
                scatter(g, 0)
                ln4_scale(g + 2)
                scatter(g + 1, 1)
            ln4_scale(NG - 1)
            scatter(NG - 2, 0)
            scatter(NG - 1, 1)
            for par in (0, 1):
                pool.wait_ge(s[f"scattered{par}"], 16 * G4 * K2 * NG // 2)

        @block.vector
        def _(dve):
            nc.vector.memset(count[:], 0.0).then_inc(s["count_ready"], 1)
            dve.wait_ge(s["count_ready"], 1)

            def ln4(g, par, pairs_before):
                for t in range(G4):
                    last = nc.vector.bn_stats(stat4[:, t, :], xrow(g, t))
                last.then_inc(s["ln4_stats"], 1)
                dve.wait_ge(s["ln4_stats"], g + 1)
                dve.sem_inc(s["passed"], 1)
                for t in range(G4):
                    last = nc.vector.bn_aggr(mom4[:, t, :], stat4[:, t, :])
                last.then_inc(s["ln4_moments"], 1)
                dve.wait_ge(s["ln4_rstd"], g + 1)
                dve.wait_ge(s["ln4_moments"], g + 1)
                if some(g - 1):
                    dve.wait_ge(s["z4T_ps"], g - 1)
                if some(16 * G4 * K2 * pairs_before):
                    dve.wait_ge(s[f"scattered{par}"], 16 * G4 * K2 * pairs_before)
                for t in range(G4):
                    last = nc.vector.tensor_scalar(z4[par][:, t, :], xrow(g, t), mom4[:, t, 0:1], rs4[:, t:t + 1], ALU.subtract, ALU.mult)
                last.then_inc(s["z4_ready"], 1)

            def choose(g, par):
                done = [0]

                def step(ins):
                    done[0] += 1
                    ins.then_inc(s["step"], 1)
                    dve.wait_ge(s["step"], STEPS * g + done[0])

                v = nc.vector
                dve.wait_ge(s["gate_ps"], g + 1)
                step(v.tensor_reduce(top[:], gate_ps, AX.X, ALU.max))
                v.tensor_tensor(dl[:], gate_ps, over(top[:], 2, E), ALU.subtract).then_inc(s["dl_ready"], 1)
                dve.wait_ge(s["ex_ready"], g + 1)
                step(v.tensor_reduce(total[:], ex[:], AX.X, ALU.add))
                step(v.reciprocal(rtotal[:], total[:]))
                step(v.tensor_tensor(pr[:], ex[:], over(rtotal[:], 2, E), ALU.mult))
                for k, p in ((0, pr), (1, pr2)):
                    step(v.tensor_reduce(best[:, k, :], p[:], AX.X, ALU.max))
                    step(v.tensor_tensor(is_top[:], p[:], over(best[:, k, :], 2, E), ALU.is_equal))
                    step(v.tensor_tensor(is_top[:], is_top[:], over(expert_no[:], 1, G4), ALU.mult))
                    step(v.tensor_reduce(chosen[:, k, :], is_top[:], AX.X, ALU.min))
                    step(v.tensor_tensor(hot[:, :, k, :], over(chosen[:, k, :], 2, E), over(expert_no[:], 1, G4), ALU.is_equal))
                    if k == 0:
                        step(v.scalar_tensor_tensor(pr2[:], hot[:, :, 0, :], -2.0, pr[:], ALU.mult, ALU.add))
                hotf = hot[:].rearrange("p t k e -> p t (k e)")
                v.tensor_copy(hotb[:], hotf)
                step(v.tensor_copy(count[:, 0, :], count[:, G4, :]))
                for t in range(G4):
                    step(v.tensor_tensor(count[:, t + 1, :], count[:, t, :], hotf[:, t, :], ALU.add))
                v.tensor_copy(before[:], count[:, 0:G4, :]).then_inc(s["hot_ready"], 1)
                step(v.scalar_tensor_tensor(pair[:], best[:, 0, :], 1e-9, best[:, 1, :], ALU.add, ALU.add))
                v.reciprocal(rpair[:], pair[:])
                dve.wait_ge(s["rank_ps"], g + 1)
                step(v.tensor_tensor(ranked[:].rearrange("p t k e -> p t (k e)"), rank_ps.rearrange("p (t c) -> p t c", t=G4), hotf, ALU.mult))
                v.tensor_tensor(weight[:], best[:].rearrange("p k t -> p t k"), over(rpair[:], 2, K2), ALU.mult)
                step(v.tensor_reduce(rank[:], ranked[:], AX.X, ALU.add))
                v.tensor_scalar(drop[:], rank[:], float(CAP), OUT_OF_RANGE, ALU.is_ge, ALU.mult)
                v.scalar_tensor_tensor(row[:], chosen[:].rearrange("p k t -> p t k"), float(K2 * CAP), rank[:], ALU.mult, ALU.add)
                step(v.scalar_tensor_tensor(W[:, bass.ts(g, G4), :], rank[:], float(CAP), weight[:], ALU.is_lt, ALU.mult))
                step(v.tensor_tensor(row[:], row[:], over(slot_base[:], 1, G4), ALU.add))
                assert done[0] == STEPS, done
                v.tensor_tensor(idx[par][:], row[:], drop[:], ALU.add)
                v.tensor_tensor(IDX[:, bass.ts(g, G4), :], row[:], drop[:], ALU.add).then_inc(s["idx_ready"], 1)

            dve.wait_ge(s["const_loaded"], n_const)
            ln4(0, 0, 0)
            ln4(1, 1, 0)
            choose(0, 0)
            with dve.Fori(1, NG - 2, 2) as g:
                ln4(g + 1, 0, (g + 1) // 2)
                choose(g, 1)
                ln4(g + 2, 1, (g + 1) // 2)
                choose(g + 1, 0)
            choose(NG - 1, 1)
            dve.wait_ge(s["idx_ready"], NG)

        @block.scalar
        def _(act):
            act.wait_ge(s["const_loaded"], n_const)

            def z4T_side(g):
                act.wait_ge(s["z4T_ps"], g + 1)
                if some(g):
                    act.wait_ge(s["gate_ps"], g)
                nc.scalar.activation(z4T[:], tp, ACT.Copy).then_inc(s["z4T_ready"], 1)

            def exps(g):
                act.wait_ge(s["dl_ready"], g + 1)
                nc.scalar.activation(ex[:], dl[:], ACT.Exp).then_inc(s["ex_ready"], 1)

            z4T_side(0)
            with act.Fori(0, NG - 1) as g:
                exps(g)
                z4T_side(g + 1)
            exps(NG - 1)

        @block.tensor
        def _(pe):
            def logits(g, par):
                pe.wait_ge(s["z4_ready"], g + 1)
                if some(g):
                    pe.wait_ge(s["z4T_ready"], g)
                for t in range(G4):
                    last = nc.tensor.transpose(tp[:, t * P:(t + 1) * P], z4[par][:, t, :], ident[:])
                last.then_inc(s["z4T_ps"], 1)
                pe.wait_ge(s["z4T_ready"], g + 1)
                if some(g):
                    pe.wait_ge(s["dl_ready"], g)
                for t in range(G4):
                    last = nc.tensor.matmul(gate_ps[:, t, :], z4T[:, t * P:(t + 1) * P], gate_w[:], start=True, stop=True)
                last.then_inc(s["gate_ps"], 1)

            def ranks(g):
                pe.wait_ge(s["hot_ready"], g + 1)
                nc.tensor.matmul(rank_ps, earlier[:], hotb[:].rearrange("p t c -> p (t c)"), start=True, stop=False)
                nc.tensor.matmul(rank_ps, ones[:], before[:].rearrange("p t c -> p (t c)"), start=False, stop=True).then_inc(s["rank_ps"], 1)

            pe.wait_ge(s["const_loaded"], n_const)
            logits(0, 0)
            with pe.Fori(0, NG - 2, 2) as g:
                logits(g + 1, 1)
                ranks(g)
                logits(g + 2, 0)
                ranks(g + 1)
            logits(NG - 1, 1)
            ranks(NG - 2)
            ranks(NG - 1)


def experts(nc, d, ident, psum, banks, xg, yg):
    with ExitStack() as ctx:
        def sb(name, shape, dt=F32):
            return ctx.enter_context(nc.sbuf_tensor(name, shape, dt))

        def sem(name):
            return ctx.enter_context(nc.semaphore(name))

        HC = HID // P
        NE = E * EG
        gate = [sb(f"gate{i}", [P, HID]) for i in range(2)]
        up = [sb(f"up{i}", [P, HID]) for i in range(2)]
        down = [sb(f"down{i}", [P, HC, P]) for i in range(2)]
        xin = sb("xin", [P, G4, P])
        xT = sb("xT", [P, GROUP_ROWS])
        act_g = sb("act_g", [P, HC, GROUP_ROWS])
        h = sb("h", [P, HC, GROUP_ROWS])
        yo = sb("yo", [P, G4, P])
        names = "w0_loaded w1_loaded x_loaded xT_ps xT_ready gate_ps up_ps g_ready h_ready y_ps y_ready y_stored".split()
        s = {n: sem("e_" + n) for n in names}
        gate_ps, up_ps = banks[0:2], banks[2:4]
        tp, y_ps = banks[4], banks[5].rearrange("p (t c) -> p t c", t=G4)
        block = ctx.enter_context(nc.Block())

        free = {"y_ps": 1, "h_ready": 1, "g_ready": 1, "y_ready": 1, "y_stored": 16}

        def grant(eng, *steps):
            for name in steps:
                eng.sem_inc(s[name], free[name])

        def groups(eng, body):
            with eng.Fori(0, E - 1, 2) as e:
                for par in (0, 1):
                    with eng.Fori(0, EG) as i:
                        body((e + par) * EG + i, par, e)

        @block.sync
        def _(sp):
            def load(n):
                sp.dma_start(xin[:], xg[bass.ts(n, GROUP_ROWS), :].rearrange("(p t) c -> p t c", p=P)).then_inc(s["x_loaded"], 16)

            grant(sp, "y_stored")
            load(0)
            with sp.Fori(0, NE) as n:
                sp.wait_ge(s["xT_ps"], n + 1)
                load(n + 1)
                sp.wait_ge(s["y_ready"], n + 2)
                sp.dma_start(yg[bass.ts(n, GROUP_ROWS), :].rearrange("(p t) c -> p t c", p=P), yo[:]).then_inc(s["y_stored"], 16)
            sp.wait_ge(s["y_stored"], 16 * NE + 16)
            sp.wait_ge(s["x_loaded"], 16 * NE + 16)

        @block.gpsimd
        def _(pool):
            def load(e, par):
                for t, n in ((gate[par], "gate_proj"), (up[par], "up_proj"), (down[par], "down_proj")):
                    src = d[n][:, bass.ds(e, 1)]
                    src = src.rearrange("p a c -> p (a c)") if len(src.shape) == 3 else src.rearrange("p a b c -> p (a b) c")
                    pool.dma_start(t[:], src).then_inc(s[f"w{par}_loaded"], 16)

            load(0, 0)
            load(1, 1)
            with pool.Fori(2, E - 1, 2) as e:
                for par in (0, 1):
                    pool.wait_ge(s["y_ps"], EG * (e + par - 1) + 1)
                    load(e + par, par)

        @block.vector
        def _(dve):
            def body(n, par, e):
                for c in range(HC):
                    dve.wait_ge(s["g_ready"], HC * n + c + 2)
                    dve.wait_ge(s["up_ps"], HC * n + c + 1)
                    dve.wait_ge(s["y_ps"], n + 1)
                    nc.vector.tensor_tensor(h[:, c, :], up_ps[c], act_g[:, c, :], ALU.mult).then_inc(s["h_ready"], 1)

            grant(dve, "h_ready")
            groups(dve, body)

        @block.scalar
        def _(act):
            def x_side(n):
                act.wait_ge(s["xT_ps"], n + 1)
                if some(HC * n):
                    act.wait_ge(s["up_ps"], HC * n)
                nc.scalar.activation(xT[:], tp, ACT.Copy).then_inc(s["xT_ready"], 1)

            def body(n, par, e):
                for c in range(HC):
                    act.wait_ge(s["gate_ps"], HC * n + c + 1)
                    act.wait_ge(s["h_ready"], HC * n + 1)
                    nc.scalar.activation(act_g[:, c, :], gate_ps[c], ACT.Silu).then_inc(s["g_ready"], 1)
                x_side(n + 1)
                act.wait_ge(s["y_ps"], n + 2)
                act.wait_ge(s["y_stored"], 16 * n + 16)
                nc.scalar.activation(yo[:], y_ps, ACT.Copy).then_inc(s["y_ready"], 1)

            grant(act, "g_ready", "y_ready")
            x_side(0)
            groups(act, body)

        @block.tensor
        def _(pe):
            def turn(n):
                pe.wait_ge(s["x_loaded"], 16 * n + 16)
                if some(n):
                    pe.wait_ge(s["xT_ready"], n)
                for t in range(G4):
                    last = nc.tensor.transpose(tp[:, t * P:(t + 1) * P], xin[:, t, :], ident[:])
                last.then_inc(s["xT_ps"], 1)

            def body(n, par, e):
                pe.wait_ge(s[f"w{par}_loaded"], 16 * 3 * (e // 2) + 48)
                pe.wait_ge(s["xT_ready"], n + 1)
                for c in range(HC):
                    pe.wait_ge(s["g_ready"], HC * n + 1)
                    nc.tensor.matmul(gate_ps[c], gate[par][:, c * P:(c + 1) * P], xT[:], start=True, stop=True).then_inc(s["gate_ps"], 1)
                for c in range(HC):
                    pe.wait_ge(s["h_ready"], HC * n + 1)
                    nc.tensor.matmul(up_ps[c], up[par][:, c * P:(c + 1) * P], xT[:], start=True, stop=True).then_inc(s["up_ps"], 1)
                turn(n + 1)
                pe.wait_ge(s["y_ready"], n + 1)
                for c in range(HC):
                    pe.wait_ge(s["h_ready"], HC * n + c + 2)
                    for t in range(G4):
                        last = nc.tensor.matmul(y_ps[:, t, :], h[:, c, t * P:(t + 1) * P], down[par][:, c, :],
                                                start=(c == 0 and t == 0), stop=(c == HC - 1), skip_group_check=True)
                last.then_inc(s["y_ps"], 1)

            grant(pe, "y_ps")
            turn(0)
            groups(pe, body)


def combine(nc, X, W, IDX, yg, out):
    with ExitStack() as ctx:
        def sb(name, shape, dt=F32):
            return ctx.enter_context(nc.sbuf_tensor(name, shape, dt))

        def sem(name):
            return ctx.enter_context(nc.semaphore(name))

        idx = [sb(f"gidx{i}", [P, G4, K2], I32) for i in range(2)]
        wt = [sb(f"gwt{i}", [P, G4, K2]) for i in range(2)]
        yb = [sb(f"yb{i}", [P, G4, K2, P]) for i in range(2)]
        part = [sb(f"part{i}", [P, G4, P]) for i in range(2)]
        ost = [sb(f"ost{i}", [P, G4, P]) for i in range(2)]
        names = "passed cleared idx_ready gathered0 gathered1 part_ready o_ready stored0 stored1".split()
        s = {n: sem("g_" + n) for n in names}
        block = ctx.enter_context(nc.Block())

        @block.sync
        def _(sp):
            with sp.Fori(0, NG - 1, 2) as g:
                for par in (0, 1):
                    sp.wait_ge(s["o_ready"], g + par + 1)
                    sp.dma_start(out[:, bass.ts(g + par, G4), :], ost[par][:]).then_inc(s[f"stored{par}"], 16)
            for par in (0, 1):
                sp.wait_ge(s[f"stored{par}"], 16 * NG // 2)

        @block.gpsimd
        def _(pool):
            pool.wait_ge(s["cleared"], 1)
            with pool.Fori(0, NG - 1, 2) as g:
                for par in (0, 1):
                    pool.wait_ge(s["idx_ready"], g + par + 1)
                    pool.sem_inc(s["passed"], 1)
                    for t in range(G4):
                        for k in range(K2):
                            pool.indirect_dma_start(yb[par][:, t, k, :], None, yg, bass.IndirectOffsetOnAxis(ap=idx[par][:, t, k:k + 1], axis=0),
                                                    bounds_check=ROWS - 1, oob_is_err=False).then_inc(s[f"gathered{par}"], 16)

        @block.vector
        def _(dve):
            for i in range(2):
                last = nc.vector.memset(yb[i][:], 0.0)
            last.then_inc(s["cleared"], 1)
            dve.wait_ge(s["cleared"], 1)

            def fetch(g, par):
                nc.vector.tensor_copy(wt[par][:], W[:, bass.ts(g, G4), :])
                nc.vector.tensor_copy(idx[par][:], IDX[:, bass.ts(g, G4), :]).then_inc(s["idx_ready"], 1)

            def add(g, par, half):
                dve.wait_ge(s[f"gathered{par}"], 16 * G4 * K2 * (half + 1))
                dve.wait_ge(s["idx_ready"], g + 1)
                for t in range(G4):
                    last = nc.vector.scalar_tensor_tensor(part[par][:, t, :], yb[par][:, t, 0, :], wt[par][:, t, 0:1],
                                                          X[:, bass.ds(G4 * g + t, 1), :].rearrange("p a c -> p (a c)"), ALU.mult, ALU.add)
                last.then_inc(s["part_ready"], 1)
                dve.wait_ge(s["part_ready"], g + 1)
                if some(16 * half):
                    dve.wait_ge(s[f"stored{par}"], 16 * half)
                for t in range(G4):
                    last = nc.vector.scalar_tensor_tensor(ost[par][:, t, :], yb[par][:, t, 1, :], wt[par][:, t, 1:2],
                                                          part[par][:, t, :], ALU.mult, ALU.add)
                last.then_inc(s["o_ready"], 1)
                dve.wait_ge(s["o_ready"], g + 1)

            fetch(0, 0)
            fetch(1, 1)
            for par in (0, 1):
                add(par, par, 0)
                fetch(par + 2, par)
            with dve.Fori(2, NG - 3, 2) as g:
                for par in (0, 1):
                    add(g + par, par, g // 2)
                    fetch(g + par + 2, par)
            for par in (0, 1):
                add(NG - 2 + par, par, NG // 2 - 1)


def lay_out(i):
    c = np.ascontiguousarray

    def col(a):
        return c(np.asarray(a).reshape(-1, P).T)

    def rows(a):
        return c(np.broadcast_to(np.asarray(a).reshape(1, -1), (P, np.asarray(a).size)))

    qkv_b = np.asarray(i["L0_attn_qkv_b"])
    head = np.arange(P) // HD
    first_row = (np.arange(P)[:, None] + np.zeros((1, P)) == 0).astype(mybir.dt.np(BF16))
    return {
        "x": c(np.asarray(i["x"]).transpose(1, 0, 2)),
        "qkv_w": c(i["L0_attn_qkv_w"]), "out_w": c(i["L0_attn_out_w"]), "w1": c(i["L0_attn_w1"]),
        "w2": c(np.asarray(i["L0_attn_w2"]).reshape(FC, P, P).transpose(1, 0, 2)),
        "q_bias": col(qkv_b[0:P]), "kb_row": rows(qkv_b[P:2 * P]), "vb_row": rows(qkv_b[2 * P:]),
        "ob_row": rows(i["L0_attn_out_b"]), "b2_row": rows(i["L0_attn_b2"]), "b1": col(i["L0_attn_b1"]),
        "g1": col(i["L0_attn_g1"]), "be1": col(i["L0_attn_be1"]), "g2": col(i["L0_attn_g2"]), "be2": col(i["L0_attn_be2"]),
        "wq": c(np.asarray(i["L0_xattn_Wq"]).T), "wk": c(np.asarray(i["L0_xattn_Wk"]).T),
        "wv": c(np.asarray(i["L0_xattn_Wv"]).T), "wo": c(np.asarray(i["L0_xattn_Wo"]).T),
        "bq": col(i["L0_xattn_bq"]), "bk": col(i["L0_xattn_bk"]),
        "bv_row": rows(i["L0_xattn_bv"]), "bo_row": rows(i["L0_xattn_bo"]),
        "ctxT": c(np.asarray(i["ctx_1024"]).transpose(2, 0, 1).reshape(P, B * S2)),
        "mask": c(np.asarray(i["mask_BxS2_bf0"]).reshape(1, B * S2)),
        "first_row": first_row,
        "gate_w": c(np.asarray(i["L0_ffn_gate_w"]).T),
        "gate_proj": c(np.asarray(i["L0_ffn_gate_proj_w"]).transpose(2, 0, 1)),
        "up_proj": c(np.asarray(i["L0_ffn_up_proj_w"]).transpose(2, 0, 1)),
        "down_proj": c(np.asarray(i["L0_ffn_down_proj_w"]).reshape(E, P, HID // P, P).transpose(3, 0, 2, 1)),
        "expert_no": rows(np.arange(E, dtype=np.float32) - E),
        "slot_base": rows(np.arange(K2, dtype=np.float32) * CAP + E * K2 * CAP),
        "earlier": np.triu(np.ones((P, P)), 1).astype(mybir.dt.np(BF16)),
        "ones": np.ones((P, P)).astype(mybir.dt.np(BF16)),
        "ident": np.eye(P, dtype=np.float32),
        "block_mask": (head[:, None] == head[None, :]).astype(np.float32),
        "head_mask": (head[:, None] == np.arange(H)[None, :]).astype(np.float32),
    }


def kernel(**inputs):
    import concourse.bacc as _bacc
    from concourse import mybir as _mybir
    from concourse.bass_utils import run_bass_kernel_spmd as _run

    nc = _bacc.Bacc("TRN2", target_bir_lowering=False, num_devices=1)
    arrays, d = {}, {}
    for name, a in lay_out(inputs).items():
        arrays[f"in_{name}"] = a
        d[name] = nc.dram_tensor(f"in_{name}", a.shape, _mybir.dt.from_np(a.dtype), kind="ExternalInput").ap()
    out = nc.dram_tensor("out", (P, B, P), F32, kind="ExternalOutput").ap()
    build(nc, d, out)
    r = _run(nc, [arrays], core_ids=[0])
    return np.ascontiguousarray(r.results[0]["out"].transpose(1, 0, 2))
```

```python
from contextlib import ExitStack

import numpy as np

import concourse.bass as bass
from concourse import mybir

F32 = mybir.dt.float32
BF16 = mybir.dt.bfloat16
F16 = mybir.dt.float16
I32 = mybir.dt.int32
U8 = mybir.dt.uint8
ALU = mybir.AluOpType
ACT = mybir.ActivationFunctionType
AX = mybir.AxisListType

P = 128
B = 64
G4 = 4
NG = B // G4
H = 16
HD = P // H
S2 = 77
HB = 4
NQ = H // HB
FF = 512
FC = FF // P
E = 8
HID = 256
K2 = 2
CAP = int(1.25 * B * P / E)
ROWS = E * K2 * CAP
GROUP_ROWS = G4 * P
EG = K2 * CAP // GROUP_ROWS
VC = 3 * HD + 1
EPS = 1e-5
ATTN_EPS = 1e-6
OUT_OF_RANGE = 1.0e6




def some(count):
    return not isinstance(count, int) or count > 0


def over(ap, axis, n):
    a = ap.unsqueeze(axis)
    shape = list(a.shape)
    shape[axis] = n
    return a.broadcast_to(shape)


def build(nc, d, out):
    ctx = ExitStack()
    with ctx:
        def sb(name, shape, dt=F32):
            return ctx.enter_context(nc.sbuf_tensor(name, shape, dt))

        def sem(name):
            return ctx.enter_context(nc.semaphore(name))

        X = sb("X", [P, B, P])
        ident = sb("ident", [P, P])
        block_mask = sb("block_mask", [P, P])
        head_mask = sb("head_mask", [P, H])
        neghalf = sb("neghalf", [P, 8])
        psum = ctx.enter_context(nc.psum_tensor("psum", [P, 8, 512], F32))
        banks = [psum[:, i, :] for i in range(8)]

        xg = nc.dram_tensor("dispatched", [ROWS + GROUP_ROWS, P], F32, kind="Internal").ap()
        yg = nc.dram_tensor("expert_out", [ROWS, P], F32, kind="Internal").ap()

        W = sb("W", [P, B, K2])
        IDX = sb("IDX", [P, B, K2], I32)

        linear_attention_and_ffn(nc, d, X, ident, block_mask, head_mask, neghalf, psum, banks, xg)
        cross_attention_and_routing(nc, d, X, ident, head_mask, neghalf, psum, banks, xg, W, IDX)
        experts(nc, d, ident, psum, banks, xg, yg)
        combine(nc, X, W, IDX, yg, out)


def linear_attention_and_ffn(nc, d, X, ident, block_mask, head_mask, neghalf, psum, banks, xg):
    with ExitStack() as ctx:
        def sb(name, shape, dt=F32):
            return ctx.enter_context(nc.sbuf_tensor(name, shape, dt))

        def sem(name):
            return ctx.enter_context(nc.semaphore(name))

        qkv_w = sb("qkv_w", [P, 3 * P])
        out_w = sb("out_w", [P, P])
        w1 = sb("w1", [P, FF])
        w2 = sb("w2", [P, FC, P])
        kb_row, vb_row, ob_row, b2_row = (sb(n, [P, P]) for n in ("kb_row", "vb_row", "ob_row", "b2_row"))
        cols = sb("cols", [P, 6 + FC])
        q_bias, q_bias1, g1, be1, g2, be2 = (cols[:, i:i + 1] for i in range(6))
        zeros = sb("zeros", [P, 4, P])

        mom0, stat0 = sb("mom0", [P, G4, 2]), sb("stat0", [P, G4, 6])
        mom2, stat2 = sb("mom2", [P, G4, 2]), sb("stat2", [P, G4, 6])
        var0, rs0 = sb("var0", [P, 2, G4]), sb("rs0", [P, 2, G4])
        var2, rs2 = sb("var2", [P, G4]), sb("rs2", [P, G4])
        n0, n0b, z1, z2 = (sb(n, [P, G4, P]) for n in ("n0", "n0b", "z1", "z2"))
        ln1T, ln2T, yT = (sb(n, [P, G4 * P]) for n in ("ln1T", "ln2T", "yT"))
        kb, ek, ekm, kf = (sb(n, [P, G4, P]) for n in ("kb", "ek", "ekm", "kf"))
        eq, eqm, qf = (sb(n, [P, G4 * P]) for n in ("eq", "eqm", "qf"))
        v1 = sb("v1", [P, G4, P + 1])
        KV = sb("KV", [P, G4, P + H])
        den, rden = sb("den", [P, G4, H]), sb("rden", [P, G4, H])
        y, x1, x1b, xs = (sb(n, [P, G4, P]) for n in ("y", "x1", "x1b", "xs"))
        hT = sb("hT", [P, FC, G4 * P])

        names = ("passed const_loaded x_loaded zeros_ready zeros_stored neghalf_ready ones_ready "
                 "ln0_stats ln0_moments ln0_var ln0_rstd z1_ready n0_ready n0b_ready z1T_ps ln1T_ready "
                 "kv_ps q_ps kb_ready v_ready ek_ready eq_ready ekm_ready eqm_ready kf_ready qf_ready "
                 "KV_ps KV_ready y_ps den_ready rden_ready y_ready yT_ps yT_ready attn_ps x1_ready x1b_ready xs_ready "
                 "ln2_stats ln2_moments ln2_var ln2_rstd z2_ready z2T_ps ln2T_ready h_ps h_ready w2_ps x_out").split()
        s = {n: sem("a_" + n) for n in names}

        kvp = psum[:, 0:2, :].rearrange("p a (b c) -> p (a b) c", b=2)
        kvs = psum[:, 2:4, :].rearrange("p a (b c) -> p (a b) c", b=2)
        q_ps = banks[2]
        attn_ps = banks[3].rearrange("p (t c) -> p t c", t=G4)
        tp = banks[4]
        w2_ps = banks[5].rearrange("p (t c) -> p t c", t=G4)
        h_ps = [banks[6], banks[7]]

        block = ctx.enter_context(nc.Block())

        consts = [(qkv_w, "qkv_w"), (out_w, "out_w"), (w1, "w1"), (w2, "w2"), (kb_row, "kb_row"),
                  (vb_row, "vb_row"), (ob_row, "ob_row"), (b2_row, "b2_row"), (ident, "ident"),
                  (block_mask, "block_mask"), (head_mask, "head_mask")]
        COLS = ["q_bias", "g1", "be1", "g2", "be2"]
        n_const = 16 * (len(consts) + len(COLS) + 1)

        @block.sync
        def _(sp):
            sp.dma_start(X[:, 0:G4, :], d["x"][:, 0:G4, :]).then_inc(s["x_loaded"], 16)
            for t, n in consts:
                sp.dma_start(t[:], d[n]).then_inc(s["const_loaded"], 16)
            for i, n in zip((0, 2, 3, 4, 5), COLS):
                sp.dma_start(cols[:, i:i + 1], d[n]).then_inc(s["const_loaded"], 16)
            sp.dma_start(cols[:, 6:6 + FC], d["b1"]).then_inc(s["const_loaded"], 16)
            with sp.Fori(1, NG) as g:
                sp.wait_ge(s["x_loaded"], 16 * g)
                sp.dma_start(X[:, bass.ts(g, G4), :], d["x"][:, bass.ts(g, G4), :]).then_inc(s["x_loaded"], 16)
            sp.wait_ge(s["zeros_ready"], 1)
            with sp.Fori(0, (ROWS + GROUP_ROWS) // GROUP_ROWS) as i:
                sp.dma_start(xg[bass.ts(i, GROUP_ROWS), :].rearrange("(p a) c -> p a c", p=P),
                             zeros[:]).then_inc(s["zeros_stored"], 16)
            sp.wait_ge(s["zeros_stored"], 16 * (ROWS + GROUP_ROWS) // GROUP_ROWS)

        @block.gpsimd
        def _(pool):
            pool.memset(neghalf[:], -0.5).then_inc(s["neghalf_ready"], 1)
            pool.memset(zeros[:], 0.0).then_inc(s["zeros_ready"], 1)
            pool.wait_ge(s["const_loaded"], n_const)
            pool.wait_ge(s["neghalf_ready"], 1)
            pool.wait_ge(s["zeros_ready"], 1)

            def ln0_scale(g):
                pool.wait_ge(s["ln0_moments"], g + 1)
                pool.sem_inc(s["passed"], 1)
                pool.tensor_scalar(var0[:, 0, :], mom0[:, :, 1], EPS, None, ALU.add)
                pool.tensor_scalar(var0[:, 1, :], mom0[:, :, 1], 1.0 + EPS, EPS * EPS, ALU.mult, ALU.add).then_inc(s["ln0_var"], 1)
                pool.wait_ge(s["ln0_var"], g + 1)
                pool.tensor_tensor(rs0[:].rearrange("p a b -> p (a b)"), var0[:].rearrange("p a b -> p (a b)"),
                                   neghalf[:, 0:2 * G4], ALU.pow).then_inc(s["ln0_rstd"], 1)

            def add_out_bias(g):
                pool.wait_ge(s["n0_ready"], g + 1)
                if some(g):
                    pool.wait_ge(s["x1_ready"], g)
                pool.tensor_tensor(n0b[:], n0[:], over(ob_row[:], 1, G4), ALU.add).then_inc(s["n0b_ready"], 1)

            def clamp_exps(g):
                pool.wait_ge(s["ek_ready"], g + 1)
                if some(g):
                    pool.wait_ge(s["kf_ready"], g)
                pool.sem_inc(s["passed"], 1)
                pool.tensor_scalar(ekm[:], ek[:], 1.0, None, ALU.min).then_inc(s["ekm_ready"], 1)
                pool.wait_ge(s["eq_ready"], g + 1)
                if some(g):
                    pool.wait_ge(s["qf_ready"], g)
                pool.sem_inc(s["passed"], 1)
                pool.tensor_scalar(eqm[:], eq[:], 1.0, None, ALU.min).then_inc(s["eqm_ready"], 1)

            def ln2_scale(f):
                pool.wait_ge(s["ln2_moments"], f + 1)
                pool.sem_inc(s["passed"], 1)
                pool.tensor_scalar(var2[:], mom2[:, :, 1], EPS, None, ALU.add).then_inc(s["ln2_var"], 1)
                pool.wait_ge(s["ln2_var"], f + 1)
                pool.tensor_tensor(rs2[:], var2[:], neghalf[:, 0:G4], ALU.pow).then_inc(s["ln2_rstd"], 1)

            def residual(f):
                pool.wait_ge(s["x1_ready"], f + 1)
                pool.tensor_tensor(x1b[:], x1[:], over(b2_row[:], 1, G4), ALU.add).then_inc(s["x1b_ready"], 1)
                pool.wait_ge(s["x1b_ready"], f + 1)
                if some(f):
                    pool.wait_ge(s["x_out"], f)
                pool.tensor_tensor(xs[:], x1b[:], X[:, bass.ts(f, G4), :], ALU.add).then_inc(s["xs_ready"], 1)

            ln0_scale(0)
            add_out_bias(0)
            clamp_exps(0)
            ln0_scale(1)

            def both(g):
                ln2_scale(g - 1)
                add_out_bias(g)
                clamp_exps(g)
                residual(g - 1)
                ln0_scale(g + 1)

            both(1)
            with pool.Fori(2, NG - 1) as g:
                both(g)
            ln2_scale(NG - 2)
            add_out_bias(NG - 1)
            clamp_exps(NG - 1)
            residual(NG - 2)
            ln2_scale(NG - 1)
            residual(NG - 1)

        @block.vector
        def _(dve):
            nc.vector.memset(v1[:, :, P:P + 1], 1.0).then_inc(s["ones_ready"], 1)

            def ln0(g):
                dve.wait_ge(s["x_loaded"], 16 * g + 16)
                for t in range(G4):
                    last = nc.vector.bn_stats(stat0[:, t, :], X[:, bass.ds(G4 * g + t, 1), :].rearrange("p a c -> p (a c)"))
                last.then_inc(s["ln0_stats"], 1)
                dve.wait_ge(s["ln0_stats"], g + 1)
                dve.sem_inc(s["passed"], 1)
                for t in range(G4):
                    last = nc.vector.bn_aggr(mom0[:, t, :], stat0[:, t, :])
                last.then_inc(s["ln0_moments"], 1)
                dve.wait_ge(s["ln0_rstd"], g + 1)
                if some(g):
                    dve.wait_ge(s["z1T_ps"], g)
                dve.wait_ge(s["ln0_moments"], g + 1)
                for t in range(G4):
                    xt = X[:, bass.ds(G4 * g + t, 1), :].rearrange("p a c -> p (a c)")
                    last = nc.vector.tensor_scalar(z1[:, t, :], xt, mom0[:, t, 0:1], rs0[:, 1, t:t + 1], ALU.subtract, ALU.mult)
                last.then_inc(s["z1_ready"], 1)
                if some(g):
                    dve.wait_ge(s["n0b_ready"], g)
                for t in range(G4):
                    xt = X[:, bass.ds(G4 * g + t, 1), :].rearrange("p a c -> p (a c)")
                    last = nc.vector.tensor_scalar(n0[:, t, :], xt, mom0[:, t, 0:1], rs0[:, 0, t:t + 1], ALU.subtract, ALU.mult)
                last.then_inc(s["n0_ready"], 1)

            def features(g):
                dve.wait_ge(s["kv_ps"], g + 1)
                if some(g):
                    dve.wait_ge(s["ek_ready"], g)
                nc.vector.tensor_tensor(kb[:], kvp[:, :, 0:P], over(kb_row[:], 1, G4), ALU.add).then_inc(s["kb_ready"], 1)
                if some(g):
                    dve.wait_ge(s["KV_ps"], g)
                nc.vector.tensor_tensor(v1[:, :, 0:P], kvp[:, :, P:2 * P], over(vb_row[:], 1, G4), ALU.add).then_inc(s["v_ready"], 1)
                dve.wait_ge(s["ekm_ready"], g + 1)
                nc.vector.scalar_tensor_tensor(kf[:], kb[:], 1.0, ekm[:], ALU.add, ALU.max).then_inc(s["kf_ready"], 1)
                dve.wait_ge(s["eqm_ready"], g + 1)
                dve.wait_ge(s["q_ps"], g + 1)
                if some(g):
                    dve.wait_ge(s["y_ps"], g)
                nc.vector.scalar_tensor_tensor(qf[:], q_ps, q_bias1, eqm[:], ALU.add, ALU.max).then_inc(s["qf_ready"], 1)

            def mask_kv(g):
                dve.wait_ge(s["KV_ps"], g + 1)
                if some(g):
                    dve.wait_ge(s["y_ps"], g)
                nc.vector.tensor_tensor(KV[:, :, 0:P], kvs[:, :, 0:P], over(block_mask[:], 1, G4), ALU.mult)
                nc.vector.tensor_tensor(KV[:, :, P:P + H], kvs[:, :, P:P + 1].broadcast_to([P, G4, H]),
                                        over(head_mask[:], 1, G4), ALU.mult).then_inc(s["KV_ready"], 1)

            def normalise(g):
                dve.wait_ge(s["y_ps"], g + 1)
                nc.vector.tensor_scalar(den[:], kvp[:, :, P:P + H], ATTN_EPS, None, ALU.max).then_inc(s["den_ready"], 1)
                dve.wait_ge(s["den_ready"], g + 1)
                nc.vector.reciprocal(rden[:], den[:]).then_inc(s["rden_ready"], 1)
                dve.wait_ge(s["rden_ready"], g + 1)
                if some(g):
                    dve.wait_ge(s["yT_ps"], g)
                nc.vector.tensor_tensor(y[:].rearrange("p t (h c) -> p t h c", h=H),
                                        kvp[:, :, 0:P].rearrange("p t (h c) -> p t h c", h=H),
                                        over(rden[:], 3, HD), ALU.mult).then_inc(s["y_ready"], 1)

            def add_attention(g):
                dve.wait_ge(s["attn_ps"], g + 1)
                dve.wait_ge(s["n0b_ready"], g + 1)
                if some(g):
                    dve.wait_ge(s["x1b_ready"], g)
                if some(g):
                    dve.wait_ge(s["z2_ready"], g)
                nc.vector.tensor_tensor(x1[:], attn_ps, n0b[:], ALU.add).then_inc(s["x1_ready"], 1)

            def ln2(f):
                dve.wait_ge(s["x1_ready"], f + 1)
                for t in range(G4):
                    last = nc.vector.bn_stats(stat2[:, t, :], x1[:, t, :])
                last.then_inc(s["ln2_stats"], 1)
                dve.wait_ge(s["ln2_stats"], f + 1)
                dve.sem_inc(s["passed"], 1)
                for t in range(G4):
                    last = nc.vector.bn_aggr(mom2[:, t, :], stat2[:, t, :])
                last.then_inc(s["ln2_moments"], 1)
                dve.wait_ge(s["ln2_rstd"], f + 1)
                if some(f):
                    dve.wait_ge(s["z2T_ps"], f)
                dve.wait_ge(s["ln2_moments"], f + 1)
                for t in range(G4):
                    last = nc.vector.tensor_scalar(z2[:, t, :], x1[:, t, :], mom2[:, t, 0:1], rs2[:, t:t + 1], ALU.subtract, ALU.mult)
                last.then_inc(s["z2_ready"], 1)

            def finish(f):
                dve.wait_ge(s["w2_ps"], f + 1)
                dve.wait_ge(s["xs_ready"], f + 1)
                nc.vector.tensor_tensor(X[:, bass.ts(f, G4), :], w2_ps, xs[:], ALU.add).then_inc(s["x_out"], 1)

            dve.wait_ge(s["const_loaded"], n_const)
            nc.vector.tensor_scalar(q_bias1, q_bias, 1.0, None, ALU.add).then_inc(s["ones_ready"], 1)
            dve.wait_ge(s["ones_ready"], 2)
            ln0(0)
            features(0)
            mask_kv(0)
            normalise(0)
            ln0(1)
            add_attention(0)

            def both(g):
                ln2(g - 1)
                features(g)
                mask_kv(g)
                normalise(g)
                ln0(g + 1)
                finish(g - 1)
                add_attention(g)

            both(1)
            with dve.Fori(2, NG - 1) as g:
                both(g)
            ln2(NG - 2)
            features(NG - 1)
            mask_kv(NG - 1)
            normalise(NG - 1)
            finish(NG - 2)
            add_attention(NG - 1)
            ln2(NG - 1)
            finish(NG - 1)
            dve.wait_ge(s["x_out"], NG)

        @block.scalar
        def _(act):
            def attention_side(g):
                act.wait_ge(s["z1T_ps"], g + 1)
                if some(g):
                    act.wait_ge(s["kv_ps"], g)
                if some(g):
                    act.wait_ge(s["q_ps"], g)
                nc.scalar.activation(ln1T[:], tp, ACT.Identity, scale=g1, bias=be1).then_inc(s["ln1T_ready"], 1)
                act.wait_ge(s["kb_ready"], g + 1)
                if some(g):
                    act.wait_ge(s["ekm_ready"], g)
                nc.scalar.activation(ek[:], kb[:], ACT.Exp).then_inc(s["ek_ready"], 1)
                act.wait_ge(s["q_ps"], g + 1)
                if some(g):
                    act.wait_ge(s["eqm_ready"], g)
                nc.scalar.activation(eq[:], q_ps, ACT.Exp, bias=q_bias).then_inc(s["eq_ready"], 1)

            def ffn_side(f):
                act.wait_ge(s["z2T_ps"], f + 1)
                if some(FC * f):
                    act.wait_ge(s["h_ps"], FC * f)
                nc.scalar.activation(ln2T[:], tp, ACT.Identity, scale=g2, bias=be2).then_inc(s["ln2T_ready"], 1)
                if some(f):
                    act.wait_ge(s["w2_ps"], f)
                for c in range(FC):
                    act.wait_ge(s["h_ps"], FC * f + c + 1)
                    nc.scalar.activation(hT[:, c, :], h_ps[c % 2], ACT.Gelu, bias=cols[:, 6 + c:7 + c]).then_inc(s["h_ready"], 1)

            def yT_side(g):
                act.wait_ge(s["yT_ps"], g + 1)
                if some(g):
                    act.wait_ge(s["attn_ps"], g)
                nc.scalar.activation(yT[:], tp, ACT.Copy).then_inc(s["yT_ready"], 1)

            act.wait_ge(s["const_loaded"], n_const)
            attention_side(0)
            yT_side(0)

            def both(g):
                attention_side(g)
                ffn_side(g - 1)
                yT_side(g)

            both(1)
            with act.Fori(2, NG) as g:
                both(g)
            ffn_side(NG - 1)

        @block.tensor
        def _(pe):
            def t1(g):
                pe.wait_ge(s["z1_ready"], g + 1)
                if some(g):
                    pe.wait_ge(s["yT_ready"], g)
                for t in range(G4):
                    last = nc.tensor.transpose(tp[:, t * P:(t + 1) * P], z1[:, t, :], ident[:])
                last.then_inc(s["z1T_ps"], 1)

            def project(g):
                pe.wait_ge(s["ln1T_ready"], g + 1)
                if some(g):
                    pe.wait_ge(s["y_ready"], g)
                for t in range(G4):
                    last = nc.tensor.matmul(kvp[:, t, :], ln1T[:, t * P:(t + 1) * P], qkv_w[:, P:3 * P], start=True, stop=True)
                last.then_inc(s["kv_ps"], 1)
                if some(g):
                    pe.wait_ge(s["KV_ready"], g)
                nc.tensor.matmul(q_ps, qkv_w[:, 0:P], ln1T[:], start=True, stop=True).then_inc(s["q_ps"], 1)

            def t2(f):
                pe.wait_ge(s["z2_ready"], f + 1)
                pe.wait_ge(s["ln1T_ready"], f + 2)
                for t in range(G4):
                    last = nc.tensor.transpose(tp[:, t * P:(t + 1) * P], z2[:, t, :], ident[:])
                last.then_inc(s["z2T_ps"], 1)

            def ffn_up(f):
                pe.wait_ge(s["ln2T_ready"], f + 1)
                for c in range(FC):
                    if c >= 2:
                        pe.wait_ge(s["h_ready"], FC * f + c - 1)
                    else:
                        if some(FC * f):
                            pe.wait_ge(s["h_ready"], FC * f)
                    nc.tensor.matmul(h_ps[c % 2], w1[:, c * P:(c + 1) * P], ln2T[:], start=True, stop=True).then_inc(s["h_ps"], 1)

            def context(g):
                pe.wait_ge(s["kf_ready"], g + 1)
                pe.wait_ge(s["v_ready"], g + 1)
                pe.wait_ge(s["qf_ready"], g + 1)
                if some(g):
                    pe.wait_ge(s["x1_ready"], g)
                for t in range(G4):
                    last = nc.tensor.matmul(kvs[:, t, 0:P + 1], kf[:, t, :], v1[:, t, :], start=True, stop=True)
                last.then_inc(s["KV_ps"], 1)

            def ffn_down(f, tiles):
                pe.wait_ge(s["h_ready"], FC * f + FC)
                if some(f):
                    pe.wait_ge(s["x_out"], f)
                for t in tiles:
                    for c in range(FC):
                        last = nc.tensor.matmul(w2_ps[:, t, :], hT[:, c, t * P:(t + 1) * P], w2[:, c, :],
                                                start=(c == 0), stop=(c == FC - 1))
                if tiles[-1] == G4 - 1:
                    last.then_inc(s["w2_ps"], 1)

            def attend(g):
                pe.wait_ge(s["KV_ready"], g + 1)
                pe.wait_ge(s["kb_ready"], g + 1)
                for t in range(G4):
                    last = nc.tensor.matmul(kvp[:, t, 0:P + H], qf[:, t * P:(t + 1) * P], KV[:, t, :], start=True, stop=True)
                last.then_inc(s["y_ps"], 1)

            def project_out(g, f):
                pe.wait_ge(s["y_ready"], g + 1)
                if some(f + 1):
                    pe.wait_ge(s["ln2T_ready"], f + 1)
                for t in range(G4):
                    last = nc.tensor.transpose(tp[:, t * P:(t + 1) * P], y[:, t, :], ident[:])
                last.then_inc(s["yT_ps"], 1)
                pe.wait_ge(s["yT_ready"], g + 1)
                for t in range(G4):
                    last = nc.tensor.matmul(attn_ps[:, t, :], yT[:, t * P:(t + 1) * P], out_w[:], start=True, stop=True)
                last.then_inc(s["attn_ps"], 1)

            pe.wait_ge(s["const_loaded"], n_const)
            pe.wait_ge(s["ones_ready"], 2)
            t1(0)
            project(0)
            context(0)
            attend(0)
            project_out(0, -1)

            def both(g):
                t1(g)
                project(g)
                t2(g - 1)
                ffn_up(g - 1)
                context(g)
                ffn_down(g - 1, (0, 1))
                attend(g)
                ffn_down(g - 1, (2, 3))
                project_out(g, g - 1)

            both(1)
            with pe.Fori(2, NG) as g:
                both(g)
            pe.wait_ge(s["z2_ready"], NG)
            pe.wait_ge(s["yT_ready"], NG)
            for t in range(G4):
                last = nc.tensor.transpose(tp[:, t * P:(t + 1) * P], z2[:, t, :], ident[:])
            last.then_inc(s["z2T_ps"], 1)
            ffn_up(NG - 1)
            ffn_down(NG - 1, (0, 1, 2, 3))


def cross_attention_and_routing(nc, d, X, ident, head_mask, neghalf, psum, banks, xg, W, IDX):
    with ExitStack() as ctx:
        def sb(name, shape, dt=F32):
            return ctx.enter_context(nc.sbuf_tensor(name, shape, dt))

        def sem(name):
            return ctx.enter_context(nc.semaphore(name))

        KE = K2 * E
        N = B * NQ
        M_ = G4 * NQ
        wq, wk, wv, wo = (sb(n, [P, P]) for n in ("wq", "wk", "wv", "wo"))
        bv_row, bo_row = sb("bv_row", [P, P]), sb("bo_row", [P, P])
        bcols = sb("bcols", [P, 3])
        first_row = sb("first_row", [P, P], BF16)
        masked = sb("masked", [P, B * S2], BF16)
        mask_u8 = sb("mask_u8", [1, B * S2], U8)

        mom3, stat3 = sb("mom3", [P, G4, 2]), sb("stat3", [P, G4, 6])
        var3, rs3 = sb("var3", [P, G4]), sb("rs3", [P, G4])
        z3 = sb("z3", [P, G4, P])
        z3T = sb("z3T", [P, G4 * P])
        cT = [sb(f"cT{i}", [P, G4 * S2]) for i in range(2)]
        qT = [sb(f"qT{i}", [P, G4 * P]) for i in range(2)]
        kT = [sb(f"kT{i}", [P, G4, S2]) for i in range(2)]
        Kb = [sb(f"Kb{i}", [P, H, S2]) for i in range(2)]
        vb, vr = sb("vb", [S2, G4, P]), sb("vr", [S2, G4, P])
        V = [sb(f"V{i}", [S2, G4, H, VC], BF16) for i in range(2)]
        top_score = sb("top_score", [P, H])
        Sd = sb("Sd", [P, H, S2])
        Pr = sb("Pr", [P, H, S2])
        hi, lo = sb("hi", [S2, H * P], F16), sb("lo", [S2, H * P], F16)
        osum, rsum = sb("osum", [P, H, HD]), sb("rsum", [P, H])
        o = sb("o", [P, G4, P])
        oT = sb("oT", [P, G4 * P])
        xb = sb("xb", [P, G4, P])

        gate_w = sb("gate_w", [P, E])
        expert_no = sb("expert_no", [P, E])
        slot_base = sb("slot_base", [P, K2])
        earlier = sb("earlier", [P, P], BF16)
        ones = sb("ones", [P, P], BF16)
        minus_one = sb("minus_one", [P, P], F16)
        mom4, stat4 = sb("mom4", [P, G4, 2]), sb("stat4", [P, G4, 6])
        var4, rs4 = sb("var4", [P, G4]), sb("rs4", [P, G4])
        z4 = [sb(f"z4{i}", [P, G4, P]) for i in range(2)]
        z4T = sb("z4T", [P, G4 * P])
        top, total, rtotal = sb("top", [P, G4]), sb("total", [P, G4]), sb("rtotal", [P, G4])
        dl, ex, pr, pr2 = (sb(n, [P, G4, E]) for n in ("dl", "ex", "pr", "pr2"))
        is_top = sb("is_top", [P, G4, E])
        best, chosen = sb("best", [P, K2, G4]), sb("chosen", [P, K2, G4])
        hot = sb("hot", [P, G4, K2, E])
        hotb, before = sb("hotb", [P, G4, KE], BF16), sb("before", [P, G4, KE], BF16)
        count = sb("count", [P, G4 + 1, KE])
        pair, rpair = sb("pair", [P, G4]), sb("rpair", [P, G4])
        weight = sb("weight", [P, G4, K2])
        ranked = sb("ranked", [P, G4, K2, E])
        rank, row, drop = (sb(n, [P, G4, K2]) for n in ("rank", "row", "drop"))
        idx = [sb(f"idx{i}", [P, G4, K2], I32) for i in range(2)]

        names = ("passed const_loaded ones_ready count_ready mask_ready q_bias_ready ctx_loaded "
                 "ln3_stats ln3_moments ln3_var ln3_rstd z3_ready z3T_ps z3T_ready q_ps qT_ready k_ps kT_ready "
                 "v_ps vb_ready v1_ready vr_ready v2_ready v3_ready Kb_ready S_ps M_ready Sd_ready P_ready PT_ps rest_ps "
                 "hi_ready lo_ready pv_done osum_ready rsum_ready o_ready oT_ps oT_ready out_ps xb_ready x_out "
                 "ln4_stats ln4_moments ln4_var ln4_rstd z4_ready z4T_ps z4T_ready gate_ps dl_ready ex_ready "
                 "hot_ready rank_ps ranked_ready idx_ready step scattered0 scattered1").split()
        s = {n: sem("b_" + n) for n in names}

        S = psum[:, 0:4, 0:HB * S2].rearrange("p a (h n) -> p a h n", h=HB)
        PT = [banks[4], banks[5]]
        O = banks[6][:, 0:H * VC].rearrange("p (h c) -> p h c", h=H)
        misc = banks[7]
        gate_ps = misc[:, 0:G4 * E].rearrange("p (t e) -> p t e", t=G4)
        rank_ps = misc[:, 0:G4 * KE]

        consts = [(wq, "wq"), (wk, "wk"), (wv, "wv"), (wo, "wo"), (bv_row, "bv_row"), (bo_row, "bo_row"),
                  (first_row, "first_row"), (mask_u8, "mask"), (gate_w, "gate_w"), (expert_no, "expert_no"),
                  (slot_base, "slot_base"), (earlier, "earlier"), (ones, "ones"),
                  (minus_one, "minus_one")]
        n_const = 16 * (len(consts) + 2)
        block = ctx.enter_context(nc.Block())

        def groups(eng, steps):
            steps(0, 0)
            steps(1, 1)
            with eng.Fori(2, NG - 3, 2) as g:
                steps(g, 0)
                steps(g + 1, 1)
            for g in range(NG - 2, NG + 2):
                steps(g, g % 2)

        def group(g):
            return not isinstance(g, int) or 0 <= g < NG

        def quarter(n):
            return not isinstance(n, int) or 0 <= n < N

        def xrow(g, t):
            return X[:, bass.ds(G4 * g + t, 1), :].rearrange("p a c -> p (a c)")

        @block.sync
        def _(sp):
            for t, n in consts:
                sp.dma_start(t[:], d[n]).then_inc(s["const_loaded"], 16)
            sp.dma_start(bcols[:, 0:1], d["bq"]).then_inc(s["const_loaded"], 16)
            sp.dma_start(bcols[:, 1:2], d["bk"]).then_inc(s["const_loaded"], 16)

            def load(g, par):
                if some(g - 1):
                    sp.wait_ge(s["v_ps"], g - 1)
                    sp.wait_ge(s["k_ps"], g - 1)
                    sp.sem_inc(s["passed"], 1)
                if some(g):
                    sp.wait_ge(s["ctx_loaded"], 16 * g)
                sp.dma_start(cT[par][:], d["ctxT"][:, bass.ts(g, G4 * S2)]).then_inc(s["ctx_loaded"], 16)

            load(0, 0)
            load(1, 1)
            with sp.Fori(2, NG - 1, 2) as g:
                load(g, 0)
                load(g + 1, 1)

        @block.gpsimd
        def _(pool):
            pool.memset(masked[:], 0.0).then_inc(s["ones_ready"], 1)
            for i in range(2):
                pool.memset(V[i][:, :, :, VC - 1:VC], 1.0).then_inc(s["ones_ready"], 1)
            pool.wait_ge(s["ones_ready"], 3)
            pool.wait_ge(s["const_loaded"], n_const)
            pool.tensor_scalar(masked[0:1, :], mask_u8[:], -3e38, 1e38, ALU.mult, ALU.mult).then_inc(s["mask_ready"], 1)

            def ln3_scale(g):
                pool.wait_ge(s["ln3_moments"], g + 1)
                pool.sem_inc(s["passed"], 1)
                pool.tensor_scalar(var3[:], mom3[:, :, 1], EPS, None, ALU.add).then_inc(s["ln3_var"], 1)
                pool.wait_ge(s["ln3_var"], g + 1)
                pool.tensor_tensor(rs3[:], var3[:], neghalf[:, 0:G4], ALU.pow).then_inc(s["ln3_rstd"], 1)

            def ln4_scale(g):
                pool.wait_ge(s["ln4_moments"], g + 1)
                pool.sem_inc(s["passed"], 1)
                pool.tensor_scalar(var4[:], mom4[:, :, 1], EPS, None, ALU.add).then_inc(s["ln4_var"], 1)
                pool.wait_ge(s["ln4_var"], g + 1)
                pool.tensor_tensor(rs4[:], var4[:], neghalf[:, 0:G4], ALU.pow).then_inc(s["ln4_rstd"], 1)

            def spread_keys(g, par, j):
                b = G4 * g + j
                pool.wait_ge(s["kT_ready"], g + 1)
                if some(b - 1):
                    pool.wait_ge(s["S_ps"], NQ * (b - 1))
                pool.tensor_tensor(Kb[j % 2][:], over(kT[par][:, j, :], 1, H), over(head_mask[:], 2, S2),
                                   ALU.mult).then_inc(s["Kb_ready"], 1)

            def first_rest(g, par):
                pool.wait_ge(s["v1_ready"], g + 1)
                pool.tensor_tensor(vr[:].rearrange("p t (h c) -> p (t h) c", h=H), vb[:].rearrange("p t (h c) -> p (t h) c", h=H),
                                   V[par][:, :, :, 0:HD].rearrange("p t h c -> p (t h) c"), ALU.subtract).then_inc(s["vr_ready"], 1)

            def second_rest(g, par):
                pool.wait_ge(s["v2_ready"], g + 1)
                pool.tensor_tensor(V[par][:, :, :, 2 * HD:3 * HD].rearrange("p t h c -> p (t h) c"), vr[:].rearrange("p t (h c) -> p (t h) c", h=H),
                                   V[par][:, :, :, HD:2 * HD].rearrange("p t h c -> p (t h) c"), ALU.subtract).then_inc(s["v3_ready"], 1)

            def add_out_bias(g):
                if some(g):
                    pool.wait_ge(s["x_out"], g)
                pool.tensor_tensor(xb[:], X[:, bass.ts(g, G4), :], over(bo_row[:], 1, G4), ALU.add).then_inc(s["xb_ready"], 1)

            def scatter(g, par, t):
                if t == 0:
                    pool.wait_ge(s["idx_ready"], g + 1)
                    pool.sem_inc(s["passed"], 1)
                for k in range(K2):
                    pool.indirect_dma_start(xg, bass.IndirectOffsetOnAxis(ap=idx[par][:, t, k:k + 1], axis=0), z4[par][:, t, :], None,
                                            bounds_check=ROWS - 1, oob_is_err=False).then_inc(s[f"scattered{par}"], 16)

            def steps(g, par):
                other = 1 - par
                if group(g):
                    spread_keys(g, par, 2)
                if group(g + 1):
                    ln3_scale(g + 1)
                if group(g - 1):
                    add_out_bias(g - 1)
                if group(g):
                    spread_keys(g, par, 3)
                if group(g - 1):
                    ln4_scale(g - 1)
                if group(g + 1):
                    spread_keys(g + 1, other, 0)
                if group(g - 2):
                    scatter(g - 2, par, 0)
                if group(g + 1):
                    first_rest(g + 1, other)
                if group(g - 2):
                    scatter(g - 2, par, 1)
                if group(g + 1):
                    spread_keys(g + 1, other, 1)
                if group(g - 2):
                    scatter(g - 2, par, 2)
                    scatter(g - 2, par, 3)
                if group(g + 1):
                    second_rest(g + 1, other)

            ln3_scale(0)
            spread_keys(0, 0, 0)
            spread_keys(0, 0, 1)
            first_rest(0, 0)
            second_rest(0, 0)
            groups(pool, steps)
            for par in (0, 1):
                pool.wait_ge(s[f"scattered{par}"], 16 * G4 * K2 * NG // 2)

        @block.vector
        def _(dve):
            v = nc.vector
            v.memset(count[:], 0.0).then_inc(s["count_ready"], 1)

            def ln3_stats(g):
                dve.sem_inc(s["passed"], 1)
                for t in range(G4):
                    last = v.bn_stats(stat3[:, t, :], xrow(g, t))
                last.then_inc(s["ln3_stats"], 1)

            def ln3_moments(g):
                dve.wait_ge(s["ln3_stats"], g + 1)
                dve.sem_inc(s["passed"], 1)
                for t in range(G4):
                    last = v.bn_aggr(mom3[:, t, :], stat3[:, t, :])
                last.then_inc(s["ln3_moments"], 1)

            def ln3_apply(g):
                dve.wait_ge(s["ln3_rstd"], g + 1)
                dve.wait_ge(s["ln3_moments"], g + 1)
                if some(g):
                    dve.wait_ge(s["z3T_ps"], g)
                for t in range(G4):
                    last = v.tensor_scalar(z3[:, t, :], xrow(g, t), mom3[:, t, 0:1], rs3[:, t:t + 1], ALU.subtract, ALU.mult)
                last.then_inc(s["z3_ready"], 1)

            def ln4_stats(g):
                dve.wait_ge(s["x_out"], g + 1)
                dve.sem_inc(s["passed"], 1)
                for t in range(G4):
                    last = v.bn_stats(stat4[:, t, :], xrow(g, t))
                last.then_inc(s["ln4_stats"], 1)

            def ln4_moments(g):
                dve.wait_ge(s["ln4_stats"], g + 1)
                dve.sem_inc(s["passed"], 1)
                for t in range(G4):
                    last = v.bn_aggr(mom4[:, t, :], stat4[:, t, :])
                last.then_inc(s["ln4_moments"], 1)

            def ln4_apply(g, par):
                dve.wait_ge(s["ln4_rstd"], g + 1)
                dve.wait_ge(s["ln4_moments"], g + 1)
                if some(g - 1):
                    dve.wait_ge(s["z4T_ps"], g - 1)
                    dve.wait_ge(s[f"scattered{par}"], 16 * G4 * K2 // 2 * (g - par))
                for t in range(G4):
                    last = v.tensor_scalar(z4[par][:, t, :], xrow(g, t), mom4[:, t, 0:1], rs4[:, t:t + 1], ALU.subtract, ALU.mult)
                last.then_inc(s["z4_ready"], 1)

            def add_value_bias(g):
                dve.wait_ge(s["v_ps"], g + 1)
                if some(g):
                    dve.wait_ge(s["vr_ready"], g)
                    dve.wait_ge(s["v1_ready"], g)
                v.tensor_tensor(vb[:], misc[0:S2, :].rearrange("p (t c) -> p t c", t=G4),
                                over(bv_row[0:S2, :], 1, G4), ALU.add).then_inc(s["vb_ready"], 1)

            def top_of(n, q):
                dve.wait_ge(s["S_ps"], n + 1)
                v.reduce_max(top_score[:, HB * q:HB * q + HB], S[:, q], AX.X).then_inc(s["M_ready"], 1)

            def shift(n, q):
                dve.wait_ge(s["M_ready"], n + 1)
                if some(n - NQ + 1):
                    dve.wait_ge(s["P_ready"], n - NQ + 1)
                v.tensor_tensor(Sd[:, HB * q:HB * q + HB, :], S[:, q], over(top_score[:, HB * q:HB * q + HB], 2, S2),
                                ALU.subtract).then_inc(s["Sd_ready"], 1)

            def normalise(b, j, turned):
                dve.wait_ge(s["pv_done"], NQ * b + NQ)
                v.tensor_reduce(osum[:], O[:, :, 0:3 * HD].rearrange("p h (i c) -> p h c i", i=3), AX.X, ALU.add).then_inc(s["osum_ready"], 1)
                v.reciprocal(rsum[:], O[:, :, 3 * HD:VC].rearrange("p h c -> p (h c)")).then_inc(s["rsum_ready"], 1)
                dve.wait_ge(s["osum_ready"], b + 1)
                dve.wait_ge(s["rsum_ready"], b + 1)
                if j == 0 and some(turned):
                    dve.wait_ge(s["oT_ps"], turned)
                v.tensor_tensor(o[:, j, :].rearrange("p (h c) -> p h c", h=H), osum[:], over(rsum[:], 2, HD), ALU.mult).then_inc(s["o_ready"], 1)

            def add_out(g):
                dve.wait_ge(s["out_ps"], g + 1)
                dve.wait_ge(s["xb_ready"], g + 1)
                v.tensor_tensor(X[:, bass.ts(g, G4), :], misc.rearrange("p (t c) -> p t c", t=G4), xb[:], ALU.add).then_inc(s["x_out"], 1)

            STEPS = 24
            done = [0]

            def step(g, ins):
                done[0] = done[0] % STEPS + 1
                ins.then_inc(s["step"], 1)
                dve.wait_ge(s["step"], STEPS * g + done[0])

            def logits_down(g):
                dve.wait_ge(s["gate_ps"], g + 1)
                v.tensor_reduce(top[:], gate_ps, AX.X, ALU.max).then_inc(s["dl_ready"], 1)
                dve.wait_ge(s["dl_ready"], 2 * g + 1)
                v.tensor_tensor(dl[:], gate_ps, over(top[:], 2, E), ALU.subtract).then_inc(s["dl_ready"], 1)

            def probabilities(g):
                dve.wait_ge(s["ex_ready"], g + 1)
                step(g, v.tensor_reduce(total[:], ex[:], AX.X, ALU.add))
                step(g, v.reciprocal(rtotal[:], total[:]))
                step(g, v.tensor_tensor(pr[:], ex[:], over(rtotal[:], 2, E), ALU.mult))

            def find_top(g, k, p):
                step(g, v.tensor_reduce(best[:, k, :], p[:], AX.X, ALU.max))
                step(g, v.tensor_tensor(is_top[:], p[:], over(best[:, k, :], 2, E), ALU.is_equal))

            def first_place(g, k):
                step(g, v.tensor_tensor(is_top[:], is_top[:], over(expert_no[:], 1, G4), ALU.mult))
                step(g, v.tensor_reduce(chosen[:, k, :], is_top[:], AX.X, ALU.min))
                step(g, v.tensor_tensor(hot[:, :, k, :], over(chosen[:, k, :], 2, E), over(expert_no[:], 1, G4), ALU.is_equal))

            def without_first(g):
                step(g, v.scalar_tensor_tensor(pr2[:], hot[:, :, 0, :], -2.0, pr[:], ALU.mult, ALU.add))

            hotf = hot[:].rearrange("p t k e -> p t (k e)")

            def count_tiles(g, tiles):
                if tiles[0] == 0:
                    if some(g):
                        dve.wait_ge(s["rank_ps"], g)
                    v.tensor_copy(hotb[:], hotf)
                    step(g, v.tensor_copy(count[:, 0, :], count[:, G4, :]))
                for t in tiles:
                    step(g, v.tensor_tensor(count[:, t + 1, :], count[:, t, :], hotf[:, t, :], ALU.add))
                if tiles[-1] == G4 - 1:
                    v.tensor_copy(before[:], count[:, 0:G4, :]).then_inc(s["hot_ready"], 1)

            def pair_weights(g):
                step(g, v.scalar_tensor_tensor(pair[:], best[:, 0, :], 1e-9, best[:, 1, :], ALU.add, ALU.add))
                step(g, v.reciprocal(rpair[:], pair[:]))

            def ranks_down(g):
                dve.wait_ge(s["rank_ps"], g + 1)
                v.tensor_tensor(ranked[:].rearrange("p t k e -> p t (k e)"), rank_ps.rearrange("p (t c) -> p t c", t=G4), hotf, ALU.mult).then_inc(s["ranked_ready"], 1)
                v.tensor_tensor(weight[:], best[:].rearrange("p k t -> p t k"), over(rpair[:], 2, K2), ALU.mult)
                dve.wait_ge(s["ranked_ready"], g + 1)
                step(g, v.tensor_reduce(rank[:], ranked[:], AX.X, ALU.add))

            def rows_down(g, par):
                v.tensor_scalar(drop[:], rank[:], float(CAP), OUT_OF_RANGE, ALU.is_ge, ALU.mult)
                v.scalar_tensor_tensor(row[:], chosen[:].rearrange("p k t -> p t k"), float(K2 * CAP), rank[:], ALU.mult, ALU.add)
                step(g, v.scalar_tensor_tensor(W[:, bass.ts(g, G4), :], rank[:], float(CAP), weight[:], ALU.is_lt, ALU.mult))
                step(g, v.tensor_tensor(row[:], row[:], over(slot_base[:], 1, G4), ALU.add))
                assert done[0] == STEPS, done
                if some(g - 1):
                    dve.wait_ge(s[f"scattered{par}"], 16 * G4 * K2 // 2 * (g - par))
                v.tensor_tensor(idx[par][:], row[:], drop[:], ALU.add)
                v.tensor_tensor(IDX[:, bass.ts(g, G4), :], row[:], drop[:], ALU.add).then_inc(s["idx_ready"], 1)

            def steps(g, par):
                other = 1 - par
                for m in range(M_):
                    n, q, j = M_ * g + m, m % NQ, m // NQ
                    if quarter(n + 2):
                        top_of(n + 2, (q + 2) % NQ)
                    if quarter(n + 2):
                        shift(n + 2, (q + 2) % NQ)
                    if q == 2 and quarter(n - NQ):
                        normalise(G4 * g + j - 1, (j - 1) % G4, g)
                    if group(g + 1):
                        if m == 0:
                            ln3_stats(g + 1)
                        if m == 1:
                            ln3_moments(g + 1)
                        if m == 3:
                            ln3_apply(g + 1)
                        if m == 12:
                            add_value_bias(g + 1)
                    if group(g - 1):
                        if m == 5:
                            add_out(g - 1)
                        if m == 7:
                            ln4_stats(g - 1)
                        if m == 8:
                            ln4_moments(g - 1)
                        if m == 9:
                            ln4_apply(g - 1, other)
                        if m == 15:
                            logits_down(g - 1)
                    if group(g - 2):
                        if m == 1:
                            probabilities(g - 2)
                            find_top(g - 2, 0, pr)
                        if m == 2:
                            first_place(g - 2, 0)
                        if m == 3:
                            without_first(g - 2)
                            find_top(g - 2, 1, pr2)
                        if m == 4:
                            first_place(g - 2, 1)
                            count_tiles(g - 2, (0,))
                        if m == 5:
                            count_tiles(g - 2, (1, 2, 3))
                        if m == 6:
                            pair_weights(g - 2)
                        if m == 7:
                            ranks_down(g - 2)
                        if m == 8:
                            rows_down(g - 2, par)

            dve.wait_ge(s["const_loaded"], n_const)
            dve.wait_ge(s["count_ready"], 1)
            v.tensor_scalar(bcols[:, 2:3], bcols[:, 0:1], float(HD) ** -0.5, None, ALU.mult).then_inc(s["q_bias_ready"], 1)
            ln3_stats(0)
            ln3_moments(0)
            ln3_apply(0)
            add_value_bias(0)
            for q in (0, 1):
                top_of(q, q)
                shift(q, q)
            groups(dve, steps)
            dve.wait_ge(s["idx_ready"], NG)

        @block.scalar
        def _(act):
            def z3T_side(g):
                act.wait_ge(s["z3T_ps"], g + 1)
                if some(g):
                    act.wait_ge(s["q_ps"], g)
                nc.scalar.activation(z3T[:], misc, ACT.Copy).then_inc(s["z3T_ready"], 1)

            def kT_side(g, par):
                act.wait_ge(s["k_ps"], g + 1)
                if some(g - 1):
                    act.wait_ge(s["Kb_ready"], G4 * g - G4)
                nc.scalar.activation(kT[par][:].rearrange("p t n -> p (t n)"), misc[:, 0:G4 * S2], ACT.Identity,
                                     bias=bcols[:, 1:2]).then_inc(s["kT_ready"], 1)

            def qT_side(g, par):
                act.wait_ge(s["q_ps"], g + 1)
                if some(g - 1):
                    act.wait_ge(s["S_ps"], M_ * (g - 1))
                nc.scalar.activation(qT[par][:], misc, ACT.Identity, bias=bcols[:, 2:3], scale=float(HD) ** -0.5).then_inc(s["qT_ready"], 1)

            def first_part(g, par):
                act.wait_ge(s["vb_ready"], g + 1)
                if some(g - 1):
                    act.wait_ge(s["pv_done"], M_ * (g - 1))
                nc.scalar.activation(V[par][:, :, :, 0:HD].rearrange("p t h c -> p (t h) c"),
                                     vb[:].rearrange("p t (h c) -> p (t h) c", h=H), ACT.Copy).then_inc(s["v1_ready"], 1)

            def second_part(g, par):
                act.wait_ge(s["vr_ready"], g + 1)
                nc.scalar.activation(V[par][:, :, :, HD:2 * HD].rearrange("p t h c -> p (t h) c"),
                                     vr[:].rearrange("p t (h c) -> p (t h) c", h=H), ACT.Copy).then_inc(s["v2_ready"], 1)

            def exps(n, q):
                act.wait_ge(s["Sd_ready"], n + 1)
                if some(n - NQ + 1):
                    act.wait_ge(s["PT_ps"], n - NQ + 1)
                nc.scalar.activation(Pr[:, HB * q:HB * q + HB, :], Sd[:, HB * q:HB * q + HB, :], ACT.Exp).then_inc(s["P_ready"], 1)

            def high_part(n, q):
                act.wait_ge(s["PT_ps"], n + 1)
                if some(n - NQ + 1):
                    act.wait_ge(s["pv_done"], n - NQ + 1)
                nc.scalar.activation(hi[:, bass.ts(q, 512)], PT[q % 2][0:S2, :], ACT.Copy).then_inc(s["hi_ready"], 1)

            def low_part(n, q):
                act.wait_ge(s["rest_ps"], n + 1)
                if some(n - NQ + 1):
                    act.wait_ge(s["pv_done"], n - NQ + 1)
                nc.scalar.activation(lo[:, bass.ts(q, 512)], PT[q % 2][0:S2, :], ACT.Copy).then_inc(s["lo_ready"], 1)

            def oT_side(g):
                act.wait_ge(s["oT_ps"], g + 1)
                if some(g):
                    act.wait_ge(s["out_ps"], g)
                nc.scalar.activation(oT[:], misc, ACT.Copy).then_inc(s["oT_ready"], 1)

            def z4T_side(g):
                act.wait_ge(s["z4T_ps"], g + 1)
                if some(g):
                    act.wait_ge(s["gate_ps"], g)
                nc.scalar.activation(z4T[:], misc, ACT.Copy).then_inc(s["z4T_ready"], 1)

            def gate_exps(g):
                act.wait_ge(s["dl_ready"], 2 * g + 2)
                if some(g):
                    act.wait_ge(s["hot_ready"], g)
                nc.scalar.activation(ex[:], dl[:], ACT.Exp).then_inc(s["ex_ready"], 1)

            def steps(g, par):
                other = 1 - par
                for m in range(M_):
                    n, q = M_ * g + m, m % NQ
                    if quarter(n + 1):
                        exps(n + 1, (q + 1) % NQ)
                    if quarter(n - 1):
                        low_part(n - 1, (q - 1) % NQ)
                    if quarter(n):
                        high_part(n, q)
                    if group(g + 1):
                        if m == 8:
                            z3T_side(g + 1)
                        if m == 9:
                            kT_side(g + 1, other)
                        if m == 10:
                            qT_side(g + 1, other)
                        if m == 12:
                            first_part(g + 1, other)
                        if m == 15:
                            second_part(g + 1, other)
                    if group(g - 1):
                        if m == 3:
                            oT_side(g - 1)
                        if m == 13:
                            z4T_side(g - 1)
                    if group(g - 2) and m == 0:
                        gate_exps(g - 2)

            act.wait_ge(s["q_bias_ready"], 1)
            act.wait_ge(s["const_loaded"], n_const)
            z3T_side(0)
            kT_side(0, 0)
            qT_side(0, 0)
            first_part(0, 0)
            second_part(0, 0)
            exps(0, 0)
            groups(act, steps)

        @block.tensor
        def _(pe):
            def t3(g):
                pe.wait_ge(s["z3_ready"], g + 1)
                if some(g - 1):
                    pe.wait_ge(s["x_out"], g - 1)
                if some(g - 2):
                    pe.wait_ge(s["ranked_ready"], g - 2)
                for t in range(G4):
                    last = nc.tensor.transpose(misc[:, t * P:(t + 1) * P], z3[:, t, :], ident[:])
                last.then_inc(s["z3T_ps"], 1)

            def keys(g, par):
                pe.wait_ge(s["z3T_ready"], g + 1)
                pe.wait_ge(s["ctx_loaded"], 16 * g + 16)
                nc.tensor.matmul(misc[:, 0:G4 * S2], wk[:], cT[par][:], start=True, stop=True).then_inc(s["k_ps"], 1)

            def queries(g):
                pe.wait_ge(s["kT_ready"], g + 1)
                nc.tensor.matmul(misc, wq[:], z3T[:], start=True, stop=True).then_inc(s["q_ps"], 1)

            def values(g, par):
                pe.wait_ge(s["qT_ready"], g + 1)
                for t in range(G4):
                    last = nc.tensor.matmul(misc[0:S2, t * P:(t + 1) * P], cT[par][:, t * S2:(t + 1) * S2], wv[:], start=True, stop=True)
                last.then_inc(s["v_ps"], 1)

            def scores(g, par, m):
                n, q, j = M_ * g + m, m % NQ, m // NQ
                if m == 0:
                    pe.wait_ge(s["qT_ready"], g + 1)
                if q == 0:
                    pe.wait_ge(s["Kb_ready"], G4 * g + j + 1)
                if some(n - NQ + 1):
                    pe.wait_ge(s["Sd_ready"], n - NQ + 1)
                nc.tensor.matmul(S[:, q], qT[par][:, j * P:(j + 1) * P], Kb[j % 2][:, HB * q:HB * q + HB, :], start=True, stop=False)
                nc.tensor.matmul(S[:, q], first_row[:], over(masked[:, bass.ds((G4 * g + j) * S2, S2)], 1, HB),
                                 start=False, stop=True).then_inc(s["S_ps"], 1)

            def turn(n, q):
                pe.wait_ge(s["P_ready"], n + 1)
                if some(n - 1):
                    pe.wait_ge(s["lo_ready"], n - 1)
                for h in range(HB):
                    last = nc.tensor.matmul(PT[q % 2][0:S2, h * P:(h + 1) * P], Pr[:, HB * q + h, :], ident[:], start=(h == 0),
                                            stop=False, is_transpose=True, skip_group_check=True)
                last.then_inc(s["PT_ps"], 1)

            def take_high(n, q):
                pe.wait_ge(s["hi_ready"], n + 1)
                nc.tensor.matmul(PT[q % 2][0:S2, :], minus_one[0:S2, 0:S2], hi[:, bass.ts(q, 512)], start=False, stop=True,
                                 skip_group_check=True).then_inc(s["rest_ps"], 1)

            def weigh(g, par, m):
                n, q, j = M_ * g + m, m % NQ, m // NQ
                if m == 0:
                    pe.wait_ge(s["v3_ready"], g + 1)
                pe.wait_ge(s["hi_ready"], n + 1)
                pe.wait_ge(s["lo_ready"], n + 1)
                if q == 0 and some(G4 * g + j):
                    pe.wait_ge(s["o_ready"], G4 * g + j)
                for h in range(HB * q, HB * q + HB):
                    nc.tensor.matmul(O[:, h, :], hi[:, h * P:(h + 1) * P], V[par][:, j, h, :], start=True, stop=False)
                    last = nc.tensor.matmul(O[:, h, :], lo[:, h * P:(h + 1) * P], V[par][:, j, h, :], start=False, stop=True)
                last.then_inc(s["pv_done"], 1)

            def turn_out(g):
                pe.wait_ge(s["o_ready"], G4 * g + G4)
                if isinstance(g, int) and g == 0:
                    pe.wait_ge(s["vb_ready"], 2)
                else:
                    pe.wait_ge(s["dl_ready"], 2 * g)
                for t in range(G4):
                    last = nc.tensor.transpose(misc[:, t * P:(t + 1) * P], o[:, t, :], ident[:])
                last.then_inc(s["oT_ps"], 1)

            def project_out(g):
                pe.wait_ge(s["oT_ready"], g + 1)
                for t in range(G4):
                    last = nc.tensor.matmul(misc[:, t * P:(t + 1) * P], oT[:, t * P:(t + 1) * P], wo[:], start=True, stop=True)
                last.then_inc(s["out_ps"], 1)

            def t4(g, par):
                pe.wait_ge(s["z4_ready"], g + 1)
                if isinstance(g, int) and g >= NG - 2:
                    pe.wait_ge(s["ranked_ready"], g)
                else:
                    pe.wait_ge(s["vb_ready"], g + 3)
                for t in range(G4):
                    last = nc.tensor.transpose(misc[:, t * P:(t + 1) * P], z4[par][:, t, :], ident[:])
                last.then_inc(s["z4T_ps"], 1)

            def gate(g):
                pe.wait_ge(s["z4T_ready"], g + 1)
                for t in range(G4):
                    last = nc.tensor.matmul(gate_ps[:, t, :], z4T[:, t * P:(t + 1) * P], gate_w[:], start=True, stop=True)
                last.then_inc(s["gate_ps"], 1)

            def ranks(g):
                pe.wait_ge(s["hot_ready"], g + 1)
                pe.wait_ge(s["x_out"], min(g + 2, NG) if isinstance(g, int) else g + 2)
                nc.tensor.matmul(rank_ps, earlier[:], hotb[:].rearrange("p t c -> p (t c)"), start=True, stop=False)
                nc.tensor.matmul(rank_ps, ones[:], before[:].rearrange("p t c -> p (t c)"), start=False, stop=True).then_inc(s["rank_ps"], 1)

            def steps(g, par):
                other = 1 - par
                for m in range(M_):
                    n, q = M_ * g + m, m % NQ
                    if quarter(n + 3):
                        if m + 3 < M_:
                            scores(g, par, m + 3)
                        else:
                            scores(g + 1, other, m + 3 - M_)
                    if quarter(n - 1):
                        take_high(n - 1, (q - 1) % NQ)
                    if quarter(n):
                        turn(n, q)
                    if quarter(n - 2):
                        if m >= 2:
                            weigh(g, par, m - 2)
                        else:
                            weigh(g - 1, other, m - 2 + M_)
                    if group(g + 1):
                        if m == 8:
                            t3(g + 1)
                        if m == 9:
                            keys(g + 1, other)
                        if m == 10:
                            queries(g + 1)
                        if m == 11:
                            values(g + 1, other)
                    if group(g - 1):
                        if m == 3:
                            turn_out(g - 1)
                        if m == 4:
                            project_out(g - 1)
                        if m == 13:
                            t4(g - 1, other)
                        if m == 14:
                            gate(g - 1)
                    if group(g - 2) and m == 6:
                        ranks(g - 2)

            pe.wait_ge(s["const_loaded"], n_const)
            pe.wait_ge(s["mask_ready"], 1)
            t3(0)
            keys(0, 0)
            queries(0)
            values(0, 0)
            pe.wait_ge(s["vb_ready"], 1)
            for m in range(3):
                scores(0, 0, m)
            groups(pe, steps)


def experts(nc, d, ident, psum, banks, xg, yg):
    with ExitStack() as ctx:
        def sb(name, shape, dt=F32):
            return ctx.enter_context(nc.sbuf_tensor(name, shape, dt))

        def sem(name):
            return ctx.enter_context(nc.semaphore(name))

        HC = HID // P
        NE = E * EG
        gate = [sb(f"gate{i}", [P, HID]) for i in range(2)]
        up = [sb(f"up{i}", [P, HID]) for i in range(2)]
        down = [sb(f"down{i}", [P, HC, P]) for i in range(2)]
        xin = sb("xin", [P, G4, P])
        xT = sb("xT", [P, GROUP_ROWS])
        act_g = sb("act_g", [P, HC, GROUP_ROWS])
        h = sb("h", [P, HC, GROUP_ROWS])
        yo = sb("yo", [P, G4, P])
        names = "w0_loaded w1_loaded x_loaded xT_ps xT_ready gate_ps up_ps g_ready h_ready y_ps y_ready y_stored".split()
        s = {n: sem("e_" + n) for n in names}
        gate_ps, up_ps = banks[0:2], banks[2:4]
        tp, y_ps = banks[4], banks[5].rearrange("p (t c) -> p t c", t=G4)
        block = ctx.enter_context(nc.Block())

        free = {"y_ps": 1, "h_ready": 1, "g_ready": 1, "y_ready": 1, "y_stored": 16}

        def grant(eng, *steps):
            for name in steps:
                eng.sem_inc(s[name], free[name])

        def groups(eng, body):
            with eng.Fori(0, E - 1, 2) as e:
                for par in (0, 1):
                    with eng.Fori(0, EG) as i:
                        body((e + par) * EG + i, par, e)

        @block.sync
        def _(sp):
            def load(n):
                sp.dma_start(xin[:], xg[bass.ts(n, GROUP_ROWS), :].rearrange("(p t) c -> p t c", p=P)).then_inc(s["x_loaded"], 16)

            grant(sp, "y_stored")
            load(0)
            with sp.Fori(0, NE) as n:
                sp.wait_ge(s["xT_ps"], n + 1)
                load(n + 1)
                sp.wait_ge(s["y_ready"], n + 2)
                sp.dma_start(yg[bass.ts(n, GROUP_ROWS), :].rearrange("(p t) c -> p t c", p=P), yo[:]).then_inc(s["y_stored"], 16)
            sp.wait_ge(s["y_stored"], 16 * NE + 16)
            sp.wait_ge(s["x_loaded"], 16 * NE + 16)

        @block.gpsimd
        def _(pool):
            def load(e, par):
                for t, n in ((gate[par], "gate_proj"), (up[par], "up_proj"), (down[par], "down_proj")):
                    src = d[n][:, bass.ds(e, 1)]
                    src = src.rearrange("p a c -> p (a c)") if len(src.shape) == 3 else src.rearrange("p a b c -> p (a b) c")
                    pool.dma_start(t[:], src).then_inc(s[f"w{par}_loaded"], 16)

            load(0, 0)
            load(1, 1)
            with pool.Fori(2, E - 1, 2) as e:
                for par in (0, 1):
                    pool.wait_ge(s["y_ps"], EG * (e + par - 1) + 1)
                    load(e + par, par)

        @block.vector
        def _(dve):
            def body(n, par, e):
                for c in range(HC):
                    dve.wait_ge(s["g_ready"], HC * n + c + 2)
                    dve.wait_ge(s["up_ps"], HC * n + c + 1)
                    dve.wait_ge(s["y_ps"], n + 1)
                    nc.vector.tensor_tensor(h[:, c, :], up_ps[c], act_g[:, c, :], ALU.mult).then_inc(s["h_ready"], 1)

            grant(dve, "h_ready")
            groups(dve, body)

        @block.scalar
        def _(act):
            def x_side(n):
                act.wait_ge(s["xT_ps"], n + 1)
                if some(HC * n):
                    act.wait_ge(s["up_ps"], HC * n)
                nc.scalar.activation(xT[:], tp, ACT.Copy).then_inc(s["xT_ready"], 1)

            def body(n, par, e):
                for c in range(HC):
                    act.wait_ge(s["gate_ps"], HC * n + c + 1)
                    act.wait_ge(s["h_ready"], HC * n + 1)
                    nc.scalar.activation(act_g[:, c, :], gate_ps[c], ACT.Silu).then_inc(s["g_ready"], 1)
                x_side(n + 1)
                act.wait_ge(s["y_ps"], n + 2)
                act.wait_ge(s["y_stored"], 16 * n + 16)
                nc.scalar.activation(yo[:], y_ps, ACT.Copy).then_inc(s["y_ready"], 1)

            grant(act, "g_ready", "y_ready")
            x_side(0)
            groups(act, body)

        @block.tensor
        def _(pe):
            def turn(n):
                pe.wait_ge(s["x_loaded"], 16 * n + 16)
                if some(n):
                    pe.wait_ge(s["xT_ready"], n)
                for t in range(G4):
                    last = nc.tensor.transpose(tp[:, t * P:(t + 1) * P], xin[:, t, :], ident[:])
                last.then_inc(s["xT_ps"], 1)

            def body(n, par, e):
                pe.wait_ge(s[f"w{par}_loaded"], 16 * 3 * (e // 2) + 48)
                pe.wait_ge(s["xT_ready"], n + 1)
                for c in range(HC):
                    pe.wait_ge(s["g_ready"], HC * n + 1)
                    nc.tensor.matmul(gate_ps[c], gate[par][:, c * P:(c + 1) * P], xT[:], start=True, stop=True).then_inc(s["gate_ps"], 1)
                for c in range(HC):
                    pe.wait_ge(s["h_ready"], HC * n + 1)
                    nc.tensor.matmul(up_ps[c], up[par][:, c * P:(c + 1) * P], xT[:], start=True, stop=True).then_inc(s["up_ps"], 1)
                turn(n + 1)
                pe.wait_ge(s["y_ready"], n + 1)
                for c in range(HC):
                    pe.wait_ge(s["h_ready"], HC * n + c + 2)
                    for t in range(G4):
                        last = nc.tensor.matmul(y_ps[:, t, :], h[:, c, t * P:(t + 1) * P], down[par][:, c, :],
                                                start=(c == 0 and t == 0), stop=(c == HC - 1), skip_group_check=True)
                last.then_inc(s["y_ps"], 1)

            grant(pe, "y_ps")
            turn(0)
            groups(pe, body)


def combine(nc, X, W, IDX, yg, out):
    with ExitStack() as ctx:
        def sb(name, shape, dt=F32):
            return ctx.enter_context(nc.sbuf_tensor(name, shape, dt))

        def sem(name):
            return ctx.enter_context(nc.semaphore(name))

        idx = [sb(f"gidx{i}", [P, G4, K2], I32) for i in range(2)]
        wt = [sb(f"gwt{i}", [P, G4, K2]) for i in range(2)]
        yb = [sb(f"yb{i}", [P, G4, K2, P]) for i in range(2)]
        part = [sb(f"part{i}", [P, G4, P]) for i in range(2)]
        ost = [sb(f"ost{i}", [P, G4, P]) for i in range(2)]
        names = "passed cleared idx_ready gathered0 gathered1 part_ready o_ready stored0 stored1".split()
        s = {n: sem("g_" + n) for n in names}
        block = ctx.enter_context(nc.Block())

        @block.sync
        def _(sp):
            with sp.Fori(0, NG - 1, 2) as g:
                for par in (0, 1):
                    sp.wait_ge(s["o_ready"], g + par + 1)
                    sp.dma_start(out[:, bass.ts(g + par, G4), :], ost[par][:]).then_inc(s[f"stored{par}"], 16)
            for par in (0, 1):
                sp.wait_ge(s[f"stored{par}"], 16 * NG // 2)

        @block.gpsimd
        def _(pool):
            pool.wait_ge(s["cleared"], 1)
            with pool.Fori(0, NG - 1, 2) as g:
                for par in (0, 1):
                    pool.wait_ge(s["idx_ready"], g + par + 1)
                    pool.sem_inc(s["passed"], 1)
                    for t in range(G4):
                        for k in range(K2):
                            pool.indirect_dma_start(yb[par][:, t, k, :], None, yg, bass.IndirectOffsetOnAxis(ap=idx[par][:, t, k:k + 1], axis=0),
                                                    bounds_check=ROWS - 1, oob_is_err=False).then_inc(s[f"gathered{par}"], 16)

        @block.vector
        def _(dve):
            for i in range(2):
                last = nc.vector.memset(yb[i][:], 0.0)
            last.then_inc(s["cleared"], 1)
            dve.wait_ge(s["cleared"], 1)

            def fetch(g, par):
                nc.vector.tensor_copy(wt[par][:], W[:, bass.ts(g, G4), :])
                nc.vector.tensor_copy(idx[par][:], IDX[:, bass.ts(g, G4), :]).then_inc(s["idx_ready"], 1)

            def add(g, par, half):
                dve.wait_ge(s[f"gathered{par}"], 16 * G4 * K2 * (half + 1))
                dve.wait_ge(s["idx_ready"], g + 1)
                for t in range(G4):
                    last = nc.vector.scalar_tensor_tensor(part[par][:, t, :], yb[par][:, t, 0, :], wt[par][:, t, 0:1],
                                                          X[:, bass.ds(G4 * g + t, 1), :].rearrange("p a c -> p (a c)"), ALU.mult, ALU.add)
                last.then_inc(s["part_ready"], 1)
                dve.wait_ge(s["part_ready"], g + 1)
                if some(16 * half):
                    dve.wait_ge(s[f"stored{par}"], 16 * half)
                for t in range(G4):
                    last = nc.vector.scalar_tensor_tensor(ost[par][:, t, :], yb[par][:, t, 1, :], wt[par][:, t, 1:2],
                                                          part[par][:, t, :], ALU.mult, ALU.add)
                last.then_inc(s["o_ready"], 1)
                dve.wait_ge(s["o_ready"], g + 1)

            fetch(0, 0)
            fetch(1, 1)
            for par in (0, 1):
                add(par, par, 0)
                fetch(par + 2, par)
            with dve.Fori(2, NG - 3, 2) as g:
                for par in (0, 1):
                    add(g + par, par, g // 2)
                    fetch(g + par + 2, par)
            for par in (0, 1):
                add(NG - 2 + par, par, NG // 2 - 1)


def lay_out(i):
    c = np.ascontiguousarray

    def col(a):
        return c(np.asarray(a).reshape(-1, P).T)

    def rows(a):
        return c(np.broadcast_to(np.asarray(a).reshape(1, -1), (P, np.asarray(a).size)))

    qkv_b = np.asarray(i["L0_attn_qkv_b"])
    head = np.arange(P) // HD
    first_row = (np.arange(P)[:, None] + np.zeros((1, P)) == 0).astype(mybir.dt.np(BF16))
    return {
        "x": c(np.asarray(i["x"]).transpose(1, 0, 2)),
        "qkv_w": c(i["L0_attn_qkv_w"]), "out_w": c(i["L0_attn_out_w"]), "w1": c(i["L0_attn_w1"]),
        "w2": c(np.asarray(i["L0_attn_w2"]).reshape(FC, P, P).transpose(1, 0, 2)),
        "q_bias": col(qkv_b[0:P]), "kb_row": rows(qkv_b[P:2 * P]), "vb_row": rows(qkv_b[2 * P:]),
        "ob_row": rows(i["L0_attn_out_b"]), "b2_row": rows(i["L0_attn_b2"]), "b1": col(i["L0_attn_b1"]),
        "g1": col(i["L0_attn_g1"]), "be1": col(i["L0_attn_be1"]), "g2": col(i["L0_attn_g2"]), "be2": col(i["L0_attn_be2"]),
        "wq": c(np.asarray(i["L0_xattn_Wq"]).T), "wk": c(np.asarray(i["L0_xattn_Wk"]).T),
        "wv": c(np.asarray(i["L0_xattn_Wv"]).T), "wo": c(np.asarray(i["L0_xattn_Wo"]).T),
        "bq": col(i["L0_xattn_bq"]), "bk": col(i["L0_xattn_bk"]),
        "bv_row": rows(i["L0_xattn_bv"]), "bo_row": rows(i["L0_xattn_bo"]),
        "ctxT": c(np.asarray(i["ctx_1024"]).transpose(2, 0, 1).reshape(P, B * S2)),
        "mask": c(np.asarray(i["mask_BxS2_bf0"]).reshape(1, B * S2)),
        "first_row": first_row,
        "gate_w": c(np.asarray(i["L0_ffn_gate_w"]).T),
        "gate_proj": c(np.asarray(i["L0_ffn_gate_proj_w"]).transpose(2, 0, 1)),
        "up_proj": c(np.asarray(i["L0_ffn_up_proj_w"]).transpose(2, 0, 1)),
        "down_proj": c(np.asarray(i["L0_ffn_down_proj_w"]).reshape(E, P, HID // P, P).transpose(3, 0, 2, 1)),
        "expert_no": rows(np.arange(E, dtype=np.float32) - E),
        "slot_base": rows(np.arange(K2, dtype=np.float32) * CAP + E * K2 * CAP),
        "earlier": np.triu(np.ones((P, P)), 1).astype(mybir.dt.np(BF16)),
        "ones": np.ones((P, P)).astype(mybir.dt.np(BF16)),
        "minus_one": (-np.eye(P)).astype(np.float16),
        "ident": np.eye(P, dtype=np.float32),
        "block_mask": (head[:, None] == head[None, :]).astype(np.float32),
        "head_mask": (head[:, None] == np.arange(H)[None, :]).astype(np.float32),
    }


def kernel(**inputs):
    import concourse.bacc as _bacc
    from concourse import mybir as _mybir
    from concourse.bass_utils import run_bass_kernel_spmd as _run

    nc = _bacc.Bacc("TRN2", target_bir_lowering=False, num_devices=1)
    arrays, d = {}, {}
    for name, a in lay_out(inputs).items():
        arrays[f"in_{name}"] = a
        d[name] = nc.dram_tensor(f"in_{name}", a.shape, _mybir.dt.from_np(a.dtype), kind="ExternalInput").ap()
    out = nc.dram_tensor("out", (P, B, P), F32, kind="ExternalOutput").ap()
    build(nc, d, out)
    r = _run(nc, [arrays], core_ids=[0])
    return np.ascontiguousarray(r.results[0]["out"].transpose(1, 0, 2))
```

```python
from contextlib import ExitStack

import numpy as np

import concourse.bass as bass
from concourse import mybir

F32 = mybir.dt.float32
BF16 = mybir.dt.bfloat16
F16 = mybir.dt.float16
I32 = mybir.dt.int32
U8 = mybir.dt.uint8
ALU = mybir.AluOpType
ACT = mybir.ActivationFunctionType
AX = mybir.AxisListType

P = 128
B = 64
G4 = 4
NG = B // G4
H = 16
HD = P // H
S2 = 77
HB = 4
NQ = H // HB
FF = 512
FC = FF // P
E = 8
HID = 256
K2 = 2
CAP = int(1.25 * B * P / E)
ROWS = E * K2 * CAP
GROUP_ROWS = G4 * P
PAIR = 2 * CAP // GROUP_ROWS
VC = 3 * HD + 1
EPS = 1e-5
ATTN_EPS = 1e-6
ROW = P + 1
OUT_OF_RANGE = 1.0e6
NO_TOKEN = float(2 ** 20)




def some(count):
    return not isinstance(count, int) or count > 0


def over(ap, axis, n):
    a = ap.unsqueeze(axis)
    shape = list(a.shape)
    shape[axis] = n
    return a.broadcast_to(shape)


def build(nc, d, out):
    ctx = ExitStack()
    with ctx:
        def sb(name, shape, dt=F32):
            return ctx.enter_context(nc.sbuf_tensor(name, shape, dt))

        def sem(name):
            return ctx.enter_context(nc.semaphore(name))

        X = sb("X", [P, B, P])
        ident = sb("ident", [P, P])
        block_mask = sb("block_mask", [P, P])
        head_mask = sb("head_mask", [P, H])
        neghalf = sb("neghalf", [P, 8])
        psum = ctx.enter_context(nc.psum_tensor("psum", [P, 8, 512], F32))
        banks = [psum[:, i, :] for i in range(8)]

        xg = nc.dram_tensor("dispatched", [ROWS, ROW], F32, kind="Internal").ap()
        yt = [nc.dram_tensor(f"expert_out{i}", [P * B, P], F32, kind="Internal").ap() for i in range(K2)]

        c = {n: sb(n, [P, P]) for n in ("wq", "wk", "wv", "wo", "bv_row", "bo_row")}
        c["bcols"] = sb("bcols", [P, 3])
        c["first_row"] = sb("first_row", [P, P], BF16)
        c["mask"] = sb("mask_u8", [1, B * S2], U8)
        c["masked"] = sb("masked", [P, B * S2], BF16)
        c["codes"] = sb("codes", [P, B])
        c["gate_w"] = sb("gate_w", [P, E])
        c["expert_no"] = sb("expert_no", [P, E])
        c["slot_base"] = sb("slot_base", [P, K2])
        c["earlier"] = sb("earlier", [P, P], BF16)
        c["ones"] = sb("ones", [P, P], BF16)
        c["minus_one"] = sb("minus_one", [P, P], F16)

        W = sb("W", [P, B, K2])

        linear_attention_and_ffn(nc, d, X, ident, block_mask, head_mask, neghalf, psum, banks, xg, yt, c)
        cross_attention_and_routing(nc, d, X, ident, head_mask, neghalf, psum, banks, xg, W, c)
        experts_and_combine(nc, d, X, ident, psum, banks, xg, yt, W, out)


def linear_attention_and_ffn(nc, d, X, ident, block_mask, head_mask, neghalf, psum, banks, xg, yt, later):
    with ExitStack() as ctx:
        def sb(name, shape, dt=F32):
            return ctx.enter_context(nc.sbuf_tensor(name, shape, dt))

        def sem(name):
            return ctx.enter_context(nc.semaphore(name))

        qkv_w = sb("qkv_w", [P, 3 * P])
        out_w = sb("out_w", [P, P])
        w1 = sb("w1", [P, FF])
        w2 = sb("w2", [P, FC, P])
        kb_row, vb_row, ob_row, b2_row = (sb(n, [P, P]) for n in ("kb_row", "vb_row", "ob_row", "b2_row"))
        cols = sb("cols", [P, 6 + FC])
        q_bias, q_bias1, g1, be1, g2, be2 = (cols[:, i:i + 1] for i in range(6))
        zeros = sb("zeros", [P, G4 * ROW])

        mom0, stat0 = sb("mom0", [P, G4, 2]), sb("stat0", [P, G4, 6])
        mom2, stat2 = sb("mom2", [P, G4, 2]), sb("stat2", [P, G4, 6])
        var0, rs0 = sb("var0", [P, 2, G4]), sb("rs0", [P, 2, G4])
        var2, rs2 = sb("var2", [P, G4]), sb("rs2", [P, G4])
        n0, n0b, z1, z2 = (sb(n, [P, G4, P]) for n in ("n0", "n0b", "z1", "z2"))
        ln1T, ln2T, yT = (sb(n, [P, G4 * P]) for n in ("ln1T", "ln2T", "yT"))
        k1, ek, kf = (sb(n, [P, G4, P]) for n in ("k1", "ek", "kf"))
        q1, eq, qf = (sb(n, [P, G4 * P]) for n in ("q1", "eq", "qf"))
        minus_one = sb("minus_one_col", [P, 1])
        v1 = sb("v1", [P, G4, P + 1])
        KV = sb("KV", [P, G4, P + H])
        den, rden = sb("den", [P, G4, H]), sb("rden", [P, G4, H])
        y, x1, x1b, xs = (sb(n, [P, G4, P]) for n in ("y", "x1", "x1b", "xs"))
        hT = sb("hT", [P, FC, G4 * P])

        names = ("passed const_loaded later_loaded masked_ready x_loaded zeros_ready zeros_stored neghalf_ready ones_ready "
                 "ln0_stats ln0_moments ln0_var ln0_rstd z1_ready n0_ready n0b_ready z1T_ps ln1T_ready "
                 "q_ps kv_ps q1_ready eq_ready qf_ready k1_ready v_ready ek_ready kf_ready "
                 "KV_ps KV_ready y_ps den_ready rden_ready y_ready yT_ps yT_ready attn_ps x1_ready x1b_ready xs_ready "
                 "ln2_stats ln2_moments ln2_var ln2_rstd z2_ready z2T_ps ln2T_ready h_ps h_ready w2_ps x_out").split()
        s = {n: sem("a_" + n) for n in names}

        kvp = psum[:, 0:2, :].rearrange("p a (b c) -> p (a b) c", b=2)
        kvs = psum[:, 2:4, :].rearrange("p a (b c) -> p (a b) c", b=2)
        q_ps = banks[2]
        tp = banks[4]
        w2_ps = attn_ps = banks[5].rearrange("p (t c) -> p t c", t=G4)
        h_ps = [banks[6], banks[7]]

        block = ctx.enter_context(nc.Block())

        def turns(eng, turn):
            for g in range(-2, 2):
                turn(g)
            with eng.Fori(2, NG - 2) as g:
                turn(g)
            for g in range(NG - 2, NG + 2):
                turn(g)

        def group(g):
            return not isinstance(g, int) or 0 <= g < NG

        consts = [(qkv_w, "qkv_w"), (out_w, "out_w"), (w1, "w1"), (w2, "w2"), (kb_row, "kb_row"),
                  (vb_row, "vb_row"), (ob_row, "ob_row"), (b2_row, "b2_row"), (ident, "ident"),
                  (block_mask, "block_mask"), (head_mask, "head_mask")]
        COLS = ["q_bias", "g1", "be1", "g2", "be2"]
        n_const = 16 * (len(consts) + len(COLS) + 1)
        LATER = [n for n in later if n not in ("bcols", "masked")]
        n_later = 16 * (len(LATER) + 2)

        @block.sync
        def _(sp):
            sp.dma_start(X[:, 0:G4, :], d["x"][:, 0:G4, :]).then_inc(s["x_loaded"], 16)
            for t, n in consts[1::2]:
                sp.dma_start(t[:], d[n]).then_inc(s["const_loaded"], 16)
            for i, n in zip((0, 2, 3, 4, 5), COLS):
                sp.dma_start(cols[:, i:i + 1], d[n]).then_inc(s["const_loaded"], 16)
            sp.dma_start(cols[:, 6:6 + FC], d["b1"]).then_inc(s["const_loaded"], 16)
            with sp.Fori(1, NG) as g:
                sp.wait_ge(s["x_loaded"], 16 * g)
                sp.dma_start(X[:, bass.ts(g, G4), :], d["x"][:, bass.ts(g, G4), :]).then_inc(s["x_loaded"], 16)
            sp.wait_ge(s["zeros_ready"], 1)
            with sp.Fori(0, ROWS // GROUP_ROWS) as i:
                sp.dma_start(xg[bass.ts(i, GROUP_ROWS), :].rearrange("(p a) c -> p (a c)", p=P),
                             zeros[:]).then_inc(s["zeros_stored"], 16)
            for y in yt:
                with sp.Fori(0, P * B // GROUP_ROWS) as i:
                    sp.dma_start(y[bass.ts(i, GROUP_ROWS), :].rearrange("(p a) c -> p (a c)", p=P),
                                 zeros[:, 0:G4 * P]).then_inc(s["zeros_stored"], 16)
            for n in LATER:
                sp.dma_start(later[n][:], d[n]).then_inc(s["later_loaded"], 16)
            sp.dma_start(later["bcols"][:, 0:1], d["bq"]).then_inc(s["later_loaded"], 16)
            sp.dma_start(later["bcols"][:, 1:2], d["bk"]).then_inc(s["later_loaded"], 16)
            sp.wait_ge(s["zeros_stored"], 16 * (ROWS + K2 * P * B) // GROUP_ROWS)

        @block.gpsimd
        def _(pool):
            pool.memset(minus_one[:], -1.0).then_inc(s["neghalf_ready"], 1)
            pool.memset(neghalf[:], -0.5).then_inc(s["neghalf_ready"], 1)
            pool.memset(zeros[:], 0.0).then_inc(s["zeros_ready"], 1)
            pool.wait_ge(s["neghalf_ready"], 2)
            pool.wait_ge(s["zeros_ready"], 1)

            def ln0_scale(g):
                pool.wait_ge(s["ln0_moments"], g + 1)
                pool.sem_inc(s["passed"], 1)
                pool.tensor_scalar(var0[:, 0, :], mom0[:, :, 1], EPS, None, ALU.add)
                pool.tensor_scalar(var0[:, 1, :], mom0[:, :, 1], 1.0 + EPS, EPS * EPS, ALU.mult, ALU.add).then_inc(s["ln0_var"], 1)
                pool.wait_ge(s["ln0_var"], g + 1)
                pool.tensor_tensor(rs0[:].rearrange("p a b -> p (a b)"), var0[:].rearrange("p a b -> p (a b)"),
                                   neghalf[:, 0:2 * G4], ALU.pow).then_inc(s["ln0_rstd"], 1)

            def add_out_bias(g):
                pool.wait_ge(s["n0_ready"], g + 1)
                if some(g):
                    pool.wait_ge(s["x1_ready"], g)
                pool.tensor_tensor(n0b[:], n0[:], over(ob_row[:], 1, G4), ALU.add).then_inc(s["n0b_ready"], 1)

            def ln2_scale(f):
                pool.wait_ge(s["ln2_moments"], f + 1)
                pool.sem_inc(s["passed"], 1)
                pool.tensor_scalar(var2[:], mom2[:, :, 1], EPS, None, ALU.add).then_inc(s["ln2_var"], 1)
                pool.wait_ge(s["ln2_var"], f + 1)
                pool.tensor_tensor(rs2[:], var2[:], neghalf[:, 0:G4], ALU.pow).then_inc(s["ln2_rstd"], 1)

            def residual(f):
                pool.wait_ge(s["x1_ready"], f + 1)
                pool.tensor_tensor(x1b[:], x1[:], over(b2_row[:], 1, G4), ALU.add).then_inc(s["x1b_ready"], 1)
                pool.wait_ge(s["x1b_ready"], f + 1)
                if some(f):
                    pool.wait_ge(s["x_out"], f)
                pool.tensor_tensor(xs[:], x1b[:], X[:, bass.ts(f, G4), :], ALU.add).then_inc(s["xs_ready"], 1)

            def turn(g):
                if isinstance(g, int) and g == -1:
                    pool.wait_ge(s["const_loaded"], n_const)
                if group(g - 1):
                    residual(g - 1)
                if group(g + 2):
                    ln0_scale(g + 2)
                if group(g + 1):
                    add_out_bias(g + 1)
                if group(g):
                    ln2_scale(g)

            turns(pool, turn)
            masked = later["masked"]
            pool.memset(masked[:], 0.0).then_inc(s["masked_ready"], 1)
            pool.wait_ge(s["masked_ready"], 1)
            pool.wait_ge(s["later_loaded"], n_later)
            pool.tensor_scalar(masked[0:1, :], later["mask"][:], -3e38, 1e38, ALU.mult, ALU.mult).then_inc(s["masked_ready"], 1)
            pool.wait_ge(s["masked_ready"], 2)

        @block.vector
        def _(dve):
            nc.vector.memset(v1[:, :, P:P + 1], 1.0).then_inc(s["ones_ready"], 1)

            def xrow(g, t):
                return X[:, bass.ds(G4 * g + t, 1), :].rearrange("p a c -> p (a c)")

            def ln0_moments(g):
                dve.wait_ge(s["x_loaded"], 16 * g + 16)
                if some(g):
                    dve.wait_ge(s["ln0_moments"], g)
                dve.sem_inc(s["passed"], 1)
                for t in range(G4):
                    last = nc.vector.bn_stats(stat0[:, t, :], xrow(g, t))
                last.then_inc(s["ln0_stats"], 1)
                dve.wait_ge(s["ln0_stats"], g + 1)
                if some(g):
                    dve.wait_ge(s["ln0_rstd"], g)
                    dve.wait_ge(s["n0_ready"], g)
                dve.sem_inc(s["passed"], 1)
                for t in range(G4):
                    last = nc.vector.bn_aggr(mom0[:, t, :], stat0[:, t, :])
                last.then_inc(s["ln0_moments"], 1)

            def ln0_ln1_apply(g):
                dve.wait_ge(s["ln0_rstd"], g + 1)
                dve.wait_ge(s["ln0_moments"], g + 1)
                if some(g):
                    dve.wait_ge(s["z1T_ps"], g)
                for t in range(G4):
                    last = nc.vector.tensor_scalar(z1[:, t, :], xrow(g, t), mom0[:, t, 0:1], rs0[:, 1, t:t + 1], ALU.subtract, ALU.mult)
                last.then_inc(s["z1_ready"], 1)

            def ln0_apply(g):
                if some(g):
                    dve.wait_ge(s["n0b_ready"], g)
                for t in range(G4):
                    last = nc.vector.tensor_scalar(n0[:, t, :], xrow(g, t), mom0[:, t, 0:1], rs0[:, 0, t:t + 1], ALU.subtract, ALU.mult)
                last.then_inc(s["n0_ready"], 1)

            def q_features(g):
                dve.wait_ge(s["eq_ready"], g + 1)
                dve.wait_ge(s["q1_ready"], g + 1)
                if some(g):
                    dve.wait_ge(s["y_ps"], g)
                nc.vector.scalar_tensor_tensor(qf[:], eq[:], 1.0, q1[:], ALU.min, ALU.max).then_inc(s["qf_ready"], 1)

            def add_kv_bias(g):
                dve.wait_ge(s["kv_ps"], g + 1)
                if some(g):
                    dve.wait_ge(s["ek_ready"], g)
                    dve.wait_ge(s["kf_ready"], g)
                nc.vector.tensor_tensor(k1[:], kvp[:, :, 0:P], over(kb_row[:], 1, G4), ALU.add).then_inc(s["k1_ready"], 1)
                if some(g):
                    dve.wait_ge(s["KV_ps"], g)
                nc.vector.tensor_tensor(v1[:, :, 0:P], kvp[:, :, P:2 * P], over(vb_row[:], 1, G4), ALU.add).then_inc(s["v_ready"], 1)

            def k_features(g):
                dve.wait_ge(s["k1_ready"], g + 1)
                dve.wait_ge(s["ek_ready"], g + 1)
                nc.vector.scalar_tensor_tensor(kf[:], ek[:], 1.0, k1[:], ALU.min, ALU.max).then_inc(s["kf_ready"], 1)

            def mask_kv(g):
                dve.wait_ge(s["KV_ps"], g + 1)
                if some(g):
                    dve.wait_ge(s["y_ps"], g)
                nc.vector.tensor_tensor(KV[:, :, 0:P], kvs[:, :, 0:P], over(block_mask[:], 1, G4), ALU.mult)
                nc.vector.tensor_tensor(KV[:, :, P:P + H], kvs[:, :, P:P + 1].broadcast_to([P, G4, H]),
                                        over(head_mask[:], 1, G4), ALU.mult).then_inc(s["KV_ready"], 1)

            def normalise(g):
                dve.wait_ge(s["y_ps"], g + 1)
                nc.vector.tensor_scalar(den[:], kvp[:, :, P:P + H], ATTN_EPS, None, ALU.max).then_inc(s["den_ready"], 1)
                dve.wait_ge(s["den_ready"], g + 1)
                nc.vector.reciprocal(rden[:], den[:]).then_inc(s["rden_ready"], 1)
                dve.wait_ge(s["rden_ready"], g + 1)
                if some(g):
                    dve.wait_ge(s["yT_ps"], g)
                nc.vector.tensor_tensor(y[:].rearrange("p t (h c) -> p t h c", h=H),
                                        kvp[:, :, 0:P].rearrange("p t (h c) -> p t h c", h=H),
                                        over(rden[:], 3, HD), ALU.mult).then_inc(s["y_ready"], 1)

            def add_attention(g):
                dve.wait_ge(s["attn_ps"], g + 1)
                dve.wait_ge(s["n0b_ready"], g + 1)
                if some(g):
                    dve.wait_ge(s["x1b_ready"], g)
                if some(g):
                    dve.wait_ge(s["z2_ready"], g)
                nc.vector.tensor_tensor(x1[:], attn_ps, n0b[:], ALU.add).then_inc(s["x1_ready"], 1)

            def ln2_stats(f):
                dve.wait_ge(s["x1_ready"], f + 1)
                if some(f):
                    dve.wait_ge(s["ln2_moments"], f)
                dve.sem_inc(s["passed"], 1)
                for t in range(G4):
                    last = nc.vector.bn_stats(stat2[:, t, :], x1[:, t, :])
                last.then_inc(s["ln2_stats"], 1)

            def ln2_moments(f):
                dve.wait_ge(s["ln2_stats"], f + 1)
                if some(f):
                    dve.wait_ge(s["ln2_rstd"], f)
                    dve.wait_ge(s["z2_ready"], f)
                dve.sem_inc(s["passed"], 1)
                for t in range(G4):
                    last = nc.vector.bn_aggr(mom2[:, t, :], stat2[:, t, :])
                last.then_inc(s["ln2_moments"], 1)

            def ln2_apply(f):
                dve.wait_ge(s["ln2_rstd"], f + 1)
                dve.wait_ge(s["ln2_moments"], f + 1)
                if some(f):
                    dve.wait_ge(s["z2T_ps"], f)
                for t in range(G4):
                    last = nc.vector.tensor_scalar(z2[:, t, :], x1[:, t, :], mom2[:, t, 0:1], rs2[:, t:t + 1], ALU.subtract, ALU.mult)
                last.then_inc(s["z2_ready"], 1)

            def finish(f):
                dve.wait_ge(s["w2_ps"], f + 1)
                dve.wait_ge(s["xs_ready"], f + 1)
                nc.vector.tensor_tensor(X[:, bass.ts(f, G4), :], w2_ps, xs[:], ALU.add).then_inc(s["x_out"], 1)

            def turn(g):
                if isinstance(g, int) and g == -1:
                    dve.wait_ge(s["const_loaded"], n_const)
                    nc.vector.tensor_scalar(q_bias1, q_bias, 1.0, None, ALU.add).then_inc(s["ones_ready"], 1)
                    nc.vector.tensor_scalar(kb_row[:], kb_row[:], 1.0, None, ALU.add).then_inc(s["ones_ready"], 1)
                    dve.wait_ge(s["ones_ready"], 3)
                if group(g + 1):
                    ln0_ln1_apply(g + 1)
                if group(g - 1):
                    ln2_apply(g - 1)
                if group(g):
                    normalise(g)
                if group(g + 1):
                    ln0_apply(g + 1)
                if group(g - 2):
                    finish(g - 2)
                if group(g + 2):
                    ln0_moments(g + 2)
                if group(g + 1):
                    add_kv_bias(g + 1)
                    k_features(g + 1)
                    q_features(g + 1)
                if group(g):
                    add_attention(g)
                    ln2_stats(g)
                if group(g + 1):
                    mask_kv(g + 1)
                if group(g):
                    ln2_moments(g)

            turns(dve, turn)
            dve.wait_ge(s["x_out"], NG)

        @block.scalar
        def _(act):
            def ln1T_side(g):
                act.wait_ge(s["z1T_ps"], g + 1)
                if some(g):
                    act.wait_ge(s["q_ps"], g)
                    act.wait_ge(s["kv_ps"], g)
                nc.scalar.activation(ln1T[:], tp, ACT.Identity, scale=g1, bias=be1).then_inc(s["ln1T_ready"], 1)

            def q_side(g):
                act.wait_ge(s["q_ps"], g + 1)
                if some(g):
                    act.wait_ge(s["qf_ready"], g)
                nc.scalar.activation(q1[:], q_ps, ACT.Identity, bias=q_bias1).then_inc(s["q1_ready"], 1)
                nc.scalar.activation(eq[:], q_ps, ACT.Exp, bias=q_bias).then_inc(s["eq_ready"], 1)

            def k_side(g):
                act.wait_ge(s["k1_ready"], g + 1)
                if some(g):
                    act.wait_ge(s["kf_ready"], g)
                nc.scalar.activation(ek[:], k1[:], ACT.Exp, bias=minus_one[:]).then_inc(s["ek_ready"], 1)

            def ln2T_side(f):
                act.wait_ge(s["z2T_ps"], f + 1)
                if some(f):
                    act.wait_ge(s["h_ps"], FC * f)
                nc.scalar.activation(ln2T[:], tp, ACT.Identity, scale=g2, bias=be2).then_inc(s["ln2T_ready"], 1)

            def gelus(f):
                if some(f):
                    act.wait_ge(s["w2_ps"], f)
                for c in range(FC):
                    act.wait_ge(s["h_ps"], FC * f + c + 1)
                    nc.scalar.activation(hT[:, c, :], h_ps[c % 2], ACT.Gelu, bias=cols[:, 6 + c:7 + c]).then_inc(s["h_ready"], 1)

            def yT_side(g):
                act.wait_ge(s["yT_ps"], g + 1)
                if some(g):
                    act.wait_ge(s["attn_ps"], g)
                nc.scalar.activation(yT[:], tp, ACT.Copy).then_inc(s["yT_ready"], 1)

            def turn(g):
                if group(g - 1):
                    ln2T_side(g - 1)
                if group(g + 1):
                    ln1T_side(g + 1)
                if group(g):
                    yT_side(g)
                if group(g + 1):
                    q_side(g + 1)
                    k_side(g + 1)
                if group(g - 1):
                    gelus(g - 1)

            for t, n in consts[0::2]:
                act.dma_start(t[:], d[n]).then_inc(s["const_loaded"], 16)
            act.wait_ge(s["const_loaded"], n_const)
            act.wait_ge(s["ones_ready"], 3)
            act.wait_ge(s["neghalf_ready"], 2)
            turns(act, turn)

        @block.tensor
        def _(pe):
            def t1(g):
                pe.wait_ge(s["z1_ready"], g + 1)
                if not isinstance(g, int) or g >= 2:
                    pe.wait_ge(s["ln2T_ready"], g - 1)
                elif g == 1:
                    pe.wait_ge(s["ln1T_ready"], 1)
                for t in range(G4):
                    last = nc.tensor.transpose(tp[:, t * P:(t + 1) * P], z1[:, t, :], ident[:])
                last.then_inc(s["z1T_ps"], 1)

            def turn_y(g):
                pe.wait_ge(s["y_ready"], g + 1)
                if isinstance(g, int) and g == NG - 1:
                    pe.wait_ge(s["ln2T_ready"], g)
                else:
                    pe.wait_ge(s["ln1T_ready"], g + 2)
                for t in range(G4):
                    last = nc.tensor.transpose(tp[:, t * P:(t + 1) * P], y[:, t, :], ident[:])
                last.then_inc(s["yT_ps"], 1)

            def t2(f):
                pe.wait_ge(s["z2_ready"], f + 1)
                pe.wait_ge(s["yT_ready"], f + 1)
                for t in range(G4):
                    last = nc.tensor.transpose(tp[:, t * P:(t + 1) * P], z2[:, t, :], ident[:])
                last.then_inc(s["z2T_ps"], 1)

            def project_q(g):
                pe.wait_ge(s["ln1T_ready"], g + 1)
                if some(g):
                    pe.wait_ge(s["KV_ready"], g)
                nc.tensor.matmul(q_ps, qkv_w[:, 0:P], ln1T[:], start=True, stop=True).then_inc(s["q_ps"], 1)

            def project_kv(g):
                if some(g):
                    pe.wait_ge(s["y_ready"], g)
                for t in range(G4):
                    last = nc.tensor.matmul(kvp[:, t, :], ln1T[:, t * P:(t + 1) * P], qkv_w[:, P:3 * P], start=True, stop=True)
                last.then_inc(s["kv_ps"], 1)

            def ffn_up(f, chunks):
                if chunks[0] == 0:
                    pe.wait_ge(s["ln2T_ready"], f + 1)
                for c in chunks:
                    if some(FC * f + c - 1):
                        pe.wait_ge(s["h_ready"], FC * f + c - 1)
                    nc.tensor.matmul(h_ps[c % 2], w1[:, c * P:(c + 1) * P], ln2T[:], start=True, stop=True).then_inc(s["h_ps"], 1)

            def context(g):
                pe.wait_ge(s["kf_ready"], g + 1)
                pe.wait_ge(s["v_ready"], g + 1)
                pe.wait_ge(s["eq_ready"], g + 1)
                pe.wait_ge(s["q1_ready"], g + 1)
                for t in range(G4):
                    last = nc.tensor.matmul(kvs[:, t, 0:P + 1], kf[:, t, :], v1[:, t, :], start=True, stop=True)
                last.then_inc(s["KV_ps"], 1)

            def ffn_down(f, tiles):
                if tiles[0] == 0:
                    pe.wait_ge(s["h_ready"], FC * f + FC)
                    if isinstance(f, int) and f == NG - 1:
                        pe.wait_ge(s["x_out"], f)
                    else:
                        pe.wait_ge(s["x1_ready"], f + 2)
                for t in tiles:
                    for c in range(FC):
                        last = nc.tensor.matmul(w2_ps[:, t, :], hT[:, c, t * P:(t + 1) * P], w2[:, c, :],
                                                start=(c == 0), stop=(c == FC - 1))
                if tiles[-1] == G4 - 1:
                    last.then_inc(s["w2_ps"], 1)

            def attend(g):
                pe.wait_ge(s["KV_ready"], g + 1)
                pe.wait_ge(s["qf_ready"], g + 1)
                pe.wait_ge(s["k1_ready"], g + 1)
                for t in range(G4):
                    last = nc.tensor.matmul(kvp[:, t, 0:P + H], qf[:, t * P:(t + 1) * P], KV[:, t, :], start=True, stop=True)
                last.then_inc(s["y_ps"], 1)

            def project_out(g):
                pe.wait_ge(s["yT_ready"], g + 1)
                if some(g - 1):
                    pe.wait_ge(s["x_out"], g - 1)
                elif g == 1:
                    pe.wait_ge(s["x1_ready"], 1)
                for t in range(G4):
                    last = nc.tensor.matmul(attn_ps[:, t, :], yT[:, t * P:(t + 1) * P], out_w[:], start=True, stop=True)
                last.then_inc(s["attn_ps"], 1)

            def turn(g):
                if group(g):
                    attend(g)
                if group(g - 2):
                    ffn_down(g - 2, (0, 1))
                if group(g - 1):
                    t2(g - 1)
                if group(g - 2):
                    ffn_down(g - 2, (2,))
                if group(g + 1):
                    t1(g + 1)
                if group(g - 2):
                    ffn_down(g - 2, (3,))
                if group(g):
                    turn_y(g)
                if group(g + 1):
                    project_q(g + 1)
                    project_kv(g + 1)
                if group(g - 1):
                    ffn_up(g - 1, (0, 1))
                if group(g):
                    project_out(g)
                if group(g + 1):
                    context(g + 1)
                if group(g - 1):
                    ffn_up(g - 1, (2, 3))

            pe.wait_ge(s["const_loaded"], n_const)
            pe.wait_ge(s["ones_ready"], 3)
            turns(pe, turn)


def cross_attention_and_routing(nc, d, X, ident, head_mask, neghalf, psum, banks, xg, W, c):
    with ExitStack() as ctx:
        def sb(name, shape, dt=F32):
            return ctx.enter_context(nc.sbuf_tensor(name, shape, dt))

        def sem(name):
            return ctx.enter_context(nc.semaphore(name))

        KE = K2 * E
        N = B * NQ
        M_ = G4 * NQ
        wq, wk, wv, wo, bv_row, bo_row, bcols, first_row, masked = (
            c[n] for n in ("wq", "wk", "wv", "wo", "bv_row", "bo_row", "bcols", "first_row", "masked"))
        codes, gate_w, expert_no, slot_base, earlier, ones, minus_one = (
            c[n] for n in ("codes", "gate_w", "expert_no", "slot_base", "earlier", "ones", "minus_one"))

        mom3, stat3 = sb("mom3", [P, G4, 2]), sb("stat3", [P, G4, 6])
        var3, rs3, shift3, minus_mean3 = (sb(n, [P, G4]) for n in ("var3", "rs3", "shift3", "minus_mean3"))
        z3 = sb("z3", [P, G4, P])
        z3T = sb("z3T", [P, G4 * P])
        cT = [sb(f"cT{i}", [P, G4 * S2]) for i in range(2)]
        qT = [sb(f"qT{i}", [P, G4 * P]) for i in range(2)]
        kT = [sb(f"kT{i}", [P, G4, S2]) for i in range(2)]
        Kb = [sb(f"Kb{i}", [P, H, S2]) for i in range(2)]
        vb, vr = sb("vb", [S2, G4, P]), sb("vr", [S2, G4, P])
        V = [sb(f"V{i}", [S2, G4, H, VC], BF16) for i in range(2)]
        top_score = sb("top_score", [P, H])
        Sd = sb("Sd", [P, H, S2])
        Pr = sb("Pr", [P, H, S2])
        hi, lo = sb("hi", [S2, H * P], F16), sb("lo", [S2, H * P], F16)
        osum, rsum = sb("osum", [P, H, HD]), sb("rsum", [P, H])
        o = sb("o", [P, G4, P])
        oT = sb("oT", [P, G4 * P])
        xb = sb("xb", [P, G4, P])

        mom4, stat4 = sb("mom4", [P, G4, 2]), sb("stat4", [P, G4, 6])
        var4, rs4, shift4, minus_mean4 = (sb(n, [P, G4]) for n in ("var4", "rs4", "shift4", "minus_mean4"))
        z4 = [sb(f"z4{i}", [P, G4, ROW]) for i in range(2)]
        z4T = sb("z4T", [P, G4 * P])
        top, total, rtotal = sb("top", [P, G4]), sb("total", [P, G4]), sb("rtotal", [P, G4])
        dl, ex, pr, pr2 = (sb(n, [P, G4, E]) for n in ("dl", "ex", "pr", "pr2"))
        is_top = sb("is_top", [P, G4, E])
        best, chosen = sb("best", [P, K2, G4]), sb("chosen", [P, K2, G4])
        hot = sb("hot", [P, G4, K2, E], BF16)
        tile_sum = sb("tile_sum", [P, KE])
        before = sb("before", [P, KE], BF16)
        pair, rpair = sb("pair", [P, G4]), sb("rpair", [P, G4])
        weight = sb("weight", [P, G4, K2])
        ranked = sb("ranked", [P, G4, K2, E])
        rank, row, drop = (sb(n, [P, G4, K2]) for n in ("rank", "row", "drop"))
        idx = [sb(f"idx{i}", [P, G4, K2], I32) for i in range(2)]

        names = ("passed ones_ready before_ready q_bias_ready ctx_loaded "
                 "ln3_stats ln3_moments ln3_var ln3_rstd ln3_shift z3_ready z3T_ps z3T_ready q_ps qT_ready k_ps kT_ready "
                 "v_ps vb_ready v1_ready vr_ready v2_ready v3_ready Kb_ready S_ps M_ready Sd_ready P_ready PT_ps rest_ps "
                 "hi_ready lo_ready pv_done osum_ready rsum_ready o_ready oT_ps oT_ready out_ps xb_ready x_out "
                 "ln4_stats ln4_moments ln4_var ln4_rstd ln4_shift z4_ready z4T_ps z4T_ready gate_ps dl_ready ex_ready "
                 "rank_ps ranked_ready idx_ready step scattered0 scattered1").split()
        s = {n: sem("b_" + n) for n in names}

        S = psum[:, 0:4, 0:HB * S2].rearrange("p a (h n) -> p a h n", h=HB)
        PT = [banks[4], banks[5]]
        O = banks[6][:, 0:H * VC].rearrange("p (h c) -> p h c", h=H)
        misc = banks[7]
        gate_ps = misc[:, 0:G4 * E].rearrange("p (t e) -> p t e", t=G4)
        rank_ps = misc[:, 0:G4 * KE]

        STEPS = 21
        block = ctx.enter_context(nc.Block())

        def groups(eng, steps):
            steps(0, 0)
            steps(1, 1)
            with eng.Fori(2, NG - 3, 2) as g:
                steps(g, 0)
                steps(g + 1, 1)
            for g in range(NG - 2, NG + 2):
                steps(g, g % 2)

        def group(g):
            return not isinstance(g, int) or 0 <= g < NG

        def quarter(n):
            return not isinstance(n, int) or 0 <= n < N

        def xrow(g, t):
            return X[:, bass.ds(G4 * g + t, 1), :].rearrange("p a c -> p (a c)")

        @block.sync
        def _(sp):
            def load(g, par):
                if some(g - 1):
                    sp.wait_ge(s["v_ps"], g - 1)
                    sp.wait_ge(s["k_ps"], g - 1)
                    sp.sem_inc(s["passed"], 1)
                if some(g):
                    sp.wait_ge(s["ctx_loaded"], 16 * g)
                sp.dma_start(cT[par][:], d["ctxT"][:, bass.ts(g, G4 * S2)]).then_inc(s["ctx_loaded"], 16)

            load(0, 0)
            load(1, 1)
            with sp.Fori(2, NG - 1, 2) as g:
                load(g, 0)
                load(g + 1, 1)

        @block.gpsimd
        def _(pool):
            for i in range(2):
                pool.memset(V[i][:, :, :, VC - 1:VC], 1.0).then_inc(s["ones_ready"], 1)

            def ln3_scale(g):
                pool.wait_ge(s["ln3_moments"], g + 1)
                if some(g):
                    pool.wait_ge(s["z3_ready"], g)
                pool.sem_inc(s["passed"], 1)
                pool.tensor_scalar(minus_mean3[:], mom3[:, :, 0], -1.0, None, ALU.mult)
                pool.tensor_scalar(var3[:], mom3[:, :, 1], EPS, None, ALU.add).then_inc(s["ln3_var"], 1)
                pool.wait_ge(s["ln3_var"], g + 1)
                pool.tensor_tensor(rs3[:], var3[:], neghalf[:, 0:G4], ALU.pow).then_inc(s["ln3_rstd"], 1)
                pool.wait_ge(s["ln3_rstd"], g + 1)
                pool.tensor_tensor(shift3[:], minus_mean3[:], rs3[:], ALU.mult).then_inc(s["ln3_shift"], 1)

            def ln4_scale(g):
                pool.wait_ge(s["ln4_moments"], g + 1)
                if some(g):
                    pool.wait_ge(s["z4_ready"], g)
                pool.sem_inc(s["passed"], 1)
                pool.tensor_scalar(minus_mean4[:], mom4[:, :, 0], -1.0, None, ALU.mult)
                pool.tensor_scalar(var4[:], mom4[:, :, 1], EPS, None, ALU.add).then_inc(s["ln4_var"], 1)
                pool.wait_ge(s["ln4_var"], g + 1)
                pool.tensor_tensor(rs4[:], var4[:], neghalf[:, 0:G4], ALU.pow).then_inc(s["ln4_rstd"], 1)
                pool.wait_ge(s["ln4_rstd"], g + 1)
                pool.tensor_tensor(shift4[:], minus_mean4[:], rs4[:], ALU.mult).then_inc(s["ln4_shift"], 1)

            def spread_keys(g, par, j):
                b = G4 * g + j
                pool.wait_ge(s["kT_ready"], g + 1)
                if some(b - 1):
                    pool.wait_ge(s["S_ps"], NQ * (b - 1))
                pool.tensor_tensor(Kb[j % 2][:], over(kT[par][:, j, :], 1, H), over(head_mask[:], 2, S2),
                                   ALU.mult).then_inc(s["Kb_ready"], 1)

            def first_rest(g, par):
                pool.wait_ge(s["v1_ready"], g + 1)
                pool.tensor_tensor(vr[:].rearrange("p t (h c) -> p (t h) c", h=H), vb[:].rearrange("p t (h c) -> p (t h) c", h=H),
                                   V[par][:, :, :, 0:HD].rearrange("p t h c -> p (t h) c"), ALU.subtract).then_inc(s["vr_ready"], 1)

            def second_rest(g, par):
                pool.wait_ge(s["v2_ready"], g + 1)
                pool.tensor_tensor(V[par][:, :, :, 2 * HD:3 * HD].rearrange("p t h c -> p (t h) c"), vr[:].rearrange("p t (h c) -> p (t h) c", h=H),
                                   V[par][:, :, :, HD:2 * HD].rearrange("p t h c -> p (t h) c"), ALU.subtract).then_inc(s["v3_ready"], 1)

            def add_out_bias(g):
                if some(g):
                    pool.wait_ge(s["x_out"], g)
                pool.tensor_tensor(xb[:], X[:, bass.ts(g, G4), :], over(bo_row[:], 1, G4), ALU.add).then_inc(s["xb_ready"], 1)

            def scatter(g, par, t):
                if t == 0:
                    pool.wait_ge(s["idx_ready"], g + 1)
                    pool.sem_inc(s["passed"], 1)
                for k in range(K2):
                    pool.indirect_dma_start(xg, bass.IndirectOffsetOnAxis(ap=idx[par][:, t, k:k + 1], axis=0), z4[par][:, t, :], None,
                                            bounds_check=ROWS - 1, oob_is_err=False).then_inc(s[f"scattered{par}"], 16)

            def steps(g, par):
                other = 1 - par
                if group(g):
                    spread_keys(g, par, 2)
                if group(g - 1):
                    add_out_bias(g - 1)
                if group(g):
                    spread_keys(g, par, 3)
                if group(g - 1):
                    ln4_scale(g - 1)
                if group(g + 1):
                    spread_keys(g + 1, other, 0)
                if group(g - 2):
                    scatter(g - 2, par, 0)
                if group(g + 1):
                    first_rest(g + 1, other)
                if group(g - 2):
                    scatter(g - 2, par, 1)
                if group(g + 1):
                    spread_keys(g + 1, other, 1)
                if group(g + 2):
                    ln3_scale(g + 2)
                if group(g + 1):
                    second_rest(g + 1, other)
                if group(g - 2):
                    scatter(g - 2, par, 2)
                    scatter(g - 2, par, 3)

            ln3_scale(0)
            spread_keys(0, 0, 0)
            spread_keys(0, 0, 1)
            first_rest(0, 0)
            second_rest(0, 0)
            ln3_scale(1)
            groups(pool, steps)
            for par in (0, 1):
                pool.wait_ge(s[f"scattered{par}"], 16 * G4 * K2 * NG // 2)

        @block.vector
        def _(dve):
            v = nc.vector
            v.memset(before[:], 0.0).then_inc(s["before_ready"], 1)

            def ln3_stats(g):
                if some(g):
                    dve.wait_ge(s["ln3_moments"], g)
                dve.sem_inc(s["passed"], 1)
                for t in range(G4):
                    last = v.bn_stats(stat3[:, t, :], xrow(g, t))
                last.then_inc(s["ln3_stats"], 1)

            def ln3_moments(g):
                dve.wait_ge(s["ln3_stats"], g + 1)
                if some(g):
                    dve.wait_ge(s["ln3_shift"], g)
                dve.sem_inc(s["passed"], 1)
                for t in range(G4):
                    last = v.bn_aggr(mom3[:, t, :], stat3[:, t, :])
                last.then_inc(s["ln3_moments"], 1)

            def ln4_stats(g):
                dve.wait_ge(s["x_out"], g + 1)
                if some(g):
                    dve.wait_ge(s["ln4_moments"], g)
                dve.sem_inc(s["passed"], 1)
                for t in range(G4):
                    last = v.bn_stats(stat4[:, t, :], xrow(g, t))
                last.then_inc(s["ln4_stats"], 1)

            def ln4_moments(g):
                dve.wait_ge(s["ln4_stats"], g + 1)
                if some(g):
                    dve.wait_ge(s["ln4_shift"], g)
                dve.sem_inc(s["passed"], 1)
                for t in range(G4):
                    last = v.bn_aggr(mom4[:, t, :], stat4[:, t, :])
                last.then_inc(s["ln4_moments"], 1)

            def add_value_bias(g):
                dve.wait_ge(s["v_ps"], g + 1)
                if some(g):
                    dve.wait_ge(s["vr_ready"], g)
                    dve.wait_ge(s["v1_ready"], g)
                v.tensor_tensor(vb[:], misc[0:S2, :].rearrange("p (t c) -> p t c", t=G4),
                                over(bv_row[0:S2, :], 1, G4), ALU.add).then_inc(s["vb_ready"], 1)

            def top_of(n, q):
                dve.wait_ge(s["S_ps"], n + 1)
                v.reduce_max(top_score[:, HB * q:HB * q + HB], S[:, q], AX.X).then_inc(s["M_ready"], 1)

            def shift(n, q):
                dve.wait_ge(s["M_ready"], n + 1)
                if some(n - NQ + 1):
                    dve.wait_ge(s["P_ready"], n - NQ + 1)
                v.tensor_tensor(Sd[:, HB * q:HB * q + HB, :], S[:, q], over(top_score[:, HB * q:HB * q + HB], 2, S2),
                                ALU.subtract).then_inc(s["Sd_ready"], 1)

            def sums_out(b):
                dve.wait_ge(s["pv_done"], NQ * b + NQ)
                v.tensor_reduce(osum[:], O[:, :, 0:3 * HD].rearrange("p h (i c) -> p h c i", i=3), AX.X, ALU.add).then_inc(s["osum_ready"], 1)
                v.reciprocal(rsum[:], O[:, :, 3 * HD:VC].rearrange("p h c -> p (h c)")).then_inc(s["rsum_ready"], 1)

            def normalise(b, j, turned):
                dve.wait_ge(s["osum_ready"], b + 1)
                dve.wait_ge(s["rsum_ready"], b + 1)
                if j == 0 and some(turned):
                    dve.wait_ge(s["oT_ps"], turned)
                v.tensor_tensor(o[:, j, :].rearrange("p (h c) -> p h c", h=H), osum[:], over(rsum[:], 2, HD), ALU.mult).then_inc(s["o_ready"], 1)

            def add_out(g):
                dve.wait_ge(s["out_ps"], g + 1)
                dve.wait_ge(s["xb_ready"], g + 1)
                v.tensor_tensor(X[:, bass.ts(g, G4), :], misc.rearrange("p (t c) -> p t c", t=G4), xb[:], ALU.add).then_inc(s["x_out"], 1)

            def logits_down(g):
                dve.wait_ge(s["gate_ps"], g + 1)
                v.tensor_reduce(top[:], gate_ps, AX.X, ALU.max).then_inc(s["dl_ready"], 1)
                dve.wait_ge(s["dl_ready"], 2 * g + 1)
                v.tensor_tensor(dl[:], gate_ps, over(top[:], 2, E), ALU.subtract).then_inc(s["dl_ready"], 1)

            def route(g, par, k):
                if k > 0:
                    dve.wait_ge(s["step"], STEPS * g + k)
                elif some(g):
                    dve.wait_ge(s["step"], STEPS * g)
                if k == 0:
                    dve.wait_ge(s["ex_ready"], g + 1)
                    ins = v.tensor_reduce(total[:], ex[:], AX.X, ALU.add)
                if k == 1:
                    ins = v.reciprocal(rtotal[:], total[:])
                if k == 2:
                    ins = v.tensor_tensor(pr[:], ex[:], over(rtotal[:], 2, E), ALU.mult)
                slot, p = (0, pr) if k < 9 else (1, pr2)
                if k in (3, 9):
                    ins = v.tensor_reduce(best[:, slot, :], p[:], AX.X, ALU.max)
                if k in (4, 10):
                    ins = v.tensor_tensor(is_top[:], p[:], over(best[:, slot, :], 2, E), ALU.is_equal)
                if k in (5, 11):
                    ins = v.tensor_tensor(is_top[:], is_top[:], over(expert_no[:], 1, G4), ALU.mult)
                if k in (6, 12):
                    ins = v.tensor_reduce(chosen[:, slot, :], is_top[:], AX.X, ALU.min)
                if k in (7, 13):
                    if k == 7 and some(g):
                        dve.wait_ge(s["rank_ps"], g)
                    ins = v.tensor_tensor(hot[:, :, slot, :], over(chosen[:, slot, :], 2, E), over(expert_no[:], 1, G4), ALU.is_equal)
                if k == 8:
                    ins = v.scalar_tensor_tensor(pr2[:], hot[:, :, 0, :], -2.0, pr[:], ALU.mult, ALU.add)
                if k == 14:
                    ins = v.tensor_reduce(tile_sum[:], hot[:].rearrange("p t k e -> p (k e) t"), AX.X, ALU.add)
                if k == 15:
                    ins = v.scalar_tensor_tensor(pair[:], best[:, 0, :], 1e-9, best[:, 1, :], ALU.add, ALU.add)
                if k == 16:
                    ins = v.reciprocal(rpair[:], pair[:])
                if k == 17:
                    dve.wait_ge(s["rank_ps"], g + 1)
                    v.tensor_tensor(ranked[:].rearrange("p t k e -> p t (k e)"), rank_ps.rearrange("p (t c) -> p t c", t=G4),
                                    hot[:].rearrange("p t k e -> p t (k e)"), ALU.mult).then_inc(s["ranked_ready"], 1)
                    v.tensor_tensor(before[:], before[:], tile_sum[:], ALU.add)
                    ins = v.tensor_tensor(weight[:], best[:].rearrange("p k t -> p t k"), over(rpair[:], 2, K2), ALU.mult)
                if k == 18:
                    ins = v.tensor_reduce(rank[:], ranked[:], AX.X, ALU.add)
                if k == 19:
                    v.tensor_scalar(drop[:], rank[:], float(CAP), OUT_OF_RANGE, ALU.is_ge, ALU.mult)
                    v.scalar_tensor_tensor(W[:, bass.ts(g, G4), :], rank[:], float(CAP), weight[:], ALU.is_lt, ALU.mult)
                    ins = v.scalar_tensor_tensor(row[:], chosen[:].rearrange("p k t -> p t k"), float(CAP), rank[:], ALU.mult, ALU.add)
                if k == 20:
                    ins = v.tensor_tensor(row[:], row[:], over(slot_base[:], 1, G4), ALU.add)
                if k == 21:
                    if some(g - 1):
                        dve.wait_ge(s[f"scattered{par}"], 16 * G4 * K2 // 2 * (g - par))
                    ins = v.tensor_tensor(idx[par][:], row[:], drop[:], ALU.add).then_inc(s["idx_ready"], 1)
                if k < STEPS:
                    ins.then_inc(s["step"], 1)

            def steps(g, par):
                for m in range(M_):
                    n, q, j = M_ * g + m, m % NQ, m // NQ
                    routed = {1: (0, 1, 2), 2: (3, 4, 5), 3: (6, 7, 8), 4: (9, 10, 11), 5: (12, 13, 14), 6: (15, 16),
                              7: (17, 18, 19), 8: (20, 21)}.get(m, ()) if group(g - 2) else ()
                    if len(routed) > 2:
                        route(g - 2, par, routed[0])
                    if quarter(n + 2):
                        top_of(n + 2, (q + 2) % NQ)
                    if len(routed) > 1:
                        route(g - 2, par, routed[-2])
                    if quarter(n + 2):
                        shift(n + 2, (q + 2) % NQ)
                    if q == 2 and quarter(n - NQ):
                        sums_out(G4 * g + j - 1)
                    if routed:
                        route(g - 2, par, routed[-1])
                    if q == 2 and quarter(n - NQ):
                        normalise(G4 * g + j - 1, (j - 1) % G4, g)
                    if group(g + 2):
                        if m == 11:
                            ln3_stats(g + 2)
                        if m == 13:
                            ln3_moments(g + 2)
                    if group(g + 1) and m == 12:
                        add_value_bias(g + 1)
                    if group(g - 1):
                        if m == 5:
                            add_out(g - 1)
                        if m == 7:
                            ln4_stats(g - 1)
                        if m == 8:
                            ln4_moments(g - 1)
                        if m == 15:
                            logits_down(g - 1)

            dve.wait_ge(s["before_ready"], 1)
            v.tensor_scalar(bcols[:, 2:3], bcols[:, 0:1], float(HD) ** -0.5, None, ALU.mult).then_inc(s["q_bias_ready"], 1)
            ln3_stats(0)
            ln3_moments(0)
            ln3_stats(1)
            ln3_moments(1)
            add_value_bias(0)
            for q in (0, 1):
                top_of(q, q)
                shift(q, q)
            groups(dve, steps)
            dve.wait_ge(s["idx_ready"], NG)

        @block.scalar
        def _(act):
            def ln3_apply(g, t):
                if t == 0:
                    act.wait_ge(s["ln3_shift"], g + 1)
                    if some(g):
                        act.wait_ge(s["z3T_ps"], g)
                ins = nc.scalar.activation(z3[:, t, :], xrow(g, t), ACT.Identity, bias=shift3[:, t:t + 1], scale=rs3[:, t:t + 1])
                if t == G4 - 1:
                    ins.then_inc(s["z3_ready"], 1)

            def ln4_apply(g, par, t):
                if t == 0:
                    act.wait_ge(s["ln4_shift"], g + 1)
                    if some(g - 1):
                        act.wait_ge(s["z4T_ps"], g - 1)
                        act.wait_ge(s[f"scattered{par}"], 16 * G4 * K2 // 2 * (g - par))
                    nc.scalar.activation(z4[par][:, :, P:ROW], codes[:, bass.ts(g, G4)].unsqueeze(2), ACT.Copy)
                ins = nc.scalar.activation(z4[par][:, t, 0:P], xrow(g, t), ACT.Identity, bias=shift4[:, t:t + 1], scale=rs4[:, t:t + 1])
                if t == G4 - 1:
                    ins.then_inc(s["z4_ready"], 1)

            def z3T_side(g):
                act.wait_ge(s["z3T_ps"], g + 1)
                if some(g):
                    act.wait_ge(s["q_ps"], g)
                nc.scalar.activation(z3T[:], misc, ACT.Copy).then_inc(s["z3T_ready"], 1)

            def kT_side(g, par):
                act.wait_ge(s["k_ps"], g + 1)
                if some(g - 1):
                    act.wait_ge(s["Kb_ready"], G4 * g - G4)
                nc.scalar.activation(kT[par][:].rearrange("p t n -> p (t n)"), misc[:, 0:G4 * S2], ACT.Identity,
                                     bias=bcols[:, 1:2]).then_inc(s["kT_ready"], 1)

            def qT_side(g, par):
                act.wait_ge(s["q_ps"], g + 1)
                if some(g - 1):
                    act.wait_ge(s["S_ps"], M_ * (g - 1))
                nc.scalar.activation(qT[par][:], misc, ACT.Identity, bias=bcols[:, 2:3], scale=float(HD) ** -0.5).then_inc(s["qT_ready"], 1)

            def first_part(g, par):
                act.wait_ge(s["vb_ready"], g + 1)
                if some(g - 1):
                    act.wait_ge(s["pv_done"], M_ * (g - 1))
                nc.scalar.activation(V[par][:, :, :, 0:HD].rearrange("p t h c -> p (t h) c"),
                                     vb[:].rearrange("p t (h c) -> p (t h) c", h=H), ACT.Copy).then_inc(s["v1_ready"], 1)

            def second_part(g, par):
                act.wait_ge(s["vr_ready"], g + 1)
                nc.scalar.activation(V[par][:, :, :, HD:2 * HD].rearrange("p t h c -> p (t h) c"),
                                     vr[:].rearrange("p t (h c) -> p (t h) c", h=H), ACT.Copy).then_inc(s["v2_ready"], 1)

            def exps(n, q):
                act.wait_ge(s["Sd_ready"], n + 1)
                if some(n - NQ + 1):
                    act.wait_ge(s["PT_ps"], n - NQ + 1)
                nc.scalar.activation(Pr[:, HB * q:HB * q + HB, :], Sd[:, HB * q:HB * q + HB, :], ACT.Exp).then_inc(s["P_ready"], 1)

            def high_part(n, q):
                act.wait_ge(s["PT_ps"], n + 1)
                if some(n - NQ + 1):
                    act.wait_ge(s["pv_done"], n - NQ + 1)
                nc.scalar.activation(hi[:, bass.ts(q, 512)], PT[q % 2][0:S2, :], ACT.Copy).then_inc(s["hi_ready"], 1)

            def low_part(n, q):
                act.wait_ge(s["rest_ps"], n + 1)
                if some(n - NQ + 1):
                    act.wait_ge(s["pv_done"], n - NQ + 1)
                nc.scalar.activation(lo[:, bass.ts(q, 512)], PT[q % 2][0:S2, :], ACT.Copy).then_inc(s["lo_ready"], 1)

            def oT_side(g):
                act.wait_ge(s["oT_ps"], g + 1)
                if some(g):
                    act.wait_ge(s["out_ps"], g)
                nc.scalar.activation(oT[:], misc, ACT.Copy).then_inc(s["oT_ready"], 1)

            def z4T_side(g):
                act.wait_ge(s["z4T_ps"], g + 1)
                if some(g):
                    act.wait_ge(s["gate_ps"], g)
                nc.scalar.activation(z4T[:], misc, ACT.Copy).then_inc(s["z4T_ready"], 1)

            def gate_exps(g):
                act.wait_ge(s["dl_ready"], 2 * g + 2)
                if some(g):
                    act.wait_ge(s["rank_ps"], g)
                nc.scalar.activation(ex[:], dl[:], ACT.Exp).then_inc(s["ex_ready"], 1)

            def steps(g, par):
                other = 1 - par
                for m in range(M_):
                    n, q = M_ * g + m, m % NQ
                    if quarter(n + 1):
                        exps(n + 1, (q + 1) % NQ)
                    if quarter(n - 1):
                        low_part(n - 1, (q - 1) % NQ)
                    if quarter(n):
                        high_part(n, q)
                    if group(g + 1):
                        if 2 <= m < 2 + G4:
                            ln3_apply(g + 1, m - 2)
                        if m == 8:
                            z3T_side(g + 1)
                        if m == 9:
                            kT_side(g + 1, other)
                        if m == 10:
                            qT_side(g + 1, other)
                        if m == 12:
                            first_part(g + 1, other)
                        if m == 15:
                            second_part(g + 1, other)
                    if group(g - 1):
                        if m == 3:
                            oT_side(g - 1)
                        if 9 <= m < 9 + G4:
                            ln4_apply(g - 1, other, m - 9)
                        if m == 13:
                            z4T_side(g - 1)
                    if group(g - 2) and m == 0:
                        gate_exps(g - 2)

            act.wait_ge(s["q_bias_ready"], 1)
            kT_side(0, 0)
            for t in range(G4):
                ln3_apply(0, t)
            z3T_side(0)
            qT_side(0, 0)
            first_part(0, 0)
            second_part(0, 0)
            exps(0, 0)
            groups(act, steps)

        @block.tensor
        def _(pe):
            def t3(g):
                pe.wait_ge(s["z3_ready"], g + 1)
                if isinstance(g, int) and g == 0:
                    pe.wait_ge(s["kT_ready"], 1)
                if some(g - 1):
                    pe.wait_ge(s["x_out"], g - 1)
                if some(g - 2):
                    pe.wait_ge(s["ranked_ready"], g - 2)
                for t in range(G4):
                    last = nc.tensor.transpose(misc[:, t * P:(t + 1) * P], z3[:, t, :], ident[:])
                last.then_inc(s["z3T_ps"], 1)

            def keys(g, par):
                if some(g):
                    pe.wait_ge(s["z3T_ready"], g + 1)
                pe.wait_ge(s["ctx_loaded"], 16 * g + 16)
                nc.tensor.matmul(misc[:, 0:G4 * S2], wk[:], cT[par][:], start=True, stop=True).then_inc(s["k_ps"], 1)

            def queries(g):
                pe.wait_ge(s["kT_ready"], g + 1)
                pe.wait_ge(s["z3T_ready"], g + 1)
                nc.tensor.matmul(misc, wq[:], z3T[:], start=True, stop=True).then_inc(s["q_ps"], 1)

            def values(g, par):
                pe.wait_ge(s["qT_ready"], g + 1)
                for t in range(G4):
                    last = nc.tensor.matmul(misc[0:S2, t * P:(t + 1) * P], cT[par][:, t * S2:(t + 1) * S2], wv[:], start=True, stop=True)
                last.then_inc(s["v_ps"], 1)

            def scores(g, par, m):
                n, q, j = M_ * g + m, m % NQ, m // NQ
                if m == 0:
                    pe.wait_ge(s["qT_ready"], g + 1)
                if q == 0:
                    pe.wait_ge(s["Kb_ready"], G4 * g + j + 1)
                if some(n - NQ + 1):
                    pe.wait_ge(s["Sd_ready"], n - NQ + 1)
                nc.tensor.matmul(S[:, q], qT[par][:, j * P:(j + 1) * P], Kb[j % 2][:, HB * q:HB * q + HB, :], start=True, stop=False)
                nc.tensor.matmul(S[:, q], first_row[:], over(masked[:, bass.ds((G4 * g + j) * S2, S2)], 1, HB),
                                 start=False, stop=True).then_inc(s["S_ps"], 1)

            def turn(n, q):
                pe.wait_ge(s["P_ready"], n + 1)
                if some(n - 1):
                    pe.wait_ge(s["lo_ready"], n - 1)
                for h in range(HB):
                    last = nc.tensor.matmul(PT[q % 2][0:S2, h * P:(h + 1) * P], Pr[:, HB * q + h, :], ident[:], start=(h == 0),
                                            stop=False, is_transpose=True, skip_group_check=True)
                last.then_inc(s["PT_ps"], 1)

            def take_high(n, q):
                pe.wait_ge(s["hi_ready"], n + 1)
                nc.tensor.matmul(PT[q % 2][0:S2, :], minus_one[0:S2, 0:S2], hi[:, bass.ts(q, 512)], start=False, stop=True,
                                 skip_group_check=True).then_inc(s["rest_ps"], 1)

            def weigh(g, par, m):
                n, q, j = M_ * g + m, m % NQ, m // NQ
                if m == 0:
                    pe.wait_ge(s["v3_ready"], g + 1)
                pe.wait_ge(s["hi_ready"], n + 1)
                pe.wait_ge(s["lo_ready"], n + 1)
                if q == 0 and some(G4 * g + j):
                    pe.wait_ge(s["rsum_ready"], G4 * g + j)
                    pe.wait_ge(s["osum_ready"], G4 * g + j)
                for h in range(HB * q, HB * q + HB):
                    nc.tensor.matmul(O[:, h, :], hi[:, h * P:(h + 1) * P], V[par][:, j, h, :], start=True, stop=False)
                    last = nc.tensor.matmul(O[:, h, :], lo[:, h * P:(h + 1) * P], V[par][:, j, h, :], start=False, stop=True)
                last.then_inc(s["pv_done"], 1)

            def turn_out(g):
                pe.wait_ge(s["o_ready"], G4 * g + G4)
                if isinstance(g, int) and g == 0:
                    pe.wait_ge(s["vb_ready"], 2)
                else:
                    pe.wait_ge(s["dl_ready"], 2 * g)
                for t in range(G4):
                    last = nc.tensor.transpose(misc[:, t * P:(t + 1) * P], o[:, t, :], ident[:])
                last.then_inc(s["oT_ps"], 1)

            def project_out(g):
                pe.wait_ge(s["oT_ready"], g + 1)
                for t in range(G4):
                    last = nc.tensor.matmul(misc[:, t * P:(t + 1) * P], oT[:, t * P:(t + 1) * P], wo[:], start=True, stop=True)
                last.then_inc(s["out_ps"], 1)

            def t4(g, par):
                pe.wait_ge(s["z4_ready"], g + 1)
                if isinstance(g, int) and g >= NG - 2:
                    pe.wait_ge(s["ranked_ready"], g)
                else:
                    pe.wait_ge(s["vb_ready"], g + 3)
                for t in range(G4):
                    last = nc.tensor.transpose(misc[:, t * P:(t + 1) * P], z4[par][:, t, 0:P], ident[:])
                last.then_inc(s["z4T_ps"], 1)

            def gate(g):
                pe.wait_ge(s["z4T_ready"], g + 1)
                for t in range(G4):
                    last = nc.tensor.matmul(gate_ps[:, t, :], z4T[:, t * P:(t + 1) * P], gate_w[:], start=True, stop=True)
                last.then_inc(s["gate_ps"], 1)

            def ranks(g):
                pe.wait_ge(s["step"], STEPS * g + 14)
                pe.wait_ge(s["x_out"], min(g + 2, NG) if isinstance(g, int) else g + 2)
                ranks_of = rank_ps.rearrange("p (t c) -> p t c", t=G4)
                tiles = [hot[:, u].rearrange("p k e -> p (k e)") for u in range(G4)]
                nc.tensor.matmul(rank_ps, earlier[:], hot[:].rearrange("p t k e -> p (t k e)"), start=True, stop=False)
                nc.tensor.matmul(rank_ps, ones[:], over(before[:], 1, G4), start=False, stop=False)
                for u in range(G4 - 1):
                    last = nc.tensor.matmul(ranks_of[:, u + 1:G4, :], ones[:], over(tiles[u], 1, G4 - 1 - u), start=False, stop=(u == G4 - 2))
                last.then_inc(s["rank_ps"], 1)

            def steps(g, par):
                other = 1 - par
                for m in range(M_):
                    n, q = M_ * g + m, m % NQ
                    if quarter(n + 3):
                        if m + 3 < M_:
                            scores(g, par, m + 3)
                        else:
                            scores(g + 1, other, m + 3 - M_)
                    if quarter(n - 1):
                        take_high(n - 1, (q - 1) % NQ)
                    if quarter(n):
                        turn(n, q)
                    if quarter(n - 2):
                        if m >= 2:
                            weigh(g, par, m - 2)
                        else:
                            weigh(g - 1, other, m - 2 + M_)
                    if group(g + 1):
                        if m == 8:
                            t3(g + 1)
                        if m == 9:
                            keys(g + 1, other)
                        if m == 10:
                            queries(g + 1)
                        if m == 11:
                            values(g + 1, other)
                    if group(g - 1):
                        if m == 3:
                            turn_out(g - 1)
                        if m == 4:
                            project_out(g - 1)
                        if m == 13:
                            t4(g - 1, other)
                        if m == 14:
                            gate(g - 1)
                    if group(g - 2) and m == 6:
                        ranks(g - 2)

            pe.wait_ge(s["ones_ready"], 2)
            keys(0, 0)
            t3(0)
            queries(0)
            values(0, 0)
            pe.wait_ge(s["vb_ready"], 1)
            for m in range(3):
                scores(0, 0, m)
            groups(pe, steps)


def experts_and_combine(nc, d, X, ident, psum, banks, xg, yt, W, out):
    with ExitStack() as ctx:
        def sb(name, shape, dt=F32):
            return ctx.enter_context(nc.sbuf_tensor(name, shape, dt))

        def sem(name):
            return ctx.enter_context(nc.semaphore(name))

        HC = HID // P
        HALF = GROUP_ROWS // 2
        PAIRS = K2 * E // 2
        NE = PAIRS * PAIR
        gate = [sb(f"gate{i}", [P, HID]) for i in range(2)]
        up = [sb(f"up{i}", [P, HID]) for i in range(2)]
        down = [sb(f"down{i}", [P, HC, P]) for i in range(2)]
        xin = [sb(f"xin{i}", [P, G4, ROW]) for i in range(PAIR)]
        xT = [sb(f"xT{i}", [P, GROUP_ROWS]) for i in range(PAIR)]
        act_g = sb("act_g", [P, HC, GROUP_ROWS])
        h = sb("h", [P, HC, GROUP_ROWS])
        yo = [sb(f"yo{i}", [P, G4, P]) for i in range(PAIR)]
        token = [sb(f"token{i}", [P, G4], I32) for i in range(PAIR)]
        wt = [sb(f"gwt{i}", [P, G4]) for i in range(2)]
        yb = [sb(f"yb{i}", [P, G4, P]) for i in range(4)]
        ost = [sb(f"ost{i}", [P, G4, P]) for i in range(2)]
        names = ("passed w0_loaded w1_loaded xT_ps xT_ready gate_ps up_ps g_ready h_ready y_ps y_ready "
                 "token_ready weights_ready x_added o_ready out0_stored out1_stored").split()
        names += [f"yb{i}_loaded" for i in range(4)] + [f"x{i}_loaded" for i in range(PAIR)] + [f"y{i}_scattered" for i in range(PAIR)]
        s = {n: sem("e_" + n) for n in names}
        gate_ps, up_ps = banks[0:2], banks[2:4]
        tp, y_ps = banks[4], banks[5].rearrange("p (t c) -> p t c", t=G4)
        block = ctx.enter_context(nc.Block())

        def pairs(eng, body):
            body(0, 0)
            with eng.Fori(1, PAIRS // 2 - 1) as p:
                body(p, 0)
            body(PAIRS // 2 - 1, 0)
            with eng.Fori(PAIRS // 2, PAIRS - 1) as p:
                body(p, 1)
            body(PAIRS - 1, 1)

        def has(n):
            return not isinstance(n, int) or 0 <= n < NE

        def rows_of(buffer, n, i):
            a = buffer[bass.ts(n, GROUP_ROWS), :]
            return a.rearrange("(t p) c -> p t c", p=P) if i == PAIR // 2 else a.rearrange("(p t) c -> p t c", p=P)

        def parts(i):
            if i == PAIR // 2:
                return (0, 0, HALF), (1, HALF, GROUP_ROWS)
            return ((0 if i < PAIR // 2 else 1, 0, GROUP_ROWS),)

        @block.sync
        def _(sp):
            def load_x(n, i, p):
                if some(p):
                    sp.wait_ge(s["xT_ps"], n - PAIR + 1)
                    sp.wait_ge(s["token_ready"], n - PAIR + 1)
                sp.dma_start(xin[i][:], rows_of(xg, n, i)).then_inc(s[f"x{i}_loaded"], 16)

            def load_weights(e, which, after):
                if some(after):
                    sp.wait_ge(s["y_ps"], after)
                for w, n in ((gate[which], "gate_proj"), (up[which], "up_proj"), (down[which], "down_proj")):
                    src = d[n][:, bass.ds(e, 1)]
                    src = src.rearrange("p a c -> p (a c)") if len(src.shape) == 3 else src.rearrange("p a b c -> p (a b) c")
                    sp.dma_start(w[:], src).then_inc(s[f"w{which}_loaded"], 16)

            def load_y(g, slot, i):
                rows = yt[slot].rearrange("(p b) c -> p b c", b=B)
                sp.dma_start(yb[i][:], rows[:, bass.ts(g, G4), :]).then_inc(s[f"yb{i}_loaded"], 16)

            def body(p, slot):
                for i in range(PAIR):
                    n = PAIR * p + i
                    if has(n + 2):
                        load_x(n + 2, (i + 2) % PAIR, p if i + 2 < PAIR else p + 1)
                    if i == 0 and some(p):
                        load_weights(2 * (p - slot * (PAIRS // 2)) + 1, 1, PAIR * p)
                    if i == 3 and has(PAIR * p + PAIR):
                        e = 2 * ((p + 1) % (PAIRS // 2)) if isinstance(p, int) else 2 * (p + 1 - slot * (PAIRS // 2))
                        load_weights(e, 0, PAIR * p + 3)
                    if slot == 1 and i < 4:
                        g = 4 * (p - PAIRS // 2) + i
                        for k in range(PAIR):
                            sp.wait_ge(s[f"y{k}_scattered"], 16 * G4 * PAIRS // K2)
                        sp.wait_ge(s["x_added"], g + 1)
                        load_y(g, 0, i)

            load_weights(0, 0, 0)
            load_x(0, 0, 0)
            load_x(1, 1, 0)
            load_weights(1, 1, 0)
            pairs(sp, body)
            for i in range(PAIR):
                sp.wait_ge(s[f"y{i}_scattered"], 16 * G4 * PAIRS)
            for i in range(4):
                sp.wait_ge(s["x_added"], NG + 1 + i)
                load_y(i, 1, i)
            with sp.Fori(0, NG - 7, 4) as g:
                for i in range(4):
                    sp.wait_ge(s["o_ready"], g + i + 1)
                    sp.dma_start(out[:, bass.ts(g + i, G4), :], ost[i % 2][:]).then_inc(s[f"out{i % 2}_stored"], 16)
                    load_y(g + i + 4, 1, i)
            for i in range(4):
                sp.wait_ge(s["o_ready"], NG - 4 + i + 1)
                sp.dma_start(out[:, (NG - 4 + i) * G4:(NG - 3 + i) * G4, :], ost[i % 2][:]).then_inc(s[f"out{i % 2}_stored"], 16)
            for par in (0, 1):
                sp.wait_ge(s[f"out{par}_stored"], 16 * NG // 2)

        @block.gpsimd
        def _(pool):
            def body(p, slot):
                for i in range(PAIR):
                    n = PAIR * p + i
                    pool.wait_ge(s["token_ready"], n + 1)
                    pool.wait_ge(s["y_ready"], n + 1)
                    pool.sem_inc(s["passed"], 1)
                    for t in range(G4):
                        pool.indirect_dma_start(yt[slot], bass.IndirectOffsetOnAxis(ap=token[i][:, t:t + 1], axis=0), yo[i][:, t, :], None,
                                                bounds_check=P * B - 1, oob_is_err=False).then_inc(s[f"y{i}_scattered"], 16)

            pairs(pool, body)

        @block.vector
        def _(dve):
            v = nc.vector
            dve.sem_inc(s["x_added"], 4)

            def tokens(n, i, p):
                dve.wait_ge(s[f"x{i}_loaded"], 16 * p + 16)
                if some(p):
                    dve.wait_ge(s[f"y{i}_scattered"], 16 * G4 * p)
                v.tensor_scalar(token[i][:].unsqueeze(2), xin[i][:, :, P:ROW], NO_TOKEN, None, ALU.add).then_inc(s["token_ready"], 1)

            def weights(g, slot, par):
                v.tensor_copy(wt[par][:].unsqueeze(2), W[:, bass.ts(g, G4), slot:slot + 1]).then_inc(s["weights_ready"], 1)

            def add_first(g, slot_pair, i):
                dve.wait_ge(s[f"yb{i}_loaded"], 16 * slot_pair + 16)
                dve.wait_ge(s["weights_ready"], g + 1)
                for t in range(G4):
                    xt = X[:, bass.ds(G4 * g + t, 1), :].rearrange("p a c -> p (a c)")
                    last = v.scalar_tensor_tensor(xt, yb[i][:, t, :], wt[i % 2][:, t:t + 1], xt, ALU.mult, ALU.add)
                last.then_inc(s["x_added"], 1)
                dve.wait_ge(s["x_added"], 4 + g + 1)

            def add_second(g, i):
                dve.wait_ge(s[f"yb{i}_loaded"], 16 * (NG // 4) + 16 + 4 * (g - i))
                dve.wait_ge(s["weights_ready"], NG + g + 1)
                if some(g - i % 2 - 1):
                    dve.wait_ge(s[f"out{i % 2}_stored"], 8 * (g - i % 2))
                for t in range(G4):
                    last = v.scalar_tensor_tensor(ost[i % 2][:, t, :], yb[i][:, t, :], wt[i % 2][:, t:t + 1],
                                                  X[:, bass.ds(G4 * g + t, 1), :].rearrange("p a c -> p (a c)"), ALU.mult, ALU.add)
                last.then_inc(s["o_ready"], 1)
                dve.wait_ge(s["o_ready"], g + 1)

            def body(p, slot):
                for i in range(PAIR):
                    n = PAIR * p + i
                    for c in range(HC):
                        dve.wait_ge(s["g_ready"], HC * n + c + 1)
                        dve.wait_ge(s["up_ps"], HC * n + c + 1)
                        if some(n):
                            dve.wait_ge(s["y_ps"], n)
                        v.tensor_tensor(h[:, c, :], up_ps[c], act_g[:, c, :], ALU.mult).then_inc(s["h_ready"], 1)
                    if has(n + 1):
                        tokens(n + 1, (i + 1) % PAIR, p if i + 1 < PAIR else p + 1)
                    if slot == 1 and i > 0:
                        g = 4 * (p - PAIRS // 2) + i - 1
                        add_first(g, p - PAIRS // 2, i - 1)
                        if isinstance(g, int) and g + 2 >= NG:
                            weights(g + 2 - NG, 1, (i - 1) % 2)
                        else:
                            weights(g + 2, 0, (i - 1) % 2)

            tokens(0, 0, 0)
            weights(0, 0, 0)
            weights(1, 0, 1)
            pairs(dve, body)
            for i in range(4):
                add_second(i, i)
                weights(i + 2, 1, i % 2)
            with dve.Fori(4, NG - 7, 4) as g:
                for i in range(4):
                    add_second(g + i, i)
                    weights(g + i + 2, 1, i % 2)
            for i in range(4):
                add_second(NG - 4 + i, i)
                if i < 2:
                    weights(NG - 2 + i, 1, i % 2)

        @block.scalar
        def _(act):
            def x_side(n, i):
                act.wait_ge(s["xT_ps"], n + 1)
                nc.scalar.activation(xT[i][:], tp, ACT.Copy).then_inc(s["xT_ready"], 1)

            def y_side(n, i, p):
                act.wait_ge(s["y_ps"], n + 1)
                if some(p):
                    act.wait_ge(s[f"y{i}_scattered"], 16 * G4 * p)
                nc.scalar.activation(yo[i][:], y_ps, ACT.Copy).then_inc(s["y_ready"], 1)

            def body(p, slot):
                for i in range(PAIR):
                    n = PAIR * p + i
                    for c in range(HC):
                        act.wait_ge(s["gate_ps"], HC * n + c + 1)
                        if some(HC * n):
                            act.wait_ge(s["h_ready"], HC * n)
                        nc.scalar.activation(act_g[:, c, :], gate_ps[c], ACT.Silu).then_inc(s["g_ready"], 1)
                    if has(n + 1):
                        x_side(n + 1, (i + 1) % PAIR)
                    if has(n - 1):
                        y_side(n - 1, (i - 1) % PAIR, p if i > 0 else p - 1)

            x_side(0, 0)
            pairs(act, body)
            y_side(NE - 1, PAIR - 1, PAIRS - 1)

        @block.tensor
        def _(pe):
            def turn(n, i, p):
                pe.wait_ge(s[f"x{i}_loaded"], 16 * p + 16)
                if some(n):
                    pe.wait_ge(s["xT_ready"], n)
                for t in range(G4):
                    last = nc.tensor.transpose(tp[:, t * P:(t + 1) * P], xin[i][:, t, 0:P], ident[:])
                last.then_inc(s["xT_ps"], 1)

            def project(n, i, weights, target, done):
                for c in range(HC):
                    for which, a, b in parts(i):
                        last = nc.tensor.matmul(target[c][:, a:b], weights[which][:, c * P:(c + 1) * P], xT[i][:, a:b], start=True, stop=True)
                    last.then_inc(s[done], 1)

            def project_down(n, i):
                pe.wait_ge(s["h_ready"], HC * n + HC)
                if some(n):
                    pe.wait_ge(s["y_ready"], n)
                for which, a, b in parts(i):
                    for t in range(a // P, b // P):
                        for c in range(HC):
                            last = nc.tensor.matmul(y_ps[:, t, :], h[:, c, t * P:(t + 1) * P], down[which][:, c, :],
                                                    start=(c == 0), stop=(c == HC - 1))
                last.then_inc(s["y_ps"], 1)

            def body(p, slot):
                for i in range(PAIR):
                    n = PAIR * p + i
                    if i == 0:
                        pe.wait_ge(s["w0_loaded"], 16 * 3 * p + 48)
                    if i == PAIR // 2:
                        pe.wait_ge(s["w1_loaded"], 16 * 3 * p + 48)
                    pe.wait_ge(s["xT_ready"], n + 1)
                    if some(HC * n):
                        pe.wait_ge(s["g_ready"], HC * n)
                    project(n, i, gate, gate_ps, "gate_ps")
                    if has(n + 1):
                        turn(n + 1, (i + 1) % PAIR, p if i + 1 < PAIR else p + 1)
                    if has(n - 1):
                        project_down(n - 1, (i - 1) % PAIR)
                    project(n, i, up, up_ps, "up_ps")

            turn(0, 0, 0)
            pairs(pe, body)
            project_down(NE - 1, PAIR - 1)


def lay_out(i):
    c = np.ascontiguousarray

    def col(a):
        return c(np.asarray(a).reshape(-1, P).T)

    def rows(a):
        return c(np.broadcast_to(np.asarray(a).reshape(1, -1), (P, np.asarray(a).size)))

    qkv_b = np.asarray(i["L0_attn_qkv_b"])
    head = np.arange(P) // HD
    first_row = (np.arange(P)[:, None] + np.zeros((1, P)) == 0).astype(mybir.dt.np(BF16))
    return {
        "x": c(np.asarray(i["x"]).transpose(1, 0, 2)),
        "qkv_w": c(i["L0_attn_qkv_w"]), "out_w": c(i["L0_attn_out_w"]), "w1": c(i["L0_attn_w1"]),
        "w2": c(np.asarray(i["L0_attn_w2"]).reshape(FC, P, P).transpose(1, 0, 2)),
        "q_bias": col(qkv_b[0:P]), "kb_row": rows(qkv_b[P:2 * P]), "vb_row": rows(qkv_b[2 * P:]),
        "ob_row": rows(i["L0_attn_out_b"]), "b2_row": rows(i["L0_attn_b2"]), "b1": col(i["L0_attn_b1"]),
        "g1": col(i["L0_attn_g1"]), "be1": col(i["L0_attn_be1"]), "g2": col(i["L0_attn_g2"]), "be2": col(i["L0_attn_be2"]),
        "wq": c(np.asarray(i["L0_xattn_Wq"]).T), "wk": c(np.asarray(i["L0_xattn_Wk"]).T),
        "wv": c(np.asarray(i["L0_xattn_Wv"]).T), "wo": c(np.asarray(i["L0_xattn_Wo"]).T),
        "bq": col(i["L0_xattn_bq"]), "bk": col(i["L0_xattn_bk"]),
        "bv_row": rows(i["L0_xattn_bv"]), "bo_row": rows(i["L0_xattn_bo"]),
        "ctxT": c(np.asarray(i["ctx_1024"]).transpose(2, 0, 1).reshape(P, B * S2)),
        "mask": c(np.asarray(i["mask_BxS2_bf0"]).reshape(1, B * S2)),
        "first_row": first_row,
        "gate_w": c(np.asarray(i["L0_ffn_gate_w"]).T),
        "gate_proj": c(np.asarray(i["L0_ffn_gate_proj_w"]).transpose(2, 0, 1)),
        "up_proj": c(np.asarray(i["L0_ffn_up_proj_w"]).transpose(2, 0, 1)),
        "down_proj": c(np.asarray(i["L0_ffn_down_proj_w"]).reshape(E, P, HID // P, P).transpose(3, 0, 2, 1)),
        "codes": (np.arange(P)[:, None] * B + np.arange(B)[None, :] - NO_TOKEN).astype(np.float32),
        "expert_no": rows(np.arange(E, dtype=np.float32) - E),
        "slot_base": rows(np.arange(K2, dtype=np.float32) * E * CAP + E * CAP),
        "earlier": np.triu(np.ones((P, P)), 1).astype(mybir.dt.np(BF16)),
        "ones": np.ones((P, P)).astype(mybir.dt.np(BF16)),
        "minus_one": (-np.eye(P)).astype(np.float16),
        "ident": np.eye(P, dtype=np.float32),
        "block_mask": (head[:, None] == head[None, :]).astype(np.float32),
        "head_mask": (head[:, None] == np.arange(H)[None, :]).astype(np.float32),
    }


def kernel(**inputs):
    import concourse.bacc as _bacc
    from concourse import mybir as _mybir
    from concourse.bass_utils import run_bass_kernel_spmd as _run

    nc = _bacc.Bacc("TRN2", target_bir_lowering=False, num_devices=1)
    arrays, d = {}, {}
    for name, a in lay_out(inputs).items():
        arrays[f"in_{name}"] = a
        d[name] = nc.dram_tensor(f"in_{name}", a.shape, _mybir.dt.from_np(a.dtype), kind="ExternalInput").ap()
    out = nc.dram_tensor("out", (P, B, P), F32, kind="ExternalOutput").ap()
    build(nc, d, out)
    r = _run(nc, [arrays], core_ids=[0])
    return np.ascontiguousarray(r.results[0]["out"].transpose(1, 0, 2))
```
